# Optimizing a Trainium2 kernel written in Bass

```python
import numpy as np
import jax
import jax.numpy as jnp

def _softmax(x, axis=-1):
    return jax.nn.softmax(x, axis=axis)

def _gelu(x):
    return jax.nn.gelu(x, approximate=True)

def _silu(x):
    return jax.nn.silu(x)

def _sigmoid(x):
    return jax.nn.sigmoid(x)

def _layernorm(x, axis=-1, eps=1e-05):
    m = jnp.mean(x, axis=axis, keepdims=True)
    v = jnp.var(x, axis=axis, keepdims=True)
    return (x - m) / jnp.sqrt(v + eps)

def _scatter_add(tgt, idx, src, axis=0):
    return tgt.at[idx].add(src)

def _segment_sum(src, seg, n):
    return jax.ops.segment_sum(src, seg, n)
kernel_name = 'mk_gnn_preln_d4_gnn_r32_4b845e'

def setup_inputs(seed: int=0):
    np.random.seed(seed)
    _w = jnp.asarray

    def _rec_inputs():
        import jax
        import jax.numpy as jnp
        _gk = jax.random.key(seed)
        x = -0.000202 + 1 * jax.random.normal(jax.random.fold_in(_gk, 1), (50000, 128), jnp.float32)
        src = jax.random.randint(jax.random.fold_in(_gk, 2), (50000,), 0, 50000, jnp.int32)
        dst = jnp.minimum((50000 * jax.random.uniform(jax.random.fold_in(_gk, 3), (50000,)) ** 2.0).astype(jnp.int32), 49999)
        _o = jnp.argsort(dst, stable=True)
        src = src[_o]
        dst = dst[_o]
        edge_attr_10 = 8.20919e-05 + 1.00017 * jax.random.normal(jax.random.fold_in(_gk, 12), (50000, 10), jnp.float32)
        return (x, src, dst, edge_attr_10)
    x, src, dst, edge_attr_10 = _rec_inputs()

    def _L0_gnn_setup():
        import jax, jax.numpy as jnp
        import numpy as np
        N, E, D, ED = (50000, 15625, 128, 10)
        EPS = 1e-05

        def _glorot(key, shape):
            return jax.random.normal(key, shape, jnp.float32) / np.sqrt(shape[0]).astype(np.float32)
        key = jax.random.key(seed)
        ks = jax.random.split(key, 8)
        x = jax.random.normal(ks[0], (N, D), jnp.float32)
        edge_index = jax.random.randint(ks[1], (2, E), 0, N, jnp.int32)
        edge_attr = jax.random.normal(ks[2], (E, ED), jnp.float32)
        W_ee = _glorot(ks[3], (ED, D))
        b_ee = jnp.zeros((D,), jnp.float32)
        W_pre = _glorot(ks[4], (3 * D, D))
        b_pre = jnp.zeros((D,), jnp.float32)
        W_post = _glorot(ks[5], (13 * D, D))
        b_post = jnp.zeros((D,), jnp.float32)
        W_lin = _glorot(ks[6], (D, D))
        b_lin = jnp.zeros((D,), jnp.float32)
        return {'x': x, 'edge_attr': edge_attr, 'W_ee': W_ee, 'b_ee': b_ee, 'W_pre': W_pre, 'b_pre': b_pre, 'W_post': W_post, 'b_post': b_post, 'W_lin': W_lin, 'b_lin': b_lin, 'edge_index': edge_index}
    _L0_gnn_all = _L0_gnn_setup()
    _L0_gnn_in = {k: v for k, v in _L0_gnn_all.items() if k in ('W_ee', 'b_ee', 'W_pre', 'b_pre', 'W_post', 'b_post', 'W_lin', 'b_lin')}
    del _L0_gnn_all

    def _L1_gnn_setup():
        import jax, jax.numpy as jnp
        import numpy as np
        N_NODES, N_EDGES = (50000, 25000)
        NODE_D, MSG_D, OUT_D = (128, 128, 128)

        def _linear_params(key, d_in, d_out):
            kw, _ = jax.random.split(key)
            W = jax.random.normal(kw, (d_in, d_out), jnp.float32) * np.float32(1.0 / np.sqrt(d_in))
            b = jnp.zeros((d_out,), jnp.float32)
            return (W, b)
        key = jax.random.key(seed)
        ks = jax.random.split(key, 12)
        node_features = jax.random.normal(ks[0], (N_NODES, NODE_D), jnp.float32)
        src = jax.random.randint(ks[1], (N_EDGES,), 0, N_NODES, dtype=jnp.int32)
        dst = jax.random.randint(ks[2], (N_EDGES,), 0, N_NODES, dtype=jnp.int32)
        W_msg_1, b_msg_1 = _linear_params(ks[3], NODE_D, MSG_D)
        W_msg_2, b_msg_2 = _linear_params(ks[4], MSG_D, MSG_D)
        W_msg_3, b_msg_3 = _linear_params(ks[5], MSG_D, MSG_D)
        W_att_1, b_att_1 = _linear_params(ks[6], 2 * NODE_D, 1)
        W_att_2, b_att_2 = _linear_params(ks[7], 2 * NODE_D, 1)
        W_att_3, b_att_3 = _linear_params(ks[8], 2 * NODE_D, 1)
        W_c1, b_c1 = _linear_params(ks[9], MSG_D + NODE_D, OUT_D)
        W_c2, b_c2 = _linear_params(ks[10], OUT_D, OUT_D)
        return {'node_features': node_features, 'src': src, 'dst': dst, 'W_msg_1': W_msg_1, 'b_msg_1': b_msg_1, 'W_msg_2': W_msg_2, 'b_msg_2': b_msg_2, 'W_msg_3': W_msg_3, 'b_msg_3': b_msg_3, 'W_att_1': W_att_1, 'b_att_1': b_att_1, 'W_att_2': W_att_2, 'b_att_2': b_att_2, 'W_att_3': W_att_3, 'b_att_3': b_att_3, 'W_c1': W_c1, 'b_c1': b_c1, 'W_c2': W_c2, 'b_c2': b_c2}
    _L1_gnn_all = _L1_gnn_setup()
    _L1_gnn_in = {k: v for k, v in _L1_gnn_all.items() if k in ('W_msg_1', 'b_msg_1', 'W_msg_2', 'b_msg_2', 'W_msg_3', 'b_msg_3', 'W_att_1', 'b_att_1', 'W_att_2', 'b_att_2', 'W_att_3', 'b_att_3', 'W_c1', 'b_c1', 'W_c2', 'b_c2')}
    del _L1_gnn_all

    def _L2_gnn_setup():
        import jax, jax.numpy as jnp
        import numpy as np
        N_NODES = 10000
        N_EDGES = 20000
        IN_C = 128
        OUT_C = 128
        key = jax.random.key(seed)
        k1, k2, k3 = jax.random.split(key, 3)
        x = jax.random.normal(k1, (N_NODES, IN_C), dtype=jnp.float32)
        std = float(np.sqrt(2.0 / (IN_C + OUT_C)))
        W = jax.random.normal(k2, (OUT_C, IN_C), dtype=jnp.float32) * std
        b = jnp.zeros((OUT_C,), dtype=jnp.float32)
        edge_index = jax.random.randint(k3, (2, N_EDGES), 0, N_NODES, dtype=jnp.int64)
        return {'x': x, 'W': W, 'b': b, 'edge_index': edge_index}
    _L2_gnn_all = _L2_gnn_setup()
    _L2_gnn_in = {k: v for k, v in _L2_gnn_all.items() if k in ('W', 'b')}
    del _L2_gnn_all

    def _L3_gnn_setup():
        import jax, jax.numpy as jnp
        import numpy as np
        N_LAYERS = 3

        def _lgconv(x, src, dst, norm, n):
            msgs = x[src] * norm[:, None]
            return jax.ops.segment_sum(msgs, dst, num_segments=n)
        key = jax.random.key(seed)
        k1, k2 = jax.random.split(key)
        n_users, d, n_edges = (50000, 128, 18750)
        edge_index = jax.random.randint(k1, (2, n_edges), 0, n_users, dtype=jnp.int64)
        user_emb = jax.random.normal(k2, (n_users, d), dtype=jnp.float32)
        return {'edge_index': edge_index, 'user_emb': user_emb}
    _L3_gnn_all = _L3_gnn_setup()
    _L3_gnn_in = {k: v for k, v in _L3_gnn_all.items() if k in ()}
    del _L3_gnn_all
    return {'x': x, 'src': src, 'dst': dst, 'edge_attr_10': edge_attr_10, 'L0_gnn_W_ee': _L0_gnn_in['W_ee'], 'L0_gnn_b_ee': _L0_gnn_in['b_ee'], 'L0_gnn_W_pre': _L0_gnn_in['W_pre'], 'L0_gnn_b_pre': _L0_gnn_in['b_pre'], 'L0_gnn_W_post': _L0_gnn_in['W_post'], 'L0_gnn_b_post': _L0_gnn_in['b_post'], 'L0_gnn_W_lin': _L0_gnn_in['W_lin'], 'L0_gnn_b_lin': _L0_gnn_in['b_lin'], 'L1_gnn_W_msg_1': _L1_gnn_in['W_msg_1'], 'L1_gnn_b_msg_1': _L1_gnn_in['b_msg_1'], 'L1_gnn_W_msg_2': _L1_gnn_in['W_msg_2'], 'L1_gnn_b_msg_2': _L1_gnn_in['b_msg_2'], 'L1_gnn_W_msg_3': _L1_gnn_in['W_msg_3'], 'L1_gnn_b_msg_3': _L1_gnn_in['b_msg_3'], 'L1_gnn_W_att_1': _L1_gnn_in['W_att_1'], 'L1_gnn_b_att_1': _L1_gnn_in['b_att_1'], 'L1_gnn_W_att_2': _L1_gnn_in['W_att_2'], 'L1_gnn_b_att_2': _L1_gnn_in['b_att_2'], 'L1_gnn_W_att_3': _L1_gnn_in['W_att_3'], 'L1_gnn_b_att_3': _L1_gnn_in['b_att_3'], 'L1_gnn_W_c1': _L1_gnn_in['W_c1'], 'L1_gnn_b_c1': _L1_gnn_in['b_c1'], 'L1_gnn_W_c2': _L1_gnn_in['W_c2'], 'L1_gnn_b_c2': _L1_gnn_in['b_c2'], 'L2_gnn_W': _L2_gnn_in['W'], 'L2_gnn_b': _L2_gnn_in['b']}

def reference(x, src, dst, edge_attr_10, L0_gnn_W_ee, L0_gnn_b_ee, L0_gnn_W_pre, L0_gnn_b_pre, L0_gnn_W_post, L0_gnn_b_post, L0_gnn_W_lin, L0_gnn_b_lin, L1_gnn_W_msg_1, L1_gnn_b_msg_1, L1_gnn_W_msg_2, L1_gnn_b_msg_2, L1_gnn_W_msg_3, L1_gnn_b_msg_3, L1_gnn_W_att_1, L1_gnn_b_att_1, L1_gnn_W_att_2, L1_gnn_b_att_2, L1_gnn_W_att_3, L1_gnn_b_att_3, L1_gnn_W_c1, L1_gnn_b_c1, L1_gnn_W_c2, L1_gnn_b_c2, L2_gnn_W, L2_gnn_b):
    import jax
    import jax.numpy as jnp

    def _L0_gnn_ref(x, edge_attr, W_ee, b_ee, W_pre, b_pre, W_post, b_post, W_lin, b_lin, edge_index):
        import jax, jax.numpy as jnp
        import numpy as np
        N, E, D, ED = (50000, 15625, 128, 10)
        EPS = 1e-05

        def _glorot(key, shape):
            return jax.random.normal(key, shape, jnp.float32) / np.sqrt(shape[0]).astype(np.float32)
        n = x.shape[0]
        src, dst = (edge_index[0], edge_index[1])
        ea = edge_attr @ W_ee + b_ee
        h = jnp.concatenate([x[dst], x[src], ea], axis=-1)
        m = h @ W_pre + b_pre
        cnt = jax.ops.segment_sum(jnp.ones((m.shape[0],), x.dtype), dst, num_segments=n)
        deg = jnp.maximum(cnt, 1.0)[:, None]
        has_edge = (cnt > 0)[:, None]
        mean = jax.ops.segment_sum(m, dst, num_segments=n) / deg
        mean_sq = jax.ops.segment_sum(m * m, dst, num_segments=n) / deg
        std = jnp.sqrt(jax.nn.relu(mean_sq - mean * mean) + EPS)
        mx = jnp.where(has_edge, jax.ops.segment_max(m, dst, num_segments=n), 0.0)
        mn = jnp.where(has_edge, jax.ops.segment_min(m, dst, num_segments=n), 0.0)
        agg = jnp.concatenate([mean, mx, mn, std], axis=-1)
        avg_log = jnp.mean(jnp.log(cnt + 1.0))
        s_log = jnp.log(deg + 1.0)
        scaled = jnp.concatenate([agg, agg * (s_log / avg_log), agg * (avg_log / s_log)], axis=-1)
        out = jnp.concatenate([x, scaled], axis=-1) @ W_post + b_post
        return out @ W_lin + b_lin

    def _L1_gnn_ref(node_features, src, dst, W_msg_1, b_msg_1, W_msg_2, b_msg_2, W_msg_3, b_msg_3, W_att_1, b_att_1, W_att_2, b_att_2, W_att_3, b_att_3, W_c1, b_c1, W_c2, b_c2):
        import jax, jax.numpy as jnp
        import numpy as np
        N_NODES, N_EDGES = (50000, 25000)
        NODE_D, MSG_D, OUT_D = (128, 128, 128)

        def _linear_params(key, d_in, d_out):
            kw, _ = jax.random.split(key)
            W = jax.random.normal(kw, (d_in, d_out), jnp.float32) * np.float32(1.0 / np.sqrt(d_in))
            b = jnp.zeros((d_out,), jnp.float32)
            return (W, b)
        h = node_features
        N = h.shape[0]
        hs = h[src]
        hd = h[dst]
        e = jnp.concatenate([hs, hd], axis=1)
        a1 = jnp.exp(jax.nn.relu(e @ W_att_1 + b_att_1))
        a2 = jnp.exp(jax.nn.relu(e @ W_att_2 + b_att_2))
        a3 = jnp.exp(jax.nn.relu(e @ W_att_3 + b_att_3))
        att1 = jax.ops.segment_sum(a1, dst, num_segments=N)
        att2 = jax.ops.segment_sum(a2, dst, num_segments=N)
        att3 = jax.ops.segment_sum(a3, dst, num_segments=N)
        avg_a = (a1 / att1[dst] + a2 / att2[dst] + a3 / att3[dst]) / 3.0
        m = avg_a * jax.nn.relu(jax.nn.relu(jax.nn.relu(hs @ W_msg_1 + b_msg_1) @ W_msg_2 + b_msg_2) @ W_msg_3 + b_msg_3)
        deg = jax.ops.segment_sum(jnp.ones((src.shape[0], 1), h.dtype), dst, num_segments=N)
        h_neigh = jax.ops.segment_sum(m, dst, num_segments=N) / jnp.maximum(deg, 1.0)
        hc = jnp.concatenate([h, h_neigh], axis=1)
        out = jax.nn.relu(hc @ W_c1 + b_c1) @ W_c2 + b_c2
        return out

    def _L2_gnn_ref(x, W, b, edge_index):
        import jax, jax.numpy as jnp
        import numpy as np
        N_NODES = 10000
        N_EDGES = 20000
        IN_C = 128
        OUT_C = 128
        N = x.shape[0]
        loops = jnp.tile(jnp.arange(N, dtype=edge_index.dtype)[None, :], (2, 1))
        ei = jnp.concatenate([edge_index, loops], axis=1)
        row, col = (ei[0], ei[1])
        h = x @ W.T
        deg = jax.ops.segment_sum(jnp.ones(col.shape, dtype=h.dtype), col, num_segments=N)
        deg_inv_sqrt = deg ** (-0.5)
        norm = deg_inv_sqrt[row] * deg_inv_sqrt[col]
        msg = norm[:, None] * h[row]
        agg = jax.ops.segment_sum(msg, col, num_segments=N)
        return agg + b

    def _L3_gnn_ref(edge_index, user_emb):
        import jax, jax.numpy as jnp
        import numpy as np
        N_LAYERS = 3

        def _lgconv(x, src, dst, norm, n):
            msgs = x[src] * norm[:, None]
            return jax.ops.segment_sum(msgs, dst, num_segments=n)
        n = user_emb.shape[0]
        src, dst = (edge_index[0], edge_index[1])
        ones = jnp.ones(src.shape[0], dtype=user_emb.dtype)
        deg = jax.ops.segment_sum(ones, dst, num_segments=n)
        dinv = jnp.where(deg > 0, jax.lax.rsqrt(jnp.maximum(deg, 1.0)), 0.0)
        norm = dinv[src] * dinv[dst]
        x = user_emb
        acc = x
        for _ in range(N_LAYERS):
            x = _lgconv(x, src, dst, norm, n)
            acc = acc + x
        return acc / (N_LAYERS + 1)
    edge_index = jnp.stack([src, dst])
    h = jnp.maximum(_layernorm(x, axis=-1), 0.0)
    x = x + _L0_gnn_ref(h, edge_attr_10, L0_gnn_W_ee, L0_gnn_b_ee, L0_gnn_W_pre, L0_gnn_b_pre, L0_gnn_W_post, L0_gnn_b_post, L0_gnn_W_lin, L0_gnn_b_lin, edge_index)
    h = jnp.maximum(_layernorm(x, axis=-1), 0.0)
    x = x + _L1_gnn_ref(h, src, dst, L1_gnn_W_msg_1, L1_gnn_b_msg_1, L1_gnn_W_msg_2, L1_gnn_b_msg_2, L1_gnn_W_msg_3, L1_gnn_b_msg_3, L1_gnn_W_att_1, L1_gnn_b_att_1, L1_gnn_W_att_2, L1_gnn_b_att_2, L1_gnn_W_att_3, L1_gnn_b_att_3, L1_gnn_W_c1, L1_gnn_b_c1, L1_gnn_W_c2, L1_gnn_b_c2)
    h = jnp.maximum(_layernorm(x, axis=-1), 0.0)
    x = x + _L2_gnn_ref(h, L2_gnn_W, L2_gnn_b, edge_index)
    h = jnp.maximum(_layernorm(x, axis=-1), 0.0)
    x = x + _L3_gnn_ref(edge_index, h)
    return x

_drawn_inputs = setup_inputs


def setup_inputs(seed=0):
    import zlib

    import numpy as np

    out = dict(_drawn_inputs(seed))
    spreads = {'L0_gnn_b_ee': (0.0, 0.1),
     'L0_gnn_b_pre': (0.0, 0.1),
     'L0_gnn_b_post': (0.0, 0.1),
     'L0_gnn_b_lin': (0.0, 0.1),
     'L1_gnn_b_msg_1': (0.0, 0.8),
     'L1_gnn_b_msg_2': (0.0, 0.8),
     'L1_gnn_b_msg_3': (0.0, 0.56),
     'L1_gnn_b_c1': (0.0, 0.1),
     'L1_gnn_b_c2': (0.0, 0.1),
     'L2_gnn_b': (0.0, 0.1)}
    factors = {'L1_gnn_W_att_1': 8.0, 'L1_gnn_W_att_2': 8.0, 'L1_gnn_W_att_3': 8.0}
    for name, (base, spread) in spreads.items():
        noise = np.random.default_rng([zlib.crc32(name.encode()), seed]).standard_normal(out[name].shape)
        drawn = base * np.exp(spread * noise) if base else spread * noise
        out[name] = jnp.asarray(drawn.astype(out[name].dtype))
    for name, factor in factors.items():
        out[name] = (out[name] * factor).astype(out[name].dtype)
    return out
```

```python
from contextlib import ExitStack

import concourse.bass as bass
from concourse import mybir

F32 = mybir.dt.float32
BF16 = mybir.dt.bfloat16
I32 = mybir.dt.int32
U8 = mybir.dt.uint8
ALU = mybir.AluOpType
ACT = mybir.ActivationFunctionType
AX_X = mybir.AxisListType.X

P = 128
D = 128
N = 50000
E = 50000
ED = 10
TPG = 4
ROWS = TPG * P
GROUPS = 98
TILES = GROUPS * TPG
NPAD = GROUPS * ROWS
ZERO_ROW = NPAD
LAST_P = (N - (GROUPS - 1) * ROWS) // TPG
NO_NODE = 60000
EPS = 1e-5
BIG = 3.0e38
W_MSG = D + 4
W_ATT = 3 * D + 4
NSC = 7
(S_INV, S_HAS, S_LOG, S_ALOG, S_GCN, S_DINV, S_THIRD) = range(NSC)
assert LAST_P * TPG + (GROUPS - 1) * ROWS == N and GROUPS % 2 == 0


def pipeline(eng, *stages):
    stages = [s if isinstance(s, tuple) else (n, s) for n, s in enumerate(stages) if s is not None]
    depth = max(delay for delay, _ in stages)
    head = 2 + depth + (depth % 2)

    def peeled(steps):
        for t in steps:
            for s, stage in stages:
                if 0 <= t - s < GROUPS:
                    stage(t - s, (t - s) % 2, (t - s) // 2)

    peeled(range(head))
    with eng.Fori(head // 2, GROUPS // 2 - 1) as j:
        for v in range(2):
            for s, stage in stages:
                back, slot = (v - s) // 2, (v - s) % 2
                stage(j * 2 + (2 * back + slot), slot, j + back)
    peeled(range(GROUPS - 2, GROUPS + depth))


def at_start(g):
    return isinstance(g, int) and g < 2


def ready(eng, sem, g, per=1):
    eng.wait_ge(sem, (g + 1) * per)


def freed(eng, sem, g, per=1):
    if not at_start(g):
        eng.wait_ge(sem, (g - 1) * per)


def passed(eng, sem, g, per=1):
    if not (isinstance(g, int) and g == 0):
        eng.wait_ge(sem, g * per)


def landed(eng, sems, u, r, inc=16):
    eng.wait_ge(sems[u], (r + 1) * inc)


def drained(eng, sems, u, r, inc=16):
    if not (isinstance(r, int) and r == 0):
        eng.wait_ge(sems[u], r * inc)


def rows_of(table, g, cols=None):
    t = table[0:NPAD, :].rearrange("(g p k) d -> g p k d", p=P, k=TPG)
    return t[g] if isinstance(g, int) else t[bass.ds(g, 1)].rearrange("o p k d -> (o p) k d")


def edge_rows_of(table, g):
    t = table[0:NPAD, :].rearrange("(g k p) d -> g p k d", p=P, k=TPG)
    return t[g] if isinstance(g, int) else t[bass.ds(g, 1)].rearrange("o p k d -> (o p) k d")


def tail_rows(table):
    return table[(GROUPS - 1) * ROWS:N, :].rearrange("(p k) d -> p k d", k=TPG)


def is_last(g):
    return isinstance(g, int) and g == GROUPS - 1


def bc(ap, n):
    return ap.unsqueeze(2).to_broadcast([ap.shape[0], ap.shape[1], n])


class Chain:

    def __init__(self, eng, sem):
        self.eng, self.sem, self.n = eng, sem, 0

    def __call__(self, ins):
        self.n += 1
        ins.then_inc(self.sem, 1)
        self.eng.wait_ge(self.sem, self.n)


class Scope:

    def __init__(self, nc, ctx, name):
        self.nc, self.ctx, self.name, self.sems = nc, ctx, name, []
        ctx.callback(self.release)

    def release(self):
        if self.sems:
            self.nc.clear_and_free_semaphores(self.sems)
            self.nc.all_engine_barrier()

    def sb(self, name, shape, dt=F32):
        return self.ctx.enter_context(self.nc.sbuf_tensor(f"{self.name}_{name}", shape, dt))

    def ps(self, name, shape, dt=F32):
        return self.ctx.enter_context(self.nc.psum_tensor(f"{self.name}_{name}", shape, dt))

    def sem(self, name):
        self.sems.append(self.nc.alloc_semaphore(f"{self.name}_{name}"))
        return self.sems[-1]

    def pair(self, name):
        return [self.sem(f"{name}{u}") for u in range(2)]


def build(nc, a, out):
    ctx = ExitStack()
    with ctx:
        R = Scope(nc, ctx, "r")
        dram = lambda name, shape, dt=F32: nc.dram_tensor(name, shape, dt).ap()
        h0_tab = dram("h0_tab", (NPAD, D))
        b0_tab = dram("b0_tab", (NPAD, D))
        e0_tab = dram("e0_tab", (NPAD + 1, 4 * D))
        x1_tab = dram("x1_tab", (NPAD, D))
        h1_tab = dram("h1_tab", (NPAD, D))
        m1_tab = dram("m1_tab", (NPAD, W_MSG))
        d1_tab = dram("d1_tab", (NPAD, 4))
        e1_tab = dram("e1_tab", (NPAD + 1, W_ATT))
        x2_tab = dram("x2_tab", (NPAD, D))
        t2_tab = dram("t2_tab", (NPAD, D))
        e2_tab = dram("e2_tab", (NPAD + 1, D))
        z0_tab = dram("z0_tab", (NPAD, D))
        y_tab = dram("y_tab", (NPAD, D))
        r1_tab = dram("r1_tab", (NPAD + 1, D))
        r2_tab = dram("r2_tab", (NPAD + 1, D))
        a2_tab = dram("a2_tab", (NPAD, D))
        a3_tab = dram("a3_tab", (NPAD + 1, D))
        hop_tab = dram("hop_tab", (NPAD, 2))
        keep_row = dram("keep_row", (TILES, P), U8)

        ident = R.sb("ident", [P, P])
        ones = R.sb("ones", [P, P])
        eps = R.sb("eps", [P, 1])
        keep = R.sb("keep", [P, NPAD], U8)
        src_i = R.sb("src_i", [P, TILES], I32)
        dst_i = R.sb("dst_i", [P, TILES], I32)
        last_i = R.sb("last_i", [P, TILES], I32)
        hop_i = R.sb("hop_i", [P, TILES], I32)
        hop_w = R.sb("hop_w", [P, TILES])
        nsc = R.sb("nsc", [P, GROUPS, NSC, TPG])
        w_a, w_b = R.sb("w_a", [P, D]), R.sb("w_b", [P, D])
        w_edge = R.sb("w_edge", [TPG * ED, TPG, D])
        w_agg = R.sb("w_agg", [P, 4, 3, D])
        w_self = R.sb("w_self", [P, D])
        w_m1, w_m2, w_m3 = (R.sb(f"w_m{i}", [P, D]) for i in (1, 2, 3))
        w_att = R.sb("w_att", [P, 6])
        w_c1a, w_c1b, w_c2 = (R.sb(n, [P, D]) for n in ("w_c1a", "w_c1b", "w_c2"))
        w_gcn = R.sb("w_gcn", [P, D])
        c_pre, c_post, c_m3, c_c2, c_gcn = (R.sb(n, [P, D]) for n in ("c_pre", "c_post", "c_m3", "c_c2", "c_gcn"))
        c_m1, c_m2, c_c1 = (R.sb(n, [P, 1]) for n in ("c_m1", "c_m2", "c_c1"))
        c_att = R.sb("c_att", [P, 4])

        with ExitStack() as c2:
            S = Scope(nc, c2, "s")
            iota_p = S.sb("iota_p", [P, P])
            iota_q = S.sb("iota_q", [P, TILES])
            before = S.sb("before", [P, P])
            target = S.sb("target", [GROUPS, TPG, P], I32)
            prev = S.sb("prev", [GROUPS, TPG, P], I32)
            source = S.sb("source", [GROUPS, TPG, P], I32)
            bits = [S.sb(f"bits{i}", [GROUPS, TPG, P], I32) for i in range(4)]
            lists = [S.sb(f"lists{i}", [GROUPS, TPG, P]) for i in range(4)]
            keep8 = S.sb("keep8", [GROUPS, TPG, P], U8)
            p_col, q_col = S.sb("p_col", [P, TILES]), S.sb("q_col", [P, TILES])
            w_ee, w_c, w_lin = S.sb("w_ee", [ED + 1, D]), S.sb("w_c", [P, D]), S.sb("w_lin", [P, D])
            w_ee_t = S.sb("w_ee_t", [P, ED + 1])
            w_post, w_post_t = S.sb("w_post", [P, 13, D]), S.sb("w_post_t", [P, 13, D])
            w_g = S.sb("w_g", [P, D])
            b_col = S.sb("b_col", [P, 2])
            b_rep = S.sb("b_rep", [P, 2, P])
            w_edge1 = S.sb("w_edge1", [ED, D])
            zero = S.sb("zero", [P, 8])
            cnt = S.sb("cnt", [P, GROUPS, TPG])
            tmp = [S.sb(f"tmp{i}", [P, GROUPS, TPG]) for i in range(4)]
            hop = S.sb("hop", [P, GROUPS, TPG, 2])
            col = [S.sb(f"col{i}", [P, GROUPS]) for i in range(3)]
            avg = S.sb("avg", [P, 4])
            hot_p = S.sb("hot_p", [P, 2, P], BF16)
            hot_q = S.sb("hot_q", [P, 2, TILES], BF16)
            ps = [S.ps(f"ps{i}", [P, 512]) for i in range(6)]
            filled, loaded, built, chain, gchain = (S.sem(n) for n in ("filled", "loaded", "built", "chain", "gchain"))

            loads = [
                (w_a[:, :], a["L0_gnn_W_pre"][0:D, :]), (w_b[:, :], a["L0_gnn_W_pre"][D:2 * D, :]),
                (w_c[:, :], a["L0_gnn_W_pre"][2 * D:3 * D, :]),
                (w_ee[0:ED, :], a["L0_gnn_W_ee"][:, :]), (w_ee[ED:ED + 1, :], a["L0_gnn_b_ee"].unsqueeze(0)),
                (w_lin[:, :], a["L0_gnn_W_lin"][:, :]),
                (w_post[:, :, :], a["L0_gnn_W_post"].rearrange("(b p) n -> p b n", p=P)),
                (w_m1[:, :], a["L1_gnn_W_msg_1"][:, :]), (w_m2[:, :], a["L1_gnn_W_msg_2"][:, :]),
                (w_m3[:, :], a["L1_gnn_W_msg_3"][:, :]),
                (w_c1a[:, :], a["L1_gnn_W_c1"][0:D, :]), (w_c1b[:, :], a["L1_gnn_W_c1"][D:2 * D, :]),
                (w_c2[:, :], a["L1_gnn_W_c2"][:, :]), (w_g[:, :], a["L2_gnn_W"][:, :]),
                (c_m3[:, :], a["L1_gnn_b_msg_3"].unsqueeze(0).to_broadcast([P, D])),
                (c_c2[:, :], a["L1_gnn_b_c2"].unsqueeze(0).to_broadcast([P, D])),
                (c_gcn[:, :], a["L2_gnn_b"].unsqueeze(0).to_broadcast([P, D])),
                (c_pre[:, :], a["L0_gnn_b_pre"].unsqueeze(0).to_broadcast([P, D])),
                (c_post[:, :], a["L0_gnn_b_lin"].unsqueeze(0).to_broadcast([P, D])),
                (c_m1[:, :], a["L1_gnn_b_msg_1"].unsqueeze(1)), (c_m2[:, :], a["L1_gnn_b_msg_2"].unsqueeze(1)),
                (c_c1[:, :], a["L1_gnn_b_c1"].unsqueeze(1)),
                (b_col[:, 0:1], a["L0_gnn_b_ee"].unsqueeze(1)), (b_col[:, 1:2], a["L0_gnn_b_post"].unsqueeze(1)),
            ]
            for k in range(3):
                w = a[f"L1_gnn_W_att_{k + 1}"]
                loads += [(w_att[:, k:k + 1], w[0:D, :]), (w_att[:, 3 + k:4 + k], w[D:2 * D, :]),
                          (c_att[:, k:k + 1], a[f"L1_gnn_b_att_{k + 1}"].unsqueeze(0).to_broadcast([P, 1]))]
            full = E // P
            rest = E - full * P
            pads = []
            for b in range(TPG):
                n = min(GROUPS, full - b * GROUPS)
                o = b * GROUPS * P
                for tile, name in ((target, "dst"), (source, "src")):
                    pads.append((tile[0:n, b, :], a[name][o:o + n * P].rearrange("(t c) -> t c", c=P)))
                    if n < GROUPS:
                        pads.append((tile[n:n + 1, b, 0:rest], a[name][full * P:E].unsqueeze(0)))
                if b == 0:
                    pads.append((prev[0:1, b, 1:P], a["dst"][0:P - 1].unsqueeze(0)))
                    pads.append((prev[1:n, b, :], a["dst"][P - 1:n * P - 1].rearrange("(t c) -> t c", c=P)))
                else:
                    pads.append((prev[0:n, b, :], a["dst"][o - 1:o + n * P - 1].rearrange("(t c) -> t c", c=P)))
                if n < GROUPS:
                    pads.append((prev[n:n + 1, b, 0:rest], a["dst"][full * P - 1:E - 1].unsqueeze(0)))

            with nc.Block() as block:
                @block.sync
                def _(sp):
                    for dst, src in loads:
                        sp.dma_start(dst, src).then_inc(loaded, 16)
                    sp.wait_ge(filled, 3)
                    for dst, src in pads:
                        sp.dma_start(dst, src).then_inc(loaded, 16)
                    sp.wait_ge(loaded, 16 * (len(loads) + len(pads)))

                @block.vector
                def _(v):
                    v.memset(target[:, :, :], NO_NODE).then_inc(filled, 1)
                    v.memset(prev[:, :, :], -1).then_inc(filled, 1)
                    v.memset(source[:, :, :], 0).then_inc(filled, 1)
                    v.memset(ones[:, :], 1.0)
                    v.memset(eps[:, :], EPS)
                    v.memset(zero[:, :], 0.0)
                    v.memset(c_att[:, 3:4], 0.0)
                    v.memset(w_edge[:, :, :], 0.0)

                @block.gpsimd
                def _(g):
                    link = Chain(g, gchain)
                    g.iota(iota_p[:, :], [[1, P]], base=0, channel_multiplier=0,
                           allow_small_or_imprecise_dtypes=True)
                    g.iota(iota_q[:, :], [[1, TILES]], base=0, channel_multiplier=0,
                           allow_small_or_imprecise_dtypes=True)
                    link(g.memset(ident[:, :], 0.0))
                    g.affine_select(out=ident[:, :], in_=ident[:, :], compare_op=ALU.not_equal, fill=1.0, base=0,
                                    pattern=[[-1, P]], channel_multiplier=1)
                    link(g.memset(before[:, :], 1.0))
                    g.affine_select(out=before[:, :], in_=before[:, :], compare_op=ALU.is_gt, fill=0.0, base=0,
                                    pattern=[[1, P]], channel_multiplier=-1)

            turned, taken, mul, kept = (S.sem(n) for n in ("turned", "taken", "mul", "kept"))
            with nc.Block() as block:
                @block.vector
                def _(v):
                    link = Chain(v, chain)
                    v.tensor_scalar(bits[0][:, :, :], target[:, :, :], 2, 127, ALU.logical_shift_right, ALU.bitwise_and)
                    v.tensor_scalar(bits[1][:, :, :], target[:, :, :], 9, 2, ALU.logical_shift_right,
                                    ALU.logical_shift_left)
                    link(v.tensor_scalar(bits[2][:, :, :], target[:, :, :], 3, None, ALU.bitwise_and))
                    v.tensor_copy(lists[0][:, :, :], bits[0][:, :, :])
                    v.tensor_tensor(lists[1][:, :, :], bits[1][:, :, :], bits[2][:, :, :], ALU.add)
                    v.tensor_copy(lists[2][:, :, :], source[:, :, :])
                    v.tensor_scalar(lists[3][:, :, :], target[:, :, :], float(NPAD - 1), None, ALU.min).then_inc(built, 1)
                    v.tensor_tensor(keep8[:, :, :], target[:, :, :], prev[:, :, :], ALU.is_equal).then_inc(built, 1)
                    v.tensor_copy(b_rep[:, :, :], bc(b_col[:, :], P)).then_inc(built, 1)
                    v.wait_ge(turned, 1)
                    for i, dst in enumerate((p_col, q_col, src_i, dst_i)):
                        v.tensor_copy(dst[:, :], ps[i][:, 0:TILES])
                    v.tensor_copy(w_gcn[:, :], ps[4][:, 0:D])
                    v.tensor_copy(w_ee_t[:, :], ps[5][:, 0:ED + 1]).then_inc(taken, 1)
                    v.wait_ge(turned, 2)
                    for i in range(4):
                        n = min(4, 13 - 4 * i)
                        ins = v.tensor_copy(w_post_t[:, 4 * i:4 * i + n, :].rearrange("p b n -> p (b n)"),
                                            ps[i][:, 0:n * D])
                    ins.then_inc(taken, 1)
                    v.wait_ge(mul, 1)
                    v.tensor_copy(w_self[:, :], ps[0][:, 0:D])
                    for i in range(3):
                        v.tensor_copy(w_agg[:, :, i, :], ps[1 + i][:, :].rearrange("p (c n) -> p c n", c=4))
                    v.tensor_copy(w_edge1[:, :], ps[4][0:ED, 0:D]).then_inc(taken, 1)
                    v.tensor_tensor(c_pre[:, :], c_pre[:, :], ps[5][:, 0:D], ALU.add)
                    v.tensor_tensor(c_post[:, :], c_post[:, :], ps[5][:, D:2 * D], ALU.add)

                @block.tensor
                def _(pe):
                    pe.wait_ge(built, 3)
                    for i in range(4):
                        for b in range(TPG):
                            pe.transpose(ps[i][:, b * GROUPS:(b + 1) * GROUPS], lists[i][:, b, :],
                                         ident[0:GROUPS, 0:GROUPS])
                    pe.transpose(ps[4][:, 0:D], w_g[:, :], ident[:, :])
                    pe.transpose(ps[5][:, 0:ED + 1], w_ee[:, :], ident[0:ED + 1, 0:ED + 1]).then_inc(turned, 1)
                    pe.wait_ge(taken, 1)
                    for b in range(13):
                        ins = pe.transpose(ps[b // 4][:, b % 4 * D:(b % 4 + 1) * D], w_post[:, b, :], ident[:, :])
                    ins.then_inc(turned, 1)
                    pe.wait_ge(taken, 2)
                    pe.matmul(ps[0][:, 0:D], w_post_t[:, 0, :], w_lin[:, :], start=True, stop=True)
                    for i in range(3):
                        for c, q in enumerate((0, 2, 1, 3)):
                            pe.matmul(ps[1 + i][:, c * D:(c + 1) * D], w_post_t[:, 1 + 4 * i + q, :], w_lin[:, :],
                                      start=True, stop=True)
                    pe.matmul(ps[4][0:ED, 0:D], w_ee_t[:, 0:ED], w_c[:, :], start=True, stop=True)
                    pe.matmul(ps[5][:, 0:D], b_rep[:, 0, :], w_c[:, :], start=True, stop=True)
                    pe.matmul(ps[5][:, D:2 * D], b_rep[:, 1, :], w_lin[:, :], start=True, stop=True).then_inc(mul, 1)

                @block.sync
                def _(sp):
                    sp.wait_ge(built, 2)
                    sp.dma_start(keep_row[:, :].rearrange("(b t) c -> t b c", t=GROUPS), keep8[:, :, :]).then_inc(kept, 16)
                    for tab, w in ((e0_tab, 4 * D), (e1_tab, W_ATT), (e2_tab, D), (r1_tab, D), (r2_tab, D), (a3_tab, D)):
                        sp.dma_start(tab[ZERO_ROW:ZERO_ROW + 1, :].rearrange("o (p c) -> (o p) c", c=4),
                                     zero[0:w // 4, 0:4]).then_inc(kept, 16)
                    sp.wait_ge(kept, 7 * 16)
                    sp.dma_start(keep[:, :], keep_row.rearrange("t c -> (t c)").unsqueeze(0).to_broadcast([P, NPAD]))\
                        .then_inc(kept, 16)
                    sp.wait_ge(taken, 3)
                    for k in range(TPG):
                        sp.dma_start(w_edge[k * ED:(k + 1) * ED, k, :], w_edge1[:, :]).then_inc(kept, 16)
                    sp.wait_ge(kept, 12 * 16)

            hot, used, counted, scanned, logs = (S.sem(n) for n in ("hot", "used", "counted", "scanned", "logs"))
            with nc.Block() as block:
                @block.vector
                def _(v):
                    def one_hots(t, u):
                        if not at_start(t):
                            v.wait_ge(used, t - 1)
                        v.tensor_scalar(hot_p[:, u, :], iota_p[:, :], p_col[:, t:t + 1] if isinstance(t, int)
                                        else p_col[:, bass.ds(t, 1)], None, ALU.is_equal)
                        v.tensor_scalar(hot_q[:, u, :], iota_q[:, :], q_col[:, t:t + 1] if isinstance(t, int)
                                        else q_col[:, bass.ds(t, 1)], None, ALU.is_equal).then_inc(hot, 1)

                    one_hots(0, 0)
                    one_hots(1, 1)
                    with v.Fori(1, TILES // 2) as j:
                        one_hots(j * 2, 0)
                        one_hots(j * 2 + 1, 1)

                    link = Chain(v, counted)
                    v.wait_ge(used, TILES)
                    link(v.tensor_copy(cnt[:, :, :].rearrange("p g k -> p (g k)"), ps[0][:, 0:TILES]))
                    link(v.tensor_reduce(col[0][:, :], cnt[:, :, :], AX_X, ALU.add))
                    v.wait_ge(scanned, 1)
                    v.tensor_copy(col[2][:, :], ps[1][:, 0:GROUPS])
                    link(v.tensor_tensor_scan(col[1][:, :], ones[:, 0:GROUPS], ps[2][:, 0:GROUPS], 0.0, ALU.mult, ALU.add))
                    link(v.tensor_tensor(col[1][:, :], col[1][:, :], ps[2][:, 0:GROUPS], ALU.subtract))
                    link(v.tensor_tensor(tmp[0][:, :, 0], cnt[:, :, 0], col[1][:, :], ALU.add))
                    link(v.tensor_tensor(tmp[0][:, :, 0], tmp[0][:, :, 0], col[2][:, :], ALU.add))
                    for k in range(1, TPG):
                        link(v.tensor_tensor(tmp[0][:, :, k], tmp[0][:, :, k - 1], cnt[:, :, k], ALU.add))
                    link(v.tensor_scalar(nsc[:, :, S_HAS, :], cnt[:, :, :], 0.0, None, ALU.is_gt))
                    link(v.scalar_tensor_tensor(out=tmp[1][:, :, :], in0=tmp[0][:, :, :], scalar=-1.0 - ZERO_ROW,
                                                in1=nsc[:, :, S_HAS, :], op0=ALU.add, op1=ALU.mult))
                    link(v.tensor_scalar(hop[:, :, :, 0], tmp[1][:, :, :], float(ZERO_ROW), None, ALU.add))
                    v.tensor_copy(last_i[:, :].rearrange("p (g k) -> p g k", k=TPG), hop[:, :, :, 0])
                    link(v.tensor_scalar(tmp[1][:, :, :], cnt[:, :, :], 1.0, None, ALU.max))
                    link(v.reciprocal(nsc[:, :, S_INV, :], tmp[1][:, :, :]))
                    v.tensor_scalar(nsc[:, :, S_THIRD, :], nsc[:, :, S_INV, :], 1.0 / 3.0, None, ALU.mult)
                    v.tensor_tensor(hop[:, :, :, 1], nsc[:, :, S_INV, :], nsc[:, :, S_HAS, :], ALU.mult)
                    link(v.tensor_scalar(tmp[2][:, :, :], cnt[:, :, :], 1.0, None, ALU.add))
                    v.wait_ge(logs, 4)
                    v.reciprocal(nsc[:, :, S_GCN, :], nsc[:, :, S_GCN, :])
                    link(v.reciprocal(tmp[0][:, :, :], nsc[:, :, S_DINV, :]))
                    link(v.tensor_tensor(nsc[:, :, S_DINV, :], tmp[0][:, :, :], nsc[:, :, S_HAS, :], ALU.mult))
                    v.wait_ge(scanned, 2)
                    link(v.tensor_scalar(avg[:, 1:2], ps[3][:, 0:1], 1.0 / N, None, ALU.mult))
                    link(v.reciprocal(avg[:, 2:3], avg[:, 1:2]))
                    link(v.reciprocal(tmp[0][:, :, :], tmp[3][:, :, :]))
                    v.tensor_scalar(nsc[:, :, S_LOG, :], tmp[3][:, :, :], avg[:, 2:3], None, ALU.mult)
                    v.tensor_scalar(nsc[:, :, S_ALOG, :], tmp[0][:, :, :], avg[:, 1:2], None, ALU.mult)

                @block.scalar
                def _(act):
                    act.wait_ge(counted, 15)
                    act.activation(nsc[:, :, S_GCN, :], tmp[2][:, :, :], ACT.Sqrt).then_inc(logs, 1)
                    act.activation(nsc[:, :, S_DINV, :], tmp[1][:, :, :], ACT.Sqrt).then_inc(logs, 1)
                    act.activation(tmp[3][:, :, :], tmp[1][:, :, :], ACT.Ln, bias=1.0).then_inc(logs, 1)
                    act.activation(tmp[0][:, :, :], cnt[:, :, :], ACT.Ln, bias=1.0, accum_out=avg[:, 0:1])\
                        .then_inc(logs, 1)

                @block.tensor
                def _(pe):
                    def add_tile(t, u, start=False, stop=False):
                        pe.wait_ge(hot, t + 1)
                        pe.matmul(ps[0][:, 0:TILES], hot_p[:, u, :], hot_q[:, u, :], start=start, stop=stop,
                                  skip_group_check=True).then_inc(used, 1)

                    add_tile(0, 0, start=True)
                    add_tile(1, 1)
                    with pe.Fori(1, TILES // 2 - 1) as j:
                        add_tile(j * 2, 0)
                        add_tile(j * 2 + 1, 1)
                    add_tile(TILES - 2, 0)
                    add_tile(TILES - 1, 1, stop=True)
                    pe.wait_ge(counted, 2)
                    pe.matmul(ps[1][:, 0:GROUPS], before[:, :], col[0][:, :], start=True, stop=True)
                    pe.matmul(ps[2][:, 0:GROUPS], ones[:, :], col[0][:, :], start=True, stop=True).then_inc(scanned, 1)
                    pe.wait_ge(logs, 4)
                    pe.matmul(ps[3][:, 0:1], ones[:, :], avg[:, 0:1], start=True, stop=True).then_inc(scanned, 1)

            hopped = S.sem("hopped")
            with nc.Block() as block:
                @block.sync
                def _(sp):
                    for h in range(2):
                        g0, g1 = h * GROUPS // 2, (h + 1) * GROUPS // 2
                        sp.dma_start(hop_tab.rearrange("(g p k) w -> p g (k w)", p=P, k=TPG)[:, g0:g1, :],
                                     hop[:, g0:g1, :, :].rearrange("p g k w -> p g (k w)")).then_inc(hopped, 16)
                    sp.wait_ge(hopped, 32)

        class Norm:

            def __init__(self, S, src, dst):
                self.src, self.dst = src, dst
                self.stats = S.sb("ln_stats", [P, 2, TPG, 6])
                self.mv = S.sb("ln_mv", [P, 2, TPG, 2])
                self.std = S.sb("ln_std", [P, 2, TPG])
                self.scale = S.sb("ln_scale", [P, 2, TPG])
                self.shift = S.sb("ln_shift", [P, 2, TPG])
                self.sums, self.moments, self.root, self.inverse, self.scaled, self.done, self.held = (
                    S.sem(n) for n in ("ln_sums", "ln_moments", "ln_root", "ln_inverse", "ln_scaled", "ln_done",
                                        "ln_held"))

            def moments_of(self, v, g, u):
                for k in range(TPG):
                    ins = v.bn_stats(self.stats[:, u, k, :], self.src(u)[:, k, :])
                ins.then_inc(self.sums, 1)
                ready(v, self.sums, g)
                freed(v, self.scaled, g)
                v.sem_inc(self.held, 1)
                for k in range(TPG):
                    ins = v.bn_aggr(self.mv[:, u, k, :], self.stats[:, u, k, :])
                ins.then_inc(self.moments, 1)

            def root_of(self, act, g, u):
                ready(act, self.moments, g)
                freed(act, self.inverse, g)
                act.activation(self.std[:, u, :], self.mv[:, u, :, 1], ACT.Sqrt, bias=eps[:, :]).then_inc(self.root, 1)

            def scale_of(self, v, g, u):
                ready(v, self.root, g)
                freed(v, self.done, g)
                v.reciprocal(self.scale[:, u, :], self.std[:, u, :]).then_inc(self.inverse, 1)
                ready(v, self.inverse, g)
                v.scalar_tensor_tensor(out=self.shift[:, u, :], in0=self.mv[:, u, :, 0], scalar=-1.0,
                                       in1=self.scale[:, u, :], op0=ALU.mult, op1=ALU.mult).then_inc(self.scaled, 1)

            def relu_of(self, act, g, u):
                ready(act, self.scaled, g)
                for k in range(TPG):
                    ins = act.activation(self.dst(u)[:, k, :], self.src(u)[:, k, :], ACT.Relu,
                                         scale=self.scale[:, u, k:k + 1], bias=self.shift[:, u, k:k + 1])
                ins.then_inc(self.done, 1)

        def flat(ap):
            return ap.rearrange("p k d -> p (k d)")

        def turn(pe, dst, src, done):
            for k in range(TPG):
                ins = pe.transpose(dst[:, k * P:(k + 1) * P], src[:, k, :], ident[:, :])
            ins.then_inc(done, 1)

        def end_of(eng, sems, uses=GROUPS // 2):
            for s in sems:
                eng.wait_ge(s, 16 * uses)

        def node_gather(pool, table, dst, index, stage, staged, got, sent, u, g):
            cols = index[:, g * TPG:(g + 1) * TPG] if isinstance(g, int) else index[:, bass.ds(g * TPG, TPG)]
            pool.tensor_copy(stage[:, u, :], cols).then_inc(staged, 1)
            ready(pool, staged, g)
            pool.sem_inc(sent, 1)
            for k in range(TPG):
                pool.indirect_dma_start(out=dst[:, k, :], out_offset=None, in_=table[:, :],
                                        in_offset=bass.IndirectOffsetOnAxis(ap=stage[:, u, k:k + 1], axis=0))\
                    .then_inc(got[u], 16)

        with ExitStack() as c2:
            S = Scope(nc, c2, "n0")
            x = S.sb("x", [P, 2, TPG, D])
            h = S.sb("h", [P, 2, TPG, D])
            ht = S.sb("ht", [P, 2, ROWS])
            b = S.sb("b", [P, 2, TPG, D])
            pt = [S.ps(f"pt{u}", [P, ROWS]) for u in range(2)]
            pb = [S.ps(f"pb{u}", [P, ROWS]) for u in range(2)]
            x_in, h_out, b_out = S.pair("x_in"), S.pair("h_out"), S.pair("b_out")
            turned, ht_there, prod, b_there = (S.sem(n) for n in ("turned", "ht_there", "prod", "b_there"))
            ln = Norm(S, lambda u: x[:, u], lambda u: h[:, u])

            with nc.Block() as block:
                @block.sync
                def _(sp):
                    def load(g, u, r):
                        freed(sp, ln.done, g)
                        if is_last(g):
                            sp.dma_start(x[0:LAST_P, u, :, :], tail_rows(a["x"])).then_inc(x_in[u], 16)
                        else:
                            t = a["x"][0:(GROUPS - 1) * ROWS, :].rearrange("(g p k) d -> g p k d", p=P, k=TPG)
                            t = t[g] if isinstance(g, int) else t[bass.ds(g, 1)].rearrange("o p k d -> (o p) k d")
                            sp.dma_start(x[:, u, :, :], t).then_inc(x_in[u], 16)

                    pipeline(sp, load)
                    end_of(sp, h_out)
                    end_of(sp, b_out)

                @block.vector
                def _(v):
                    def moments(g, u, r):
                        landed(v, x_in, u, r)
                        ln.moments_of(v, g, u)

                    def scales(g, u, r):
                        ln.scale_of(v, g, u)

                    def take_turned(g, u, r):
                        ready(v, turned, g)
                        freed(v, prod, g)
                        v.tensor_copy(ht[:, u, :], pt[u][:, :]).then_inc(ht_there, 1)

                    pipeline(v, (1, scales), (0, moments), (2, take_turned))

                @block.scalar
                def _(act):
                    def root(g, u, r):
                        ln.root_of(act, g, u)

                    def relu(g, u, r):
                        drained(act, h_out, u, r)
                        freed(act, turned, g)
                        ln.relu_of(act, g, u)

                    def take_b(g, u, r):
                        ready(act, prod, g)
                        drained(act, b_out, u, r)
                        act.copy(flat(b[:, u]), pb[u][:, :]).then_inc(b_there, 1)

                    def store_h(g, u, r):
                        ready(act, ln.done, g)
                        act.dma_start(rows_of(h0_tab, g), h[:, u, :, :]).then_inc(h_out[u], 16)

                    def store_b(g, u, r):
                        ready(act, b_there, g)
                        act.dma_start(rows_of(b0_tab, g), b[:, u, :, :]).then_inc(b_out[u], 16)

                    pipeline(act, (1, relu), (0, root), (1, store_h), (2, take_b), (2, store_b))

                @block.tensor
                def _(pe):
                    def turn_h(g, u, r):
                        ready(pe, ln.done, g)
                        freed(pe, ht_there, g)
                        turn(pe, pt[u], h[:, u], turned)

                    def times_w(g, u, r):
                        ready(pe, ht_there, g)
                        freed(pe, b_there, g)
                        for k in range(TPG):
                            ins = pe.matmul(pb[u][:, k * D:(k + 1) * D], ht[:, u, k * P:(k + 1) * P], w_b[:, :],
                                            start=True, stop=True)
                        ins.then_inc(prod, 1)

                    pipeline(pe, turn_h, times_w)

        with ExitStack() as c2:
            S = Scope(nc, c2, "e0")
            rows = S.sb("rows", [P, 2, TPG, D])
            stage = S.sb("stage", [P, 2, TPG], I32)
            ea = S.sb("ea", [P, 2, TPG, ED])
            ea_t = S.sb("ea_t", [TPG * ED, 2, P])
            sq = S.sb("sq", [P, 2, ROWS])
            low, high = S.sb("low", [P, 2, ROWS]), S.sb("high", [P, 2, ROWS])
            run = [S.sb(f"run{q}", [P, 2, ROWS]) for q in range(4)]
            res = S.sb("res", [P, 2, TPG, 4, D])
            pt = [S.ps(f"pt{u}", [P, ROWS]) for u in range(2)]
            pe_t = S.ps("pe_t", [P, P])
            pr = [S.ps(f"pr{q}", [P, ROWS]) for q in range(4)]
            got, ea_in, res_out = S.pair("got"), S.pair("ea_in"), S.pair("res_out")
            staged, sent, ea_turned, ea_there, msg, squared, bounds, held = (
                S.sem(n) for n in ("staged", "sent", "ea_turned", "ea_there", "msg", "squared", "bounds", "held"))
            scanned = [S.sem(f"scanned{q}") for q in range(4)]
            back = [S.sem(f"back{q}") for q in range(4)]
            taken = [S.sem(f"taken{q}") for q in range(4)]
            EA_FULL = E // P - (GROUPS - 1) * TPG
            EA_REST = E - (E // P) * P

            with nc.Block() as block:
                @block.gpsimd
                def _(pool):
                    def gather(g, u, r):
                        drained(pool, got, u, r, 16 * TPG)
                        pool.sem_inc(sent, 1)
                        freed(pool, msg, g)
                        pool.sem_inc(sent, 1)
                        node_gather(pool, b0_tab, rows[:, u], src_i, stage, staged, got, sent, u, g)

                    pipeline(pool, gather)

                @block.sync
                def _(sp):
                    def load(g, u, r):
                        freed(sp, ea_turned, g)
                        src = a["edge_attr_10"]
                        if is_last(g):
                            o = (GROUPS - 1) * ROWS
                            sp.dma_start(ea[:, u, 0:EA_FULL, :], src[o:o + EA_FULL * P, :]
                                         .rearrange("(k p) d -> p k d", p=P)).then_inc(ea_in[u], 16)
                            sp.dma_start(ea[0:EA_REST, u, EA_FULL, :], src[o + EA_FULL * P:E, :]).then_inc(ea_in[u], 16)
                        else:
                            t = src[0:(GROUPS - 1) * ROWS, :].rearrange("(g k p) d -> g p k d", p=P, k=TPG)
                            t = t[g] if isinstance(g, int) else t[bass.ds(g, 1)].rearrange("o p k d -> (o p) k d")
                            sp.dma_start(ea[:, u, :, :], t).then_inc(ea_in[u], 16)

                    pipeline(sp, load)
                    end_of(sp, res_out)

                @block.tensor
                def _(pe):
                    def turn_ea(g, u, r):
                        if is_last(g):
                            pe.wait_ge(ea_in[u], 16 * (r + 2))
                        else:
                            landed(pe, ea_in, u, r)
                        passed(pe, ea_there, g)
                        pe.sem_inc(held, 1)
                        pe.transpose(pe_t[0:TPG * ED, :], ea[:, u].rearrange("p k d -> p (k d)"), ident[:, :])\
                            .then_inc(ea_turned, 1)

                    def messages(g, u, r):
                        landed(pe, got, u, r, 16 * TPG)
                        ready(pe, ea_there, g)
                        for q in range(4):
                            freed(pe, scanned[q], g)
                        for k in range(TPG):
                            pe.matmul(pt[u][:, k * P:(k + 1) * P], rows[:, u, k, :], ident[:, :], start=True, stop=False)
                            ins = pe.matmul(pt[u][:, k * P:(k + 1) * P], w_edge[:, k, :], ea_t[:, u, :],
                                            start=False, stop=True)
                        ins.then_inc(msg, 1)

                    def turn_back(g, u, r):
                        for q in range(4):
                            pe.wait_ge(scanned[q], g + 2)
                            passed(pe, taken[q], g)
                            for k in range(TPG):
                                ins = pe.transpose(pr[q][:, k * P:(k + 1) * P], run[q][:, u, k * P:(k + 1) * P],
                                                   ident[:, :])
                            ins.then_inc(back[q], 1)

                    pipeline(pe, turn_ea, messages, turn_back)

                @block.vector
                def _(v):
                    for q in range(4):
                        v.memset(run[q][:, 1, ROWS - 1:ROWS], 0.0).then_inc(scanned[q], 1)

                    def scans(g, u, r):
                        m = keep[:, g * ROWS:(g + 1) * ROWS] if isinstance(g, int) else keep[:, bass.ds(g * ROWS, ROWS)]
                        ready(v, squared, g)
                        for q, (gate, data, op0, op1) in enumerate((
                                (m, pt[u][:, :], ALU.mult, ALU.add), (m, sq[:, u, :], ALU.mult, ALU.add),
                                (low[:, u, :], pt[u][:, :], ALU.add, ALU.max),
                                (high[:, u, :], pt[u][:, :], ALU.add, ALU.min))):
                            if q == 2:
                                ready(v, bounds, g)
                            v.wait_ge(scanned[q], g + 1)
                            freed(v, back[q], g)
                            v.tensor_tensor_scan(run[q][:, u, :], gate, data, run[q][:, 1 - u, ROWS - 1:ROWS],
                                                 op0, op1).then_inc(scanned[q], 1)

                    pipeline(v, None, scans)

                @block.scalar
                def _(act):
                    def take_ea(g, u, r):
                        ready(act, ea_turned, g)
                        freed(act, msg, g)
                        act.copy(ea_t[:, u, :], pe_t[0:TPG * ED, :]).then_inc(ea_there, 1)

                    def gates(g, u, r):
                        m = keep[:, g * ROWS:(g + 1) * ROWS] if isinstance(g, int) else keep[:, bass.ds(g * ROWS, ROWS)]
                        if not at_start(g):
                            act.wait_ge(scanned[3], g)
                        act.activation(low[:, u, :], m, ACT.Copy, scale=BIG, bias=-BIG)
                        act.activation(high[:, u, :], m, ACT.Copy, scale=-BIG, bias=BIG).then_inc(bounds, 1)
                        ready(act, msg, g)
                        act.activation(sq[:, u, :], pt[u][:, :], ACT.Square).then_inc(squared, 1)

                    def take_back(g, u, r):
                        for q in range(4):
                            ready(act, back[q], g)
                            if q == 0:
                                drained(act, res_out, u, r)
                            act.copy(res[:, u, :, q, :], pr[q][:, :].rearrange("p (k d) -> p k d", k=TPG))\
                                .then_inc(taken[q], 1)

                    def store(g, u, r):
                        ready(act, taken[3], g)
                        act.dma_start(edge_rows_of(e0_tab, g), res[:, u, :, :, :].rearrange("p k q d -> p k (q d)"))\
                            .then_inc(res_out[u], 16)

                    pipeline(act, (0, take_ea), (1, gates), (2, take_back), (2, store))

        def scalars(g, which):
            s = nsc[:, g, which, :] if isinstance(g, int) else nsc[:, bass.ds(g, 1), which, :].rearrange("p o k -> p (o k)")
            return bc(s, D)

        def scalar_of(g, which, k):
            if isinstance(g, int):
                return nsc[:, g, which, k:k + 1]
            return nsc[:, bass.ds(g, 1), which, k]

        def row_bc(ap):
            return ap.unsqueeze(1).to_broadcast([P, TPG, D])

        def gather_steps(pool, table, rows, index, stage, staged, got, sent, used):
            def gather(g, u, r):
                drained(pool, got, u, r, 16 * TPG)
                pool.sem_inc(sent, 1)
                used(pool, g)
                pool.sem_inc(sent, 1)
                node_gather(pool, table, rows[:, u], index, stage, staged, got, sent, u, g)
            return gather

        with ExitStack() as c2:
            S = Scope(nc, c2, "n1")
            x, h0 = S.sb("x", [P, 2, TPG, D]), S.sb("h0", [P, 2, TPG, D])
            xc = S.sb("xc", [P, 2, TPG, D])
            h0t = S.sb("h0t", [P, 2, ROWS])
            agg = S.sb("agg", [P, 2, TPG, 4 * D])
            stage = S.sb("stage", [P, 2, TPG], I32)
            am, sq = S.sb("am", [P, TPG, D]), S.sb("sq", [P, TPG, D])
            mean = S.sb("mean", [P, TPG, D])
            var = S.sb("var", [P, 2, TPG, D])
            aggt = S.sb("aggt", [P, 4, ROWS])
            x1, h1 = S.sb("x1", [P, 2, TPG, D]), S.sb("h1", [P, 2, TPG, D])
            pt, pa = S.ps("pt", [P, ROWS]), S.ps("pa", [P, ROWS])
            pq = [S.ps(f"pq{i}", [P, ROWS]) for i in range(2)]
            py = [S.ps(f"py{k}", [P, 3 * D]) for k in range(TPG)]
            got, x_in, h_in, x_out, h_out = (S.pair(n) for n in ("got", "x_in", "h_in", "x_out", "h_out"))
            (staged, sent, turned, h0t_there, a_prod, a_biased, a_masked, means, sqs, squares, var_there, shifted, std_there, xc_there,
             q_turned, q_taken, prod, mix1, mix2, x1_there) = (S.sem(n) for n in (
                 "staged", "sent", "turned", "h0t_there", "a_prod", "a_biased", "a_masked", "means", "sqs", "squares",
                 "var_there", "shifted", "std_there", "xc_there", "q_turned", "q_taken", "prod", "mix1", "mix2", "x1_there"))
            relud, hop_staged, hop_taken = S.sem("relud"), S.sem("hop_staged"), S.sem("hop_taken")
            hop_rows = S.sb("hop_rows", [P, 2, TPG, 2])
            hop_stage = S.sb("hop_stage", [P, 2, TPG], I32)
            hop_got = S.pair("hop_got")
            ln = Norm(S, lambda u: x1[:, u], lambda u: h1[:, u])

            with nc.Block() as block:
                @block.gpsimd
                def _(pool):
                    gather = gather_steps(pool, e0_tab, agg, last_i, stage, staged, got, sent,
                                          lambda p, g: freed(p, q_turned, g, 4))

                    def add_bias(g, u, r):
                        landed(pool, x_in, u, r)
                        pool.sem_inc(sent, 1)
                        freed(pool, mix1, g)
                        pool.sem_inc(sent, 1)
                        pool.tensor_tensor(xc[:, u], x[:, u], row_bc(c_post[:, :]), ALU.add).then_inc(xc_there, 1)

                    hops = gather_steps(pool, hop_tab, hop_rows, src_i, hop_stage, hop_staged, hop_got, sent,
                                        lambda p, g: freed(p, hop_taken, g))
                    pipeline(pool, (0, gather), (0, add_bias), (0, hops))

                @block.sync
                def _(sp):
                    def load(g, u, r):
                        freed(sp, xc_there, g)
                        if is_last(g):
                            sp.dma_start(x[0:LAST_P, u, :, :], tail_rows(a["x"])).then_inc(x_in[u], 16)
                        else:
                            t = a["x"][0:(GROUPS - 1) * ROWS, :].rearrange("(g p k) d -> g p k d", p=P, k=TPG)
                            t = t[g] if isinstance(g, int) else t[bass.ds(g, 1)].rearrange("o p k d -> (o p) k d")
                            sp.dma_start(x[:, u, :, :], t).then_inc(x_in[u], 16)
                        freed(sp, turned, g)
                        sp.dma_start(h0[:, u, :, :], rows_of(h0_tab, g)).then_inc(h_in[u], 16)

                    pipeline(sp, load)
                    end_of(sp, x_out)
                    end_of(sp, h_out)

                @block.tensor
                def _(pe):
                    def turn_h0(g, u, r):
                        landed(pe, h_in, u, r)
                        passed(pe, h0t_there, g)
                        turn(pe, pt, h0[:, u], turned)

                    def times_a(g, u, r):
                        ready(pe, h0t_there, g)
                        passed(pe, a_biased, g)
                        for k in range(TPG):
                            ins = pe.matmul(pa[:, k * D:(k + 1) * D], h0t[:, u, k * P:(k + 1) * P], w_a[:, :],
                                            start=True, stop=True)
                        ins.then_inc(a_prod, 1)

                    def turn_agg(g, u, r):
                        for q in range(4):
                            if q == 0:
                                ready(pe, shifted, g)
                            if q == 3:
                                ready(pe, std_there, g)
                            if q < 2:
                                if not (isinstance(g, int) and g == 0):
                                    pe.wait_ge(q_taken, g * 4 - 1 + q)
                            else:
                                pe.wait_ge(q_taken, g * 4 + q - 1)
                            turn(pe, pq[q % 2], agg[:, u, :, q * D:(q + 1) * D], q_turned)

                    def project(g, u, r):
                        ready(pe, q_taken, g, 4)
                        for k in range(TPG):
                            if k == 0:
                                passed(pe, x1_there, g)
                            for q in range(4):
                                pe.matmul(py[k][:, :], aggt[:, q, k * P:(k + 1) * P],
                                          w_agg[:, q, :, :].rearrange("p j n -> p (j n)"), start=(q == 0), stop=False,
                                          skip_group_check=True)
                            ins = pe.matmul(py[k][:, 0:D], h0t[:, u, k * P:(k + 1) * P], w_self[:, :],
                                            start=False, stop=True, skip_group_check=True)
                        ins.then_inc(prod, 1)

                    def front(g, u, r):
                        turn_h0(g, u, r)
                        times_a(g, u, r)

                    pipeline(pe, (1, turn_agg), (0, front), (1, project))

                @block.vector
                def _(v):
                    def aggregates(g, u, r):
                        A = agg[:, u]
                        ready(v, a_prod, g)
                        passed(v, shifted, g)
                        v.tensor_tensor(am[:, :, :], pa[:, :].rearrange("p (k d) -> p k d", k=TPG), row_bc(c_pre[:, :]),
                                        ALU.add).then_inc(a_biased, 1)
                        landed(v, got, u, r, 16 * TPG)
                        v.tensor_tensor(mean[:, :, :], A[:, :, 0:D], scalars(g, S_INV), ALU.mult).then_inc(means, 1)
                        v.tensor_tensor(sq[:, :, :], A[:, :, D:2 * D], scalars(g, S_INV), ALU.mult).then_inc(sqs, 1)
                        ready(v, a_biased, g)
                        v.tensor_tensor(am[:, :, :], am[:, :, :], scalars(g, S_HAS), ALU.mult).then_inc(a_masked, 1)
                        ready(v, means, g)
                        freed(v, std_there, g)
                        v.tensor_tensor(var[:, u], mean[:, :, :], mean[:, :, :], ALU.mult).then_inc(squares, 1)
                        ready(v, a_masked, g)
                        ready(v, sqs, g)
                        v.tensor_tensor(A[:, :, 2 * D:3 * D], A[:, :, 2 * D:3 * D], am[:, :, :], ALU.add)
                        v.tensor_tensor(A[:, :, D:2 * D], A[:, :, 3 * D:4 * D], am[:, :, :], ALU.add)
                        v.tensor_tensor(A[:, :, 0:D], mean[:, :, :], am[:, :, :], ALU.add).then_inc(shifted, 1)
                        ready(v, squares, g)
                        v.tensor_tensor(var[:, u], sq[:, :, :], var[:, u], ALU.subtract).then_inc(var_there, 1)

                    def mix(g, u, r):
                        ready(v, prod, g)
                        ready(v, xc_there, g)
                        drained(v, x_out, u, r)
                        freed(v, ln.done, g)
                        for k in range(TPG):
                            ins = v.scalar_tensor_tensor(out=x1[:, u, k, :], in0=py[k][:, D:2 * D],
                                                         scalar=scalar_of(g, S_LOG, k), in1=xc[:, u, k, :],
                                                         op0=ALU.mult, op1=ALU.add)
                        ins.then_inc(mix1, 1)
                        ready(v, mix1, g)
                        for k in range(TPG):
                            ins = v.scalar_tensor_tensor(out=x1[:, u, k, :], in0=py[k][:, 2 * D:3 * D],
                                                         scalar=scalar_of(g, S_ALOG, k), in1=x1[:, u, k, :],
                                                         op0=ALU.mult, op1=ALU.add)
                        ins.then_inc(mix2, 1)
                        ready(v, mix2, g)
                        for k in range(TPG):
                            ins = v.tensor_tensor(x1[:, u, k, :], x1[:, u, k, :], py[k][:, 0:D], ALU.add)
                        ins.then_inc(x1_there, 1)
                        ready(v, x1_there, g)
                        ln.moments_of(v, g, u)

                    def scales(g, u, r):
                        ln.scale_of(v, g, u)

                    def take_hops(g, u, r):
                        landed(v, hop_got, u, r, 16 * TPG)
                        c = slice(g * TPG, (g + 1) * TPG) if isinstance(g, int) else bass.ds(g * TPG, TPG)
                        v.tensor_copy(hop_i[:, c], hop_rows[:, u, :, 0])
                        v.tensor_copy(hop_w[:, c], hop_rows[:, u, :, 1]).then_inc(hop_taken, 1)

                    pipeline(v, (2, scales), (0, aggregates), (1, take_hops), (1, mix))

                @block.scalar
                def _(act):
                    def take_h0t(g, u, r):
                        ready(act, turned, g)
                        freed(act, prod, g)
                        act.copy(h0t[:, u, :], pt[:, :]).then_inc(h0t_there, 1)

                    def std(g, u, r):
                        ready(act, var_there, g)
                        act.activation(var[:, u], var[:, u], ACT.Relu).then_inc(relud, 1)
                        ready(act, relud, g)
                        ready(act, shifted, g)
                        act.activation(agg[:, u, :, 3 * D:4 * D], var[:, u], ACT.Sqrt, bias=eps[:, :])\
                            .then_inc(std_there, 1)

                    def take_agg(g, u, r):
                        for q in range(4):
                            act.wait_ge(q_turned, g * 4 + q + 1)
                            if q == 0:
                                passed(act, prod, g)
                            act.copy(aggt[:, q, :], pq[q % 2][:, :]).then_inc(q_taken, 1)

                    def norm(g, u, r):
                        ln.root_of(act, g, u)
                        drained(act, h_out, u, r)
                        ln.relu_of(act, g, u)

                    def store(g, u, r):
                        ready(act, x1_there, g)
                        act.dma_start(rows_of(x1_tab, g), x1[:, u, :, :]).then_inc(x_out[u], 16)
                        ready(act, ln.done, g)
                        act.dma_start(rows_of(h1_tab, g), h1[:, u, :, :]).then_inc(h_out[u], 16)

                    pipeline(act, (1, take_agg), (0, take_h0t), (2, norm), (2, store), (0, std))

        with ExitStack() as c2:
            S = Scope(nc, c2, "m1")
            h1 = S.sb("h1", [P, 2, TPG, D])
            h1t, m1t, m2t = (S.sb(n, [P, 2, ROWS]) for n in ("h1t", "m1t", "m2t"))
            raw = S.sb("raw", [P, 2, TPG, D])
            msg = S.sb("msg", [P, 2, TPG, W_MSG])
            dlog = S.sb("dlog", [P, 2, TPG, 4])
            pt, p1, p2 = (S.ps(n, [P, ROWS]) for n in ("pt", "p1", "p2"))
            p3 = [S.ps(f"p3_{u}", [P, ROWS]) for u in range(2)]
            p4 = [S.ps(f"p4_{u}", [P, TPG, 6]) for u in range(2)]
            h_in, m_out, d_out = S.pair("h_in"), S.pair("m_out"), S.pair("d_out")
            turned, h1t_there, prod1, m1_there, prod2, m2_there, prod3, raw_there, d_there, msg_there, cleared = (
                S.sem(n) for n in ("turned", "h1t_there", "prod1", "m1_there", "prod2", "m2_there", "prod3",
                                   "raw_there", "d_there", "msg_there", "cleared"))
            with nc.Block() as block:
                @block.sync
                def _(sp):
                    def load(g, u, r):
                        freed(sp, turned, g)
                        sp.dma_start(h1[:, u, :, :], rows_of(h1_tab, g)).then_inc(h_in[u], 16)

                    pipeline(sp, load)
                    end_of(sp, m_out)
                    end_of(sp, d_out)

                @block.tensor
                def _(pe):
                    def turn_h(g, u, r):
                        landed(pe, h_in, u, r)
                        passed(pe, h1t_there, g)
                        turn(pe, pt, h1[:, u], turned)

                    def first(g, u, r):
                        ready(pe, h1t_there, g)
                        passed(pe, m1_there, g)
                        pe.matmul(p1[:, :], w_m1[:, :], h1t[:, u, :], start=True, stop=True).then_inc(prod1, 1)

                    def second(g, u, r):
                        ready(pe, m1_there, g)
                        passed(pe, m2_there, g)
                        pe.matmul(p2[:, :], w_m2[:, :], m1t[:, u, :], start=True, stop=True).then_inc(prod2, 1)

                    def third(g, u, r):
                        ready(pe, m2_there, g)
                        freed(pe, raw_there, g)
                        freed(pe, d_there, g)
                        for k in range(TPG):
                            rows = slice(k * P, (k + 1) * P)
                            pe.matmul(p4[u][:, k, :], h1t[:, u, rows], w_att[:, :], start=True, stop=True)
                            ins = pe.matmul(p3[u][:, k * D:(k + 1) * D], m2t[:, u, rows], w_m3[:, :],
                                            start=True, stop=True)
                        ins.then_inc(prod3, 1)

                    pipeline(pe, (0, turn_h), (2, third), (1, second), (0, first))

                @block.scalar
                def _(act):
                    def take_h(g, u, r):
                        ready(act, turned, g)
                        freed(act, prod3, g)
                        act.copy(h1t[:, u, :], pt[:, :]).then_inc(h1t_there, 1)

                    def relu1(g, u, r):
                        ready(act, prod1, g)
                        freed(act, prod2, g)
                        act.activation(m1t[:, u, :], p1[:, :], ACT.Relu, bias=c_m1[:, :]).then_inc(m1_there, 1)

                    def relu2(g, u, r):
                        ready(act, prod2, g)
                        freed(act, prod3, g)
                        act.activation(m2t[:, u, :], p2[:, :], ACT.Relu, bias=c_m2[:, :]).then_inc(m2_there, 1)

                    def relu3(g, u, r):
                        ready(act, raw_there, g)
                        drained(act, m_out, u, r)
                        act.activation(msg[:, u, :, 0:D], raw[:, u], ACT.Relu).then_inc(msg_there, 1)

                    def store(g, u, r):
                        ready(act, msg_there, g)
                        act.dma_start(rows_of(m1_tab, g), msg[:, u, :, :]).then_inc(m_out[u], 16)
                        ready(act, d_there, g)
                        act.dma_start(rows_of(d1_tab, g), dlog[:, u, :, :]).then_inc(d_out[u], 16)

                    pipeline(act, (0, take_h), (1, relu2), (0, relu1), (2, relu3), (2, store))

                @block.vector
                def _(v):
                    v.memset(msg[:, :, :, D + 3:D + 4], 0.0)
                    v.memset(dlog[:, :, :, 3:4], 0.0).then_inc(cleared, 1)

                    def take(g, u, r):
                        ready(v, prod3, g)
                        freed(v, msg_there, g)
                        drained(v, m_out, u, r)
                        v.tensor_tensor(raw[:, u], p3[u][:, :].rearrange("p (k d) -> p k d", k=TPG),
                                        row_bc(c_m3[:, :]), ALU.add)
                        v.tensor_copy(msg[:, u, :, D:D + 3], p4[u][:, :, 0:3]).then_inc(raw_there, 1)
                        drained(v, d_out, u, r)
                        v.tensor_tensor(dlog[:, u, :, 0:3], p4[u][:, :, 3:6],
                                        c_att[:, 0:3].unsqueeze(1).to_broadcast([P, TPG, 3]), ALU.add).then_inc(d_there, 1)

                    pipeline(v, (2, take))

        with ExitStack() as c2:
            S = Scope(nc, c2, "e1")
            rows = S.sb("rows", [P, 2, TPG, W_MSG])
            drow = S.sb("drow", [P, 2, TPG, 4])
            stage, dstage = S.sb("stage", [P, 2, TPG], I32), S.sb("dstage", [P, 2, TPG], I32)
            logit = S.sb("logit", [P, 2, TPG, 3])
            weight = S.sb("weight", [P, 2, TPG, 3])
            scaled = S.sb("scaled", [P, 2, TPG, 3, D])
            run = [S.sb(f"run{j}", [P, 2, ROWS]) for j in range(3)]
            runw = S.sb("runw", [3, 2, ROWS])
            res = S.sb("res", [P, 2, TPG, W_ATT])
            pt = [S.ps(f"pt{j}", [P, ROWS]) for j in range(3)]
            pw = S.ps("pw", [3, ROWS])
            pr = [S.ps(f"pr{j}", [P, ROWS]) for j in range(3)]
            prw = S.ps("prw", [P, TPG, 4])
            got, dgot, res_out = S.pair("got"), S.pair("dgot"), S.pair("res_out")
            (staged, dstaged, sent, logits, logits2, weights, scaled_there, cleared, held) = (
                S.sem(n) for n in ("staged", "dstaged", "sent", "logits", "logits2", "weights", "scaled_there", "cleared", "held"))
            turned = [S.sem(f"turned{j}") for j in range(4)]
            scanned = [S.sem(f"scanned{j}") for j in range(4)]
            back = [S.sem(f"back{j}") for j in range(4)]
            taken = [S.sem(f"taken{j}") for j in range(4)]

            with nc.Block() as block:
                @block.gpsimd
                def _(pool):
                    used = lambda p, g: freed(p, scaled_there, g)
                    one = gather_steps(pool, m1_tab, rows, src_i, stage, staged, got, sent, used)
                    two = gather_steps(pool, d1_tab, drow, dst_i, dstage, dstaged, dgot, sent, used)

                    def both(g, u, r):
                        one(g, u, r)
                        two(g, u, r)

                    pipeline(pool, both)

                @block.vector
                def _(v):
                    for j in range(3):
                        v.memset(run[j][:, 1, ROWS - 1:ROWS], 0.0).then_inc(scanned[j], 1)
                    v.memset(runw[:, 1, ROWS - 1:ROWS], 0.0).then_inc(scanned[3], 1)
                    v.memset(res[:, :, :, 3 * D + 3:W_ATT], 0.0).then_inc(cleared, 1)

                    def logits_of(g, u, r):
                        landed(v, got, u, r, 16 * TPG)
                        landed(v, dgot, u, r, 16 * TPG)
                        freed(v, weights, g)
                        v.tensor_tensor(logit[:, u], rows[:, u, :, D:D + 3], drow[:, u, :, 0:3], ALU.add)\
                            .then_inc(logits, 1)
                        ready(v, logits, g)
                        v.tensor_scalar(logit[:, u], logit[:, u], 0.0, None, ALU.max).then_inc(logits2, 1)

                    def scale_rows(g, u, r):
                        ready(v, weights, g)
                        for j in range(4):
                            freed(v, turned[j], g)
                        for k in range(TPG):
                            ins = v.tensor_tensor(scaled[:, u, k], rows[:, u, k, 0:D].unsqueeze(1).to_broadcast([P, 3, D]),
                                                  bc(weight[:, u, k, :], D), ALU.mult)
                        ins.then_inc(scaled_there, 1)

                    def scans(g, u, r):
                        m = keep[:, g * ROWS:(g + 1) * ROWS] if isinstance(g, int) else keep[:, bass.ds(g * ROWS, ROWS)]
                        for j in range(4):
                            ready(v, turned[j], g)
                            v.wait_ge(scanned[j], g + 1)
                            freed(v, back[j], g)
                            t, p = (run[j], pt[j]) if j < 3 else (runw, pw)
                            n = P if j < 3 else 3
                            v.tensor_tensor_scan(t[:, u, :], m[0:n], p[:, :], t[:, 1 - u, ROWS - 1:ROWS],
                                                 ALU.mult, ALU.add).then_inc(scanned[j], 1)

                    pipeline(v, logits_of, scale_rows, scans)

                @block.scalar
                def _(act):
                    def exps(g, u, r):
                        ready(act, logits2, g)
                        freed(act, scaled_there, g)
                        freed(act, turned[3], g)
                        act.activation(weight[:, u], logit[:, u], ACT.Exp).then_inc(weights, 1)

                    def take_back(g, u, r):
                        for j in range(4):
                            ready(act, back[j], g)
                            if j == 0:
                                drained(act, res_out, u, r)
                            if j < 3:
                                act.copy(res[:, u, :, j * D:(j + 1) * D],
                                         pr[j][:, :].rearrange("p (k d) -> p k d", k=TPG)).then_inc(taken[j], 1)
                            else:
                                act.copy(res[:, u, :, 3 * D:3 * D + 3], prw[:, :, 0:3]).then_inc(taken[3], 1)

                    def store(g, u, r):
                        ready(act, taken[3], g)
                        act.dma_start(edge_rows_of(e1_tab, g), res[:, u, :, :]).then_inc(res_out[u], 16)

                    act.wait_ge(cleared, 1)
                    pipeline(act, (0, exps), (2, take_back), (2, store))

                @block.tensor
                def _(pe):
                    def turn_in(g, u, r):
                        ready(pe, scaled_there, g)
                        for j in range(3):
                            pe.wait_ge(scanned[j], g + 1)
                            turn(pe, pt[j], scaled[:, u, :, j, :], turned[j])
                        pe.wait_ge(scanned[3], g + 1)
                        pe.sem_inc(held, 1)
                        for k in range(TPG):
                            ins = pe.transpose(pw[0:3, k * P:(k + 1) * P], weight[:, u, k, :], ident[:, :])
                        ins.then_inc(turned[3], 1)

                    def turn_back(g, u, r):
                        for j in range(3):
                            pe.wait_ge(scanned[j], g + 2)
                            passed(pe, taken[j], g)
                            for k in range(TPG):
                                ins = pe.transpose(pr[j][:, k * P:(k + 1) * P], run[j][:, u, k * P:(k + 1) * P],
                                                   ident[:, :])
                            ins.then_inc(back[j], 1)
                        pe.wait_ge(scanned[3], g + 2)
                        passed(pe, taken[3], g)
                        pe.sem_inc(held, 1)
                        for k in range(TPG):
                            ins = pe.transpose(prw[:, k, 0:3], runw[0:3, u, k * P:(k + 1) * P], ident[0:3, 0:3])
                        ins.then_inc(back[3], 1)

                    pipeline(pe, turn_in, turn_back)

                @block.sync
                def _(sp):
                    end_of(sp, res_out)

        with ExitStack() as c2:
            S = Scope(nc, c2, "n2")
            x1, h1 = S.sb("x1", [P, 2, TPG, D]), S.sb("h1", [P, 2, TPG, D])
            x1c = S.sb("x1c", [P, 2, TPG, D])
            sums = S.sb("sums", [P, 2, TPG, W_ATT])
            stage = S.sb("stage", [P, 2, TPG], I32)
            wsum = S.sb("wsum", [P, TPG, 3])
            winv = S.sb("winv", [P, TPG, 3])
            wnode = S.sb("wnode", [P, TPG, 3])
            hn = S.sb("hn", [P, 2, TPG, D])
            h1t, hnt, ut, h2t = (S.sb(n, [P, 2, ROWS]) for n in ("h1t", "hnt", "ut", "h2t"))
            x2, h2, t2 = (S.sb(n, [P, 2, TPG, D]) for n in ("x2", "h2", "t2"))
            pt, pn, pu, pt2 = (S.ps(n, [P, ROWS]) for n in ("pt", "pn", "pu", "pt2"))
            po = [S.ps(f"po{u}", [P, ROWS]) for u in range(2)]
            pg = [S.ps(f"pg{u}", [P, ROWS]) for u in range(2)]
            got, x_in, h_in, x_out, t_out = (S.pair(n) for n in ("got", "x_in", "h_in", "x_out", "t_out"))
            (staged, sent, w_floor, w_inv, w_there, hn1, hn2, hn_there, h_turned, n_turned, h1t_there, hnt_there, u_prod,
             u_there, o_prod, x1c_there, x2_there, h2_turned, h2t_there, g_prod, t2_there) = (S.sem(n) for n in (
                 "staged", "sent", "w_floor", "w_inv", "w_there", "hn1", "hn2", "hn_there", "h_turned", "n_turned",
                 "h1t_there", "hnt_there", "u_prod", "u_there", "o_prod", "x1c_there", "x2_there", "h2_turned",
                 "h2t_there", "g_prod", "t2_there"))
            ln = Norm(S, lambda u: x2[:, u], lambda u: h2[:, u])

            with nc.Block() as block:
                @block.gpsimd
                def _(pool):
                    gather = gather_steps(pool, e1_tab, sums, last_i, stage, staged, got, sent,
                                          lambda p, g: freed(p, hn_there, g))

                    def add_bias(g, u, r):
                        landed(pool, x_in, u, r)
                        pool.sem_inc(sent, 1)
                        freed(pool, x2_there, g)
                        pool.sem_inc(sent, 1)
                        pool.tensor_tensor(x1c[:, u], x1[:, u], row_bc(c_c2[:, :]), ALU.add).then_inc(x1c_there, 1)

                    pipeline(pool, gather, add_bias)

                @block.sync
                def _(sp):
                    def load(g, u, r):
                        freed(sp, x1c_there, g)
                        sp.dma_start(x1[:, u, :, :], rows_of(x1_tab, g)).then_inc(x_in[u], 16)
                        freed(sp, h_turned, g)
                        sp.dma_start(h1[:, u, :, :], rows_of(h1_tab, g)).then_inc(h_in[u], 16)

                    pipeline(sp, load)
                    end_of(sp, x_out)
                    end_of(sp, t_out)

                @block.vector
                def _(v):
                    def neighbours(g, u, r):
                        landed(v, got, u, r, 16 * TPG)
                        v.tensor_scalar(wsum[:, :, :], sums[:, u, :, 3 * D:3 * D + 3], 1.0, None, ALU.max).then_inc(w_floor, 1)
                        ready(v, w_floor, g)
                        v.reciprocal(winv[:, :, :], wsum[:, :, :]).then_inc(w_inv, 1)
                        ready(v, w_inv, g)
                        third = nsc[:, g, S_THIRD, :] if isinstance(g, int) else nsc[:, bass.ds(g, 1), S_THIRD, :]\
                            .rearrange("p o k -> p (o k)")
                        v.tensor_tensor(wnode[:, :, :], winv[:, :, :], bc(third, 3), ALU.mult).then_inc(w_there, 1)
                        ready(v, w_there, g)
                        freed(v, n_turned, g)
                        for k in range(TPG):
                            ins = v.tensor_scalar(hn[:, u, k, :], sums[:, u, k, 0:D], wnode[:, k, 0:1], None, ALU.mult)
                        ins.then_inc(hn1, 1)
                        for j, (before_, after_) in ((1, (hn1, hn2)), (2, (hn2, hn_there))):
                            ready(v, before_, g)
                            for k in range(TPG):
                                ins = v.scalar_tensor_tensor(out=hn[:, u, k, :], in0=sums[:, u, k, j * D:(j + 1) * D],
                                                             scalar=wnode[:, k, j:j + 1], in1=hn[:, u, k, :],
                                                             op0=ALU.mult, op1=ALU.add)
                            ins.then_inc(after_, 1)

                    def update(g, u, r):
                        ready(v, o_prod, g)
                        ready(v, x1c_there, g)
                        drained(v, x_out, u, r)
                        freed(v, ln.done, g)
                        v.tensor_tensor(flat(x2[:, u]), flat(x1c[:, u]), po[u][:, :], ALU.add).then_inc(x2_there, 1)
                        ready(v, x2_there, g)
                        ln.moments_of(v, g, u)

                    def scales(g, u, r):
                        ln.scale_of(v, g, u)

                    def gcn_rows(g, u, r):
                        ready(v, g_prod, g)
                        drained(v, t_out, u, r)
                        v.tensor_tensor(t2[:, u], pg[u][:, :].rearrange("p (k d) -> p k d", k=TPG), scalars(g, S_GCN),
                                        ALU.mult).then_inc(t2_there, 1)

                    pipeline(v, (2, scales), (0, neighbours), (3, gcn_rows), (1, update))

                @block.scalar
                def _(act):
                    def take_in(g, u, r):
                        ready(act, h_turned, g)
                        freed(act, u_prod, g)
                        act.copy(h1t[:, u, :], pt[:, :]).then_inc(h1t_there, 1)
                        ready(act, n_turned, g)
                        act.copy(hnt[:, u, :], pn[:, :]).then_inc(hnt_there, 1)

                    def relu_u(g, u, r):
                        ready(act, u_prod, g)
                        freed(act, o_prod, g)
                        act.activation(ut[:, u, :], pu[:, :], ACT.Relu, bias=c_c1[:, :]).then_inc(u_there, 1)

                    def norm(g, u, r):
                        ln.root_of(act, g, u)
                        freed(act, h2_turned, g)
                        ln.relu_of(act, g, u)

                    def take_h2(g, u, r):
                        ready(act, h2_turned, g)
                        freed(act, g_prod, g)
                        act.copy(h2t[:, u, :], pt2[:, :]).then_inc(h2t_there, 1)

                    def store(g, u, r):
                        ready(act, x2_there, g)
                        act.dma_start(rows_of(x2_tab, g), x2[:, u, :, :]).then_inc(x_out[u], 16)

                    def store_t(g, u, r):
                        ready(act, t2_there, g)
                        act.dma_start(rows_of(t2_tab, g), t2[:, u, :, :]).then_inc(t_out[u], 16)

                    pipeline(act, (2, norm), (2, store), (0, take_in), (2, take_h2), (3, store_t), (0, relu_u))

                @block.tensor
                def _(pe):
                    def turn_in(g, u, r):
                        landed(pe, h_in, u, r)
                        passed(pe, h1t_there, g)
                        turn(pe, pt, h1[:, u], h_turned)
                        ready(pe, hn_there, g)
                        passed(pe, hnt_there, g)
                        turn(pe, pn, hn[:, u], n_turned)

                    def hidden(g, u, r):
                        ready(pe, hnt_there, g)
                        passed(pe, u_there, g)
                        pe.matmul(pu[:, :], w_c1a[:, :], h1t[:, u, :], start=True, stop=False)
                        pe.matmul(pu[:, :], w_c1b[:, :], hnt[:, u, :], start=False, stop=True).then_inc(u_prod, 1)

                    def output(g, u, r):
                        ready(pe, u_there, g)
                        freed(pe, x2_there, g)
                        for k in range(TPG):
                            ins = pe.matmul(po[u][:, k * D:(k + 1) * D], ut[:, u, k * P:(k + 1) * P], w_c2[:, :],
                                            start=True, stop=True)
                        ins.then_inc(o_prod, 1)

                    def turn_h2(g, u, r):
                        ready(pe, ln.done, g)
                        passed(pe, h2t_there, g)
                        turn(pe, pt2, h2[:, u], h2_turned)

                    def gcn(g, u, r):
                        ready(pe, h2t_there, g)
                        freed(pe, t2_there, g)
                        for k in range(TPG):
                            ins = pe.matmul(pg[u][:, k * D:(k + 1) * D], h2t[:, u, k * P:(k + 1) * P], w_gcn[:, :],
                                            start=True, stop=True)
                        ins.then_inc(g_prod, 1)

                    pipeline(pe, (1, output), (2, turn_h2), (0, turn_in), (2, gcn), (0, hidden))

        def edge_sums(name, table, index, weights, out_tab, sum_in=None, sum_out=None):
            with ExitStack() as c2:
                S = Scope(nc, c2, name)
                rows = S.sb("rows", [P, 2, TPG, D])
                scaled = S.sb("scaled", [P, 2, TPG, D])
                stage = S.sb("stage", [P, 2, TPG], I32)
                run = S.sb("run", [P, 2, ROWS])
                res, tot, more = (S.sb(n, [P, 2, TPG, D]) for n in ("res", "tot", "more"))
                pt = [S.ps(f"pt{u}", [P, ROWS]) for u in range(2)]
                pr = [S.ps(f"pr{u}", [P, ROWS]) for u in range(2)]
                got, res_out, tot_out, more_in = (S.pair(n) for n in ("got", "res_out", "tot_out", "more_in"))
                staged, sent, weighted, turned, scanned, back, res_there, tot_there = (S.sem(n) for n in (
                    "staged", "sent", "weighted", "turned", "scanned", "back", "res_there", "tot_there"))
                with nc.Block() as block:
                    @block.gpsimd
                    def _(pool):
                        pipeline(pool, gather_steps(pool, table, rows, index, stage, staged, got, sent,
                                                    lambda p, g: freed(p, weighted if weights is not None else turned, g)))

                    @block.tensor
                    def _(pe):
                        def turn_in(g, u, r):
                            if weights is not None:
                                ready(pe, weighted, g)
                            else:
                                landed(pe, got, u, r, 16 * TPG)
                            if not at_start(g):
                                pe.wait_ge(scanned, g)
                            turn(pe, pt[u], (rows if weights is None else scaled)[:, u], turned)

                        def turn_back(g, u, r):
                            pe.wait_ge(scanned, g + 2)
                            freed(pe, res_there if out_tab is not None else tot_there, g)
                            if out_tab is not None and sum_in is not None:
                                freed(pe, tot_there, g)
                            for k in range(TPG):
                                ins = pe.transpose(pr[u][:, k * P:(k + 1) * P], run[:, u, k * P:(k + 1) * P], ident[:, :])
                            ins.then_inc(back, 1)

                        pipeline(pe, turn_in, turn_back)

                    @block.vector
                    def _(v):
                        v.memset(run[:, 1, ROWS - 1:ROWS], 0.0).then_inc(scanned, 1)

                        def scan(g, u, r):
                            m = keep[:, g * ROWS:(g + 1) * ROWS] if isinstance(g, int) else keep[:, bass.ds(g * ROWS, ROWS)]
                            ready(v, turned, g)
                            v.wait_ge(scanned, g + 1)
                            freed(v, back, g)
                            v.tensor_tensor_scan(run[:, u, :], m, pt[u][:, :], run[:, 1 - u, ROWS - 1:ROWS],
                                                 ALU.mult, ALU.add).then_inc(scanned, 1)

                        def total(g, u, r):
                            landed(v, more_in, u, r)
                            drained(v, tot_out, u, r)
                            if out_tab is not None:
                                ready(v, res_there, g)
                                v.tensor_tensor(tot[:, u], res[:, u], more[:, u], ALU.add).then_inc(tot_there, 1)
                            else:
                                ready(v, back, g)
                                v.tensor_tensor(flat(tot[:, u]), pr[u][:, :], flat(more[:, u]), ALU.add).then_inc(tot_there, 1)

                        pipeline(v, *([(0, scan)] + [(2, total)] * (sum_in is not None)))

                    if True:
                        @block.scalar
                        def _(act):
                            def weigh(g, u, r):
                                landed(act, got, u, r, 16 * TPG)
                                freed(act, turned, g)
                                for k in range(TPG):
                                    c = slice(g * TPG + k, g * TPG + k + 1) if isinstance(g, int) else bass.ds(g * TPG + k, 1)
                                    ins = act.activation(scaled[:, u, k, :], rows[:, u, k, :], ACT.Copy, scale=weights[:, c])
                                ins.then_inc(weighted, 1)

                            def take(g, u, r):
                                ready(act, back, g)
                                drained(act, res_out, u, r)
                                if sum_in is not None:
                                    freed(act, tot_there, g)
                                act.copy(flat(res[:, u]), pr[u][:, :]).then_inc(res_there, 1)

                            def store(g, u, r):
                                ready(act, res_there, g)
                                act.dma_start(edge_rows_of(out_tab, g), res[:, u, :, :]).then_inc(res_out[u], 16)

                            def store_tot(g, u, r):
                                ready(act, tot_there, g)
                                act.dma_start(edge_rows_of(sum_out, g), tot[:, u, :, :]).then_inc(tot_out[u], 16)

                            pipeline(act, *([(0, weigh)] * (weights is not None)
                                            + [(1, take), (1, store)] * (out_tab is not None)
                                            + [(3, store_tot)] * (sum_in is not None)))

                    @block.sync
                    def _(sp):
                        def load(g, u, r):
                            freed(sp, tot_there, g)
                            sp.dma_start(more[:, u, :, :], edge_rows_of(sum_in, g)).then_inc(more_in[u], 16)

                        if sum_in is not None:
                            pipeline(sp, load)
                        if out_tab is not None:
                            end_of(sp, res_out)
                        if sum_in is not None:
                            end_of(sp, tot_out)

        edge_sums("e2", t2_tab, src_i, None, e2_tab)

        with ExitStack() as c2:
            S = Scope(nc, c2, "n3")
            e2, x2, t2, x2c, s2, x3, h3, z0, y = (S.sb(n, [P, 2, TPG, D]) for n in (
                "e2", "x2", "t2", "x2c", "s2", "x3", "h3", "z0", "y"))
            stage = S.sb("stage", [P, 2, TPG], I32)
            got, x_in, t_in, z_out, y_out = (S.pair(n) for n in ("got", "x_in", "t_in", "z_out", "y_out"))
            staged, sent, x2c_there, sum1, sum2, x3_there, z0_there, y_there = (S.sem(n) for n in (
                "staged", "sent", "x2c_there", "sum1", "sum2", "x3_there", "z0_there", "y_there"))
            ln = Norm(S, lambda u: x3[:, u], lambda u: h3[:, u])
            with nc.Block() as block:
                @block.gpsimd
                def _(pool):
                    gather = gather_steps(pool, e2_tab, e2, last_i, stage, staged, got, sent,
                                          lambda p, g: freed(p, sum1, g))

                    pipeline(pool, gather)

                @block.sync
                def _(sp):
                    def load(g, u, r):
                        freed(sp, x2c_there, g)
                        sp.dma_start(x2[:, u, :, :], rows_of(x2_tab, g)).then_inc(x_in[u], 16)
                        freed(sp, sum1, g)
                        sp.dma_start(t2[:, u, :, :], rows_of(t2_tab, g)).then_inc(t_in[u], 16)

                    pipeline(sp, load)
                    end_of(sp, z_out)
                    end_of(sp, y_out)

                @block.vector
                def _(v):
                    def update(g, u, r):
                        landed(v, x_in, u, r)
                        freed(v, x3_there, g)
                        v.tensor_tensor(x2c[:, u], x2[:, u], row_bc(c_gcn[:, :]), ALU.add).then_inc(x2c_there, 1)
                        landed(v, got, u, r, 16 * TPG)
                        landed(v, t_in, u, r)
                        v.tensor_tensor(s2[:, u], e2[:, u], t2[:, u], ALU.add).then_inc(sum1, 1)
                        ready(v, sum1, g)
                        v.tensor_tensor(s2[:, u], s2[:, u], scalars(g, S_GCN), ALU.mult).then_inc(sum2, 1)
                        ready(v, sum2, g)
                        ready(v, x2c_there, g)
                        freed(v, ln.done, g)
                        freed(v, y_there, g)
                        v.tensor_tensor(x3[:, u], s2[:, u], x2c[:, u], ALU.add).then_inc(x3_there, 1)
                        ready(v, x3_there, g)
                        ln.moments_of(v, g, u)

                    def scales(g, u, r):
                        ln.scale_of(v, g, u)

                    def outputs(g, u, r):
                        ready(v, ln.done, g)
                        drained(v, z_out, u, r)
                        v.tensor_tensor(z0[:, u], h3[:, u], scalars(g, S_DINV), ALU.mult).then_inc(z0_there, 1)
                        drained(v, y_out, u, r)
                        v.scalar_tensor_tensor(out=y[:, u], in0=h3[:, u], scalar=0.25, in1=x3[:, u],
                                               op0=ALU.mult, op1=ALU.add).then_inc(y_there, 1)

                    pipeline(v, (1, scales), (0, update), (1, outputs))

                @block.scalar
                def _(act):
                    def norm(g, u, r):
                        ln.root_of(act, g, u)
                        freed(act, y_there, g)
                        ln.relu_of(act, g, u)

                    def store(g, u, r):
                        ready(act, z0_there, g)
                        act.dma_start(rows_of(z0_tab, g), z0[:, u, :, :]).then_inc(z_out[u], 16)
                        ready(act, y_there, g)
                        act.dma_start(rows_of(y_tab, g), y[:, u, :, :]).then_inc(y_out[u], 16)

                    pipeline(act, (0, norm), (2, store))

        edge_sums("g1", z0_tab, src_i, None, r1_tab)
        edge_sums("g2", r1_tab, hop_i, hop_w, r2_tab, sum_in=r1_tab, sum_out=a2_tab)
        edge_sums("g3", r2_tab, hop_i, hop_w, None, sum_in=a2_tab, sum_out=a3_tab)

        with ExitStack() as c2:
            S = Scope(nc, c2, "n4")
            e3, y, s3, res = (S.sb(n, [P, 2, TPG, D]) for n in ("e3", "y", "s3", "res"))
            stage = S.sb("stage", [P, 2, TPG], I32)
            got, y_in, res_out = (S.pair(n) for n in ("got", "y_in", "res_out"))
            staged, sent, scaled, res_there = (S.sem(n) for n in ("staged", "sent", "scaled", "res_there"))
            with nc.Block() as block:
                @block.gpsimd
                def _(pool):
                    pipeline(pool, gather_steps(pool, a3_tab, e3, last_i, stage, staged, got, sent,
                                                lambda p, g: freed(p, scaled, g)))

                @block.vector
                def _(v):
                    def update(g, u, r):
                        landed(v, got, u, r, 16 * TPG)
                        v.tensor_tensor(s3[:, u], e3[:, u], scalars(g, S_DINV), ALU.mult).then_inc(scaled, 1)
                        ready(v, scaled, g)
                        landed(v, y_in, u, r)
                        drained(v, res_out, u, r)
                        v.scalar_tensor_tensor(out=res[:, u], in0=s3[:, u], scalar=0.25, in1=y[:, u],
                                               op0=ALU.mult, op1=ALU.add).then_inc(res_there, 1)

                    pipeline(v, update)

                @block.sync
                def _(sp):
                    def load(g, u, r):
                        freed(sp, res_there, g)
                        sp.dma_start(y[:, u, :, :], rows_of(y_tab, g)).then_inc(y_in[u], 16)

                    pipeline(sp, load)
                    end_of(sp, res_out)

                @block.scalar
                def _(act):
                    def store(g, u, r):
                        ready(act, res_there, g)
                        if is_last(g):
                            act.dma_start(tail_rows(out), res[0:LAST_P, u, :, :]).then_inc(res_out[u], 16)
                        else:
                            t = out[0:(GROUPS - 1) * ROWS, :].rearrange("(g p k) d -> g p k d", p=P, k=TPG)
                            t = t[g] if isinstance(g, int) else t[bass.ds(g, 1)].rearrange("o p k d -> (o p) k d")
                            act.dma_start(t, res[:, u, :, :]).then_inc(res_out[u], 16)

                    pipeline(act, store)


_OUT = ((N, D), "float32")


def kernel(**inputs):
    import numpy as np
    import concourse.bacc as bacc
    from concourse.bass_utils import run_bass_kernel_spmd as run

    nc = bacc.Bacc("TRN2", target_bir_lowering=False, num_devices=1)
    arrays, aps = {}, {}
    for name, value in inputs.items():
        v = np.ascontiguousarray(value)
        arrays["in_" + name] = v
        aps[name] = nc.dram_tensor("in_" + name, v.shape, mybir.dt.from_np(v.dtype), kind="ExternalInput").ap()
    out = nc.dram_tensor("out_x", _OUT[0], F32, kind="ExternalOutput").ap()
    build(nc, aps, out)
    r = run(nc, [arrays], core_ids=[0])
    return r.results[0]["out_x"]
```

```python
from contextlib import ExitStack

import concourse.bass as bass
from concourse import mybir

F32 = mybir.dt.float32
BF16 = mybir.dt.bfloat16
I32 = mybir.dt.int32
U8 = mybir.dt.uint8
U16 = mybir.dt.uint16
ALU = mybir.AluOpType
ACT = mybir.ActivationFunctionType
AX_X = mybir.AxisListType.X

P = 128
D = 128
N = 50000
E = 50000
ED = 10
TPG = 4
ROWS = TPG * P
GROUPS = 98
TILES = GROUPS * TPG
NPAD = GROUPS * ROWS
ZERO_ROW = NPAD
LAST_P = (N - (GROUPS - 1) * ROWS) // TPG
NO_NODE = 60000
ORD_C, ORD_P = 400, 125
EPS = 1e-5
BIG = 3.0e38
W_MSG = D + 4
W_ATT = 3 * D + 4
NSC = 7
(S_INV, S_HAS, S_LOG, S_ALOG, S_GCN, S_DINV, S_THIRD) = range(NSC)
assert ORD_C * ORD_P == E
assert LAST_P * TPG + (GROUPS - 1) * ROWS == N and GROUPS % 2 == 0


def pipeline(eng, *stages):
    stages = [s if isinstance(s, tuple) else (n, s) for n, s in enumerate(stages) if s is not None]
    depth = max(delay for delay, _ in stages)
    head = 2 + depth + (depth % 2)

    def peeled(steps):
        for t in steps:
            for s, stage in stages:
                if 0 <= t - s < GROUPS:
                    stage(t - s, (t - s) % 2, (t - s) // 2)

    peeled(range(head))
    with eng.Fori(head // 2, GROUPS // 2 - 1) as j:
        for v in range(2):
            for s, stage in stages:
                back, slot = (v - s) // 2, (v - s) % 2
                stage(j * 2 + (2 * back + slot), slot, j + back)
    peeled(range(GROUPS - 2, GROUPS + depth))


def at_start(g):
    return isinstance(g, int) and g < 2


def ready(eng, sem, g, per=1):
    eng.wait_ge(sem, (g + 1) * per)


def freed(eng, sem, g, per=1):
    if not at_start(g):
        eng.wait_ge(sem, (g - 1) * per)


def passed(eng, sem, g, per=1):
    if not (isinstance(g, int) and g == 0):
        eng.wait_ge(sem, g * per)


def landed(eng, sems, u, r, inc=16):
    eng.wait_ge(sems[u], (r + 1) * inc)


def drained(eng, sems, u, r, inc=16):
    if not (isinstance(r, int) and r == 0):
        eng.wait_ge(sems[u], r * inc)


def rows_of(table, g, cols=None):
    t = table[0:NPAD, :].rearrange("(g p k) d -> g p k d", p=P, k=TPG)
    return t[g] if isinstance(g, int) else t[bass.ds(g, 1)].rearrange("o p k d -> (o p) k d")


def edge_rows_of(table, g):
    t = table[0:NPAD, :].rearrange("(g k p) d -> g p k d", p=P, k=TPG)
    return t[g] if isinstance(g, int) else t[bass.ds(g, 1)].rearrange("o p k d -> (o p) k d")


def tail_rows(table):
    return table[(GROUPS - 1) * ROWS:N, :].rearrange("(p k) d -> p k d", k=TPG)


def is_last(g):
    return isinstance(g, int) and g == GROUPS - 1


def bc(ap, n):
    return ap.unsqueeze(2).to_broadcast([ap.shape[0], ap.shape[1], n])


class Chain:

    def __init__(self, eng, sem):
        self.eng, self.sem, self.n = eng, sem, 0

    def __call__(self, ins):
        self.n += 1
        ins.then_inc(self.sem, 1)
        self.eng.wait_ge(self.sem, self.n)


class Scope:

    def __init__(self, nc, ctx, name):
        self.nc, self.ctx, self.name, self.sems = nc, ctx, name, []
        ctx.callback(self.release)

    def release(self):
        if self.sems:
            self.nc.clear_and_free_semaphores(self.sems)
            self.nc.all_engine_barrier()

    def sb(self, name, shape, dt=F32):
        return self.ctx.enter_context(self.nc.sbuf_tensor(f"{self.name}_{name}", shape, dt))

    def ps(self, name, shape, dt=F32):
        return self.ctx.enter_context(self.nc.psum_tensor(f"{self.name}_{name}", shape, dt))

    def sem(self, name):
        self.sems.append(self.nc.alloc_semaphore(f"{self.name}_{name}"))
        return self.sems[-1]

    def pair(self, name):
        return [self.sem(f"{name}{u}") for u in range(2)]

def order_edges(nc, a):
    tab = lambda name, shape, dt: nc.dram_tensor(name, shape, dt).ap()
    o_dst, o_src = tab("o_dst", (E, 1), I32), tab("o_src", (E, 1), I32)
    o_attr = tab("o_attr", (E, ED), F32)
    key_row, place_row = tab("key_row", (E,), U16), tab("place_row", (E,), U16)

    with ExitStack() as c2:
        S = Scope(nc, c2, "ord")
        target, prev = S.sb("target", [ORD_P, ORD_C], I32), S.sb("prev", [ORD_P, ORD_C], I32)
        falls = S.sb("falls", [ORD_P, ORD_C])
        fall = S.sb("fall", [ORD_P, 1])
        one = S.sb("one", [ORD_P, 1])
        flag = S.sb("flag", [1, 1], I32)
        pf = S.ps("pf", [1, 1])
        filled, loaded, fell, flagged = (S.sem(n) for n in ("filled", "loaded", "fell", "flagged"))

        with nc.Block() as block:
            @block.sync
            def _(sp):
                sp.dma_start(target[:, :], a["dst"].rearrange("(p c) -> p c", c=ORD_C)).then_inc(loaded, 16)
                sp.wait_ge(filled, 1)
                sp.dma_start(prev[1:ORD_P, :], a["dst"][ORD_C - 1:E - 1].rearrange("(p c) -> p c", c=ORD_C))\
                    .then_inc(loaded, 16)
                sp.dma_start(prev[0:1, 1:ORD_C], a["dst"][0:ORD_C - 1].unsqueeze(0)).then_inc(loaded, 16)
                sp.dma_start(o_dst, a["dst"].unsqueeze(1)).then_inc(loaded, 16)
                sp.dma_start(o_src, a["src"].unsqueeze(1)).then_inc(loaded, 16)
                sp.dma_start(o_attr, a["edge_attr_10"]).then_inc(loaded, 16)
                sp.wait_ge(loaded, 16 * 6)

            @block.vector
            def _(v):
                v.memset(prev[0:1, 0:1], 0).then_inc(filled, 1)
                v.memset(one[:, :], 1.0).then_inc(filled, 1)
                v.wait_ge(loaded, 16 * 6)
                v.tensor_tensor(falls[:, :], prev[:, :], target[:, :], ALU.is_gt).then_inc(fell, 1)
                v.wait_ge(fell, 1)
                v.tensor_reduce(out=fall[:, :], in_=falls[:, :], axis=AX_X, op=ALU.max).then_inc(fell, 1)
                v.wait_ge(flagged, 1)
                v.tensor_copy(flag[:, :], pf[:, :])

            @block.tensor
            def _(pe):
                pe.wait_ge(filled, 2)
                pe.wait_ge(fell, 2)
                pe.matmul(pf[:, :], fall[:, :], one[:, :], start=True, stop=True).then_inc(flagged, 1)

        source = S.sb("source", [ORD_P, ORD_C], I32)
        attr = S.sb("attr", [ORD_P, ORD_C, ED])
        place, key = S.sb("place", [ORD_P, ORD_C]), S.sb("key", [ORD_P, ORD_C])
        place16, key16 = S.sb("place16", [ORD_P, ORD_C], U16), S.sb("key16", [ORD_P, ORD_C], U16)
        part = S.sb("part", [ORD_P, 2, ORD_C])
        rank = S.sb("rank", [ORD_P, ORD_C], I32)
        keys, places = S.sb("keys", [ORD_P, E // 2], U16), S.sb("places", [ORD_P, E // 2], U16)
        early, tie = S.sb("early", [ORD_P, E // 2], U8), S.sb("tie", [ORD_P, E // 2], U8)
        stage_i = S.sb("stage_i", [ORD_P, 3], I32)
        stage_a = S.sb("stage_a", [ORD_P, ED])
        (placed, narrow, written, half_in, earlier, tied, ranked, halves, placed_all, rows_in, staged, moved,
         sent) = (S.sem(n) for n in ("placed", "narrow", "written", "half_in", "earlier", "tied", "ranked", "halves",
                                     "placed_all", "rows_in", "staged", "moved", "sent"))
        with nc.Block() as block:
            @block.gpsimd
            def _(pool):
                unordered = pool.value_load(flag[0:1, 0:1], min_val=0, max_val=P)
                with pool.If(unordered > 0):
                    pool.iota(place[:, :], [[1, ORD_C]], base=0, channel_multiplier=ORD_C,
                              allow_small_or_imprecise_dtypes=True).then_inc(placed, 1)
                    pool.dma_start(source[:, :], a["src"].rearrange("(p c) -> p c", c=ORD_C)).then_inc(rows_in, 16)
                    pool.dma_start(attr[:, :, :], a["edge_attr_10"].rearrange("(p c) d -> p c d", c=ORD_C))\
                        .then_inc(rows_in, 16)
                    pool.wait_ge(narrow, 2)
                    pool.dma_start(key_row.rearrange("(p c) -> p c", c=ORD_C), key16[:, :]).then_inc(written, 16)
                    pool.dma_start(place_row.rearrange("(p c) -> p c", c=ORD_C), place16[:, :]).then_inc(written, 16)
                    pool.wait_ge(written, 32)
                    for h in range(2):
                        if h:
                            pool.wait_ge(halves, 1)
                        span = slice(h * E // 2, (h + 1) * E // 2)
                        for dst, src in ((keys, key_row), (places, place_row)):
                            pool.dma_start(dst[:, :], src[span].unsqueeze(0).to_broadcast([ORD_P, E // 2]))\
                                .then_inc(half_in, 16)
                    pool.wait_ge(placed_all, 1)
                    pool.wait_ge(rows_in, 32)

                    def scatter(t):
                        col = slice(t, t + 1) if isinstance(t, int) else bass.ds(t, 1)
                        if not isinstance(t, int):
                            pool.wait_ge(moved, t * (3 * 16))
                            pool.sem_inc(sent, 1)
                        for i, values in enumerate((rank, target, source)):
                            pool.tensor_copy(stage_i[:, i:i + 1], values[:, col])
                        pool.tensor_copy(stage_a[:, :], attr[:, col, :].rearrange("p o d -> p (o d)")).then_inc(staged, 1)
                        pool.wait_ge(staged, t + 1)
                        pool.sem_inc(sent, 1)
                        for dst, src in ((o_dst, stage_i[:, 1:2]), (o_src, stage_i[:, 2:3]), (o_attr, stage_a[:, :])):
                            pool.indirect_dma_start(out=dst[:, :], in_=src, in_offset=None,
                                                    out_offset=bass.IndirectOffsetOnAxis(ap=stage_i[:, 0:1], axis=0))\
                                .then_inc(moved, 16)

                    scatter(0)
                    with pool.Fori(1, ORD_C) as t:
                        scatter(t)
                    pool.wait_ge(moved, ORD_C * 3 * 16)

            @block.vector
            def _(v):
                unordered = v.value_load(flag[0:1, 0:1], min_val=0, max_val=P)
                with v.If(unordered > 0):
                    v.tensor_copy(key[:, :], target[:, :])
                    v.tensor_copy(key16[:, :], target[:, :]).then_inc(narrow, 1)
                    v.wait_ge(placed, 1)
                    v.tensor_copy(place16[:, :], place[:, :]).then_inc(narrow, 1)
                    v.memset(rank[:, :], 0).then_inc(ranked, 1)
                    for h in range(2):
                        v.wait_ge(half_in, 32 * (h + 1))
                        with v.Fori(0, ORD_C) as t:
                            done = t + (h * ORD_C + 1)
                            v.wait_ge(ranked, done)
                            v.tensor_scalar(early[:, :], places[:, :], place[:, bass.ds(t, 1)], None, ALU.is_lt)\
                                .then_inc(earlier, 1)
                            v.wait_ge(earlier, done)
                            v.scalar_tensor_tensor(out=tie[:, :], in0=keys[:, :], scalar=key[:, bass.ds(t, 1)],
                                                   in1=early[:, :], op0=ALU.is_equal, op1=ALU.mult).then_inc(tied, 1)
                            v.wait_ge(tied, done)
                            v.scalar_tensor_tensor(out=early[:, :], in0=keys[:, :], scalar=key[:, bass.ds(t, 1)],
                                                   in1=tie[:, :], op0=ALU.is_lt, op1=ALU.add,
                                                   accum_out=part[:, h, bass.ds(t, 1)]).then_inc(ranked, 1)
                        v.wait_ge(ranked, (h + 1) * ORD_C + 1)
                        v.sem_inc(halves, 1)
                    v.tensor_tensor(rank[:, :], part[:, 0, :], part[:, 1, :], ALU.add).then_inc(placed_all, 1)

    return {**a, "dst": o_dst.rearrange("e o -> (e o)"), "src": o_src.rearrange("e o -> (e o)"), "edge_attr_10": o_attr}



def build(nc, a, out):
    a = order_edges(nc, a)
    ctx = ExitStack()
    with ctx:
        R = Scope(nc, ctx, "r")
        dram = lambda name, shape, dt=F32: nc.dram_tensor(name, shape, dt).ap()
        h0_tab = dram("h0_tab", (NPAD, D))
        b0_tab = dram("b0_tab", (NPAD, D))
        e0_tab = dram("e0_tab", (NPAD + 1, 4 * D))
        x1_tab = dram("x1_tab", (NPAD, D))
        h1_tab = dram("h1_tab", (NPAD, D))
        m1_tab = dram("m1_tab", (NPAD, W_MSG))
        dn_tab = dram("dn_tab", (2 * NPAD, 4))
        d1_tab = dram("d1_tab", (NPAD, 4))
        e1_tab = dram("e1_tab", (NPAD + 1, W_ATT))
        x2_tab = dram("x2_tab", (NPAD, D))
        t2_tab = dram("t2_tab", (NPAD, D))
        e2_tab = dram("e2_tab", (NPAD + 1, D))
        z0_tab = dram("z0_tab", (NPAD, D))
        y_tab = dram("y_tab", (NPAD, D))
        r1_tab = dram("r1_tab", (NPAD + 1, D))
        r2_tab = dram("r2_tab", (NPAD + 1, D))
        a2_tab = dram("a2_tab", (NPAD, D))
        a3_tab = dram("a3_tab", (NPAD + 1, D))
        hop_tab = dram("hop_tab", (NPAD, 2))
        keep_row = dram("keep_row", (TILES, P), U8)

        ident = R.sb("ident", [P, P])
        ones = R.sb("ones", [P, P])
        eps = R.sb("eps", [P, 1])
        keep = R.sb("keep", [P, NPAD], U8)
        src_i = R.sb("src_i", [P, TILES], I32)
        last_i = R.sb("last_i", [P, TILES], I32)
        first_i = R.sb("first_i", [P, TILES], I32)
        hop_i = R.sb("hop_i", [P, TILES], I32)
        hop_w = R.sb("hop_w", [P, TILES])
        nsc = R.sb("nsc", [P, GROUPS, NSC, TPG])
        w_a, w_b = R.sb("w_a", [P, D]), R.sb("w_b", [P, D])
        w_edge = R.sb("w_edge", [TPG * ED, TPG, D])
        w_agg = R.sb("w_agg", [P, 4, 3, D])
        w_self = R.sb("w_self", [P, D])
        w_m1, w_m2, w_m3 = (R.sb(f"w_m{i}", [P, D]) for i in (1, 2, 3))
        w_att = R.sb("w_att", [P, 6])
        w_c1a, w_c1b, w_c2 = (R.sb(n, [P, D]) for n in ("w_c1a", "w_c1b", "w_c2"))
        w_gcn = R.sb("w_gcn", [P, D])
        c_pre, c_post, c_m3, c_c2, c_gcn = (R.sb(n, [P, D]) for n in ("c_pre", "c_post", "c_m3", "c_c2", "c_gcn"))
        c_m1, c_m2, c_c1 = (R.sb(n, [P, 1]) for n in ("c_m1", "c_m2", "c_c1"))
        c_att = R.sb("c_att", [P, 4])

        class Norm:

            def __init__(self, S, src, dst):
                self.src, self.dst = src, dst
                self.stats = S.sb("ln_stats", [P, 2, TPG, 6])
                self.mv = S.sb("ln_mv", [P, 2, TPG, 2])
                self.std = S.sb("ln_std", [P, 2, TPG])
                self.scale = S.sb("ln_scale", [P, 2, TPG])
                self.shift = S.sb("ln_shift", [P, 2, TPG])
                self.sums, self.moments, self.root, self.inverse, self.scaled, self.done, self.held = (
                    S.sem(n) for n in ("ln_sums", "ln_moments", "ln_root", "ln_inverse", "ln_scaled", "ln_done",
                                        "ln_held"))

            def moments_of(self, v, g, u):
                for k in range(TPG):
                    ins = v.bn_stats(self.stats[:, u, k, :], self.src(u)[:, k, :])
                ins.then_inc(self.sums, 1)
                ready(v, self.sums, g)
                freed(v, self.scaled, g)
                v.sem_inc(self.held, 1)
                for k in range(TPG):
                    ins = v.bn_aggr(self.mv[:, u, k, :], self.stats[:, u, k, :])
                ins.then_inc(self.moments, 1)

            def root_of(self, act, g, u):
                ready(act, self.moments, g)
                freed(act, self.inverse, g)
                act.activation(self.std[:, u, :], self.mv[:, u, :, 1], ACT.Sqrt, bias=eps[:, :]).then_inc(self.root, 1)

            def scale_of(self, v, g, u):
                ready(v, self.root, g)
                freed(v, self.done, g)
                v.reciprocal(self.scale[:, u, :], self.std[:, u, :]).then_inc(self.inverse, 1)
                ready(v, self.inverse, g)
                v.scalar_tensor_tensor(out=self.shift[:, u, :], in0=self.mv[:, u, :, 0], scalar=-1.0,
                                       in1=self.scale[:, u, :], op0=ALU.mult, op1=ALU.mult).then_inc(self.scaled, 1)

            def relu_of(self, act, g, u):
                ready(act, self.scaled, g)
                for k in range(TPG):
                    ins = act.activation(self.dst(u)[:, k, :], self.src(u)[:, k, :], ACT.Relu,
                                         scale=self.scale[:, u, k:k + 1], bias=self.shift[:, u, k:k + 1])
                ins.then_inc(self.done, 1)

        def flat(ap):
            return ap.rearrange("p k d -> p (k d)")

        def turn(pe, dst, src, done):
            for k in range(TPG):
                ins = pe.transpose(dst[:, k * P:(k + 1) * P], src[:, k, :], ident[:, :])
            ins.then_inc(done, 1)

        def end_of(eng, sems, uses=GROUPS // 2):
            for s in sems:
                eng.wait_ge(s, 16 * uses)

        def node_gather(pool, table, dst, index, stage, staged, got, sent, u, g):
            cols = index[:, g * TPG:(g + 1) * TPG] if isinstance(g, int) else index[:, bass.ds(g * TPG, TPG)]
            pool.tensor_copy(stage[:, u, :], cols).then_inc(staged, 1)
            ready(pool, staged, g)
            pool.sem_inc(sent, 1)
            for k in range(TPG):
                pool.indirect_dma_start(out=dst[:, k, :], out_offset=None, in_=table[:, :],
                                        in_offset=bass.IndirectOffsetOnAxis(ap=stage[:, u, k:k + 1], axis=0))\
                    .then_inc(got[u], 16)

        with ExitStack() as c2:
            S = Scope(nc, c2, "s")
            iota_p = S.sb("iota_p", [P, P])
            iota_q = S.sb("iota_q", [P, TILES])
            before = S.sb("before", [P, P])
            target = S.sb("target", [GROUPS, TPG, P], I32)
            prev = S.sb("prev", [GROUPS, TPG, P], I32)
            source = S.sb("source", [GROUPS, TPG, P], I32)
            bits = [S.sb(f"bits{i}", [GROUPS, TPG, P], I32) for i in range(4)]
            lists = [S.sb(f"lists{i}", [GROUPS, TPG, P]) for i in range(3)]
            keep8 = S.sb("keep8", [GROUPS, TPG, P], U8)
            p_col, q_col = S.sb("p_col", [P, TILES]), S.sb("q_col", [P, TILES])
            w_ee, w_c, w_lin = S.sb("w_ee", [ED + 1, D]), S.sb("w_c", [P, D]), S.sb("w_lin", [P, D])
            w_ee_t = S.sb("w_ee_t", [P, ED + 1])
            w_post, w_post_t = S.sb("w_post", [P, 13, D]), S.sb("w_post_t", [P, 13, D])
            w_g = S.sb("w_g", [P, D])
            b_col = S.sb("b_col", [P, 2])
            b_rep = S.sb("b_rep", [P, 2, P])
            w_edge1 = S.sb("w_edge1", [ED, D])
            zero = S.sb("zero", [P, NPAD * 4 // P])
            own_row = S.sb("own_row", [P, GROUPS, TPG])
            first = S.sb("first", [P, GROUPS, TPG])
            cnt = S.sb("cnt", [P, GROUPS, TPG])
            tmp = [S.sb(f"tmp{i}", [P, GROUPS, TPG]) for i in range(4)]
            hop = S.sb("hop", [P, GROUPS, TPG, 2])
            col = [S.sb(f"col{i}", [P, GROUPS]) for i in range(3)]
            avg = S.sb("avg", [P, 4])
            hot_p = S.sb("hot_p", [P, 2, TPG, P], BF16)
            hot_q = S.sb("hot_q", [P, 2, TPG, TILES], BF16)
            ps = [S.ps(f"ps{i}", [P, 512]) for i in range(6)]
            filled, loaded, built, chain, gchain = (S.sem(n) for n in ("filled", "loaded", "built", "chain", "gchain"))

            loads = [
                (w_a[:, :], a["L0_gnn_W_pre"][0:D, :]), (w_b[:, :], a["L0_gnn_W_pre"][D:2 * D, :]),
                (w_c[:, :], a["L0_gnn_W_pre"][2 * D:3 * D, :]),
                (w_ee[0:ED, :], a["L0_gnn_W_ee"][:, :]), (w_ee[ED:ED + 1, :], a["L0_gnn_b_ee"].unsqueeze(0)),
                (w_lin[:, :], a["L0_gnn_W_lin"][:, :]),
                (w_post[:, :, :], a["L0_gnn_W_post"].rearrange("(b p) n -> p b n", p=P)),
                (w_m1[:, :], a["L1_gnn_W_msg_1"][:, :]), (w_m2[:, :], a["L1_gnn_W_msg_2"][:, :]),
                (w_m3[:, :], a["L1_gnn_W_msg_3"][:, :]),
                (w_c1a[:, :], a["L1_gnn_W_c1"][0:D, :]), (w_c1b[:, :], a["L1_gnn_W_c1"][D:2 * D, :]),
                (w_c2[:, :], a["L1_gnn_W_c2"][:, :]), (w_g[:, :], a["L2_gnn_W"][:, :]),
                (c_m3[:, :], a["L1_gnn_b_msg_3"].unsqueeze(0).to_broadcast([P, D])),
                (c_c2[:, :], a["L1_gnn_b_c2"].unsqueeze(0).to_broadcast([P, D])),
                (c_gcn[:, :], a["L2_gnn_b"].unsqueeze(0).to_broadcast([P, D])),
                (c_pre[:, :], a["L0_gnn_b_pre"].unsqueeze(0).to_broadcast([P, D])),
                (c_post[:, :], a["L0_gnn_b_lin"].unsqueeze(0).to_broadcast([P, D])),
                (c_m1[:, :], a["L1_gnn_b_msg_1"].unsqueeze(1)), (c_m2[:, :], a["L1_gnn_b_msg_2"].unsqueeze(1)),
                (c_c1[:, :], a["L1_gnn_b_c1"].unsqueeze(1)),
                (b_col[:, 0:1], a["L0_gnn_b_ee"].unsqueeze(1)), (b_col[:, 1:2], a["L0_gnn_b_post"].unsqueeze(1)),
            ]
            for k in range(3):
                w = a[f"L1_gnn_W_att_{k + 1}"]
                loads += [(w_att[:, k:k + 1], w[0:D, :]), (w_att[:, 3 + k:4 + k], w[D:2 * D, :]),
                          (c_att[:, k:k + 1], a[f"L1_gnn_b_att_{k + 1}"].unsqueeze(0).to_broadcast([P, 1]))]
            full = E // P
            rest = E - full * P
            pads = []
            for b in range(TPG):
                n = min(GROUPS, full - b * GROUPS)
                o = b * GROUPS * P
                for tile, name in ((target, "dst"), (source, "src")):
                    pads.append((tile[0:n, b, :], a[name][o:o + n * P].rearrange("(t c) -> t c", c=P)))
                    if n < GROUPS:
                        pads.append((tile[n:n + 1, b, 0:rest], a[name][full * P:E].unsqueeze(0)))
                if b == 0:
                    pads.append((prev[0:1, b, 1:P], a["dst"][0:P - 1].unsqueeze(0)))
                    pads.append((prev[1:n, b, :], a["dst"][P - 1:n * P - 1].rearrange("(t c) -> t c", c=P)))
                else:
                    pads.append((prev[0:n, b, :], a["dst"][o - 1:o + n * P - 1].rearrange("(t c) -> t c", c=P)))
                if n < GROUPS:
                    pads.append((prev[n:n + 1, b, 0:rest], a["dst"][full * P - 1:E - 1].unsqueeze(0)))

            with nc.Block() as block:
                @block.sync
                def _(sp):
                    for dst, src in loads:
                        sp.dma_start(dst, src).then_inc(loaded, 16)
                    sp.wait_ge(filled, 3)
                    for dst, src in pads:
                        sp.dma_start(dst, src).then_inc(loaded, 16)
                    sp.wait_ge(loaded, 16 * (len(loads) + len(pads)))

                @block.vector
                def _(v):
                    v.memset(target[:, :, :], NO_NODE).then_inc(filled, 1)
                    v.memset(prev[:, :, :], -1).then_inc(filled, 1)
                    v.memset(source[:, :, :], 0).then_inc(filled, 1)
                    v.memset(ones[:, :], 1.0)
                    v.memset(eps[:, :], EPS)
                    v.memset(zero[:, :], 0.0)
                    v.memset(c_att[:, 3:4], 0.0)
                    v.memset(w_edge[:, :, :], 0.0)

                @block.gpsimd
                def _(g):
                    link = Chain(g, gchain)
                    g.iota(iota_p[:, :], [[1, P]], base=0, channel_multiplier=0,
                           allow_small_or_imprecise_dtypes=True)
                    g.iota(iota_q[:, :], [[1, TILES]], base=0, channel_multiplier=0,
                           allow_small_or_imprecise_dtypes=True)
                    g.iota(own_row[:, :, :], [[ROWS, GROUPS], [1, TPG]], base=NPAD, channel_multiplier=TPG,
                           allow_small_or_imprecise_dtypes=True)
                    link(g.memset(ident[:, :], 0.0))
                    g.affine_select(out=ident[:, :], in_=ident[:, :], compare_op=ALU.not_equal, fill=1.0, base=0,
                                    pattern=[[-1, P]], channel_multiplier=1)
                    link(g.memset(before[:, :], 1.0))
                    g.affine_select(out=before[:, :], in_=before[:, :], compare_op=ALU.is_gt, fill=0.0, base=0,
                                    pattern=[[1, P]], channel_multiplier=-1)

            turned, taken, mul, kept = (S.sem(n) for n in ("turned", "taken", "mul", "kept"))
            with nc.Block() as block:
                @block.vector
                def _(v):
                    link = Chain(v, chain)
                    v.tensor_scalar(bits[0][:, :, :], target[:, :, :], 2, 127, ALU.logical_shift_right, ALU.bitwise_and)
                    v.tensor_scalar(bits[1][:, :, :], target[:, :, :], 9, 2, ALU.logical_shift_right,
                                    ALU.logical_shift_left)
                    link(v.tensor_scalar(bits[2][:, :, :], target[:, :, :], 3, None, ALU.bitwise_and))
                    v.tensor_copy(lists[0][:, :, :], bits[0][:, :, :])
                    v.tensor_tensor(lists[1][:, :, :], bits[1][:, :, :], bits[2][:, :, :], ALU.add)
                    v.tensor_copy(lists[2][:, :, :], source[:, :, :]).then_inc(built, 1)
                    v.tensor_tensor(keep8[:, :, :], target[:, :, :], prev[:, :, :], ALU.is_equal).then_inc(built, 1)
                    v.tensor_copy(b_rep[:, :, :], bc(b_col[:, :], P)).then_inc(built, 1)
                    v.wait_ge(turned, 1)
                    for i, dst in enumerate((p_col, q_col, src_i)):
                        v.tensor_copy(dst[:, :], ps[i][:, 0:TILES])
                    v.tensor_copy(w_gcn[:, :], ps[4][:, 0:D])
                    v.tensor_copy(w_ee_t[:, :], ps[5][:, 0:ED + 1]).then_inc(taken, 1)
                    v.wait_ge(turned, 2)
                    for i in range(4):
                        n = min(4, 13 - 4 * i)
                        ins = v.tensor_copy(w_post_t[:, 4 * i:4 * i + n, :].rearrange("p b n -> p (b n)"),
                                            ps[i][:, 0:n * D])
                    ins.then_inc(taken, 1)
                    v.wait_ge(mul, 1)
                    v.tensor_copy(w_self[:, :], ps[0][:, 0:D])
                    for i in range(3):
                        v.tensor_copy(w_agg[:, :, i, :], ps[1 + i][:, :].rearrange("p (c n) -> p c n", c=4))
                    v.tensor_copy(w_edge1[:, :], ps[4][0:ED, 0:D]).then_inc(taken, 1)
                    v.tensor_tensor(c_pre[:, :], c_pre[:, :], ps[5][:, 0:D], ALU.add)
                    v.tensor_tensor(c_post[:, :], c_post[:, :], ps[5][:, D:2 * D], ALU.add)

                @block.tensor
                def _(pe):
                    pe.wait_ge(built, 3)
                    for i in range(3):
                        for b in range(TPG):
                            pe.transpose(ps[i][:, b * GROUPS:(b + 1) * GROUPS], lists[i][:, b, :],
                                         ident[0:GROUPS, 0:GROUPS])
                    pe.transpose(ps[4][:, 0:D], w_g[:, :], ident[:, :])
                    pe.transpose(ps[5][:, 0:ED + 1], w_ee[:, :], ident[0:ED + 1, 0:ED + 1]).then_inc(turned, 1)
                    pe.wait_ge(taken, 1)
                    for b in range(13):
                        ins = pe.transpose(ps[b // 4][:, b % 4 * D:(b % 4 + 1) * D], w_post[:, b, :], ident[:, :])
                    ins.then_inc(turned, 1)
                    pe.wait_ge(taken, 2)
                    pe.matmul(ps[0][:, 0:D], w_post_t[:, 0, :], w_lin[:, :], start=True, stop=True)
                    for i in range(3):
                        for c, q in enumerate((0, 2, 1, 3)):
                            pe.matmul(ps[1 + i][:, c * D:(c + 1) * D], w_post_t[:, 1 + 4 * i + q, :], w_lin[:, :],
                                      start=True, stop=True)
                    pe.matmul(ps[4][0:ED, 0:D], w_ee_t[:, 0:ED], w_c[:, :], start=True, stop=True)
                    pe.matmul(ps[5][:, 0:D], b_rep[:, 0, :], w_c[:, :], start=True, stop=True)
                    pe.matmul(ps[5][:, D:2 * D], b_rep[:, 1, :], w_lin[:, :], start=True, stop=True).then_inc(mul, 1)

                @block.sync
                def _(sp):
                    sp.wait_ge(built, 2)
                    sp.dma_start(keep_row[:, :].rearrange("(b t) c -> t b c", t=GROUPS), keep8[:, :, :]).then_inc(kept, 16)
                    for tab, w in ((e0_tab, 4 * D), (e1_tab, W_ATT), (e2_tab, D), (r1_tab, D), (r2_tab, D), (a3_tab, D)):
                        sp.dma_start(tab[ZERO_ROW:ZERO_ROW + 1, :].rearrange("o (p c) -> (o p) c", c=4),
                                     zero[0:w // 4, 0:4]).then_inc(kept, 16)
                    sp.dma_start(dn_tab[0:NPAD, :].rearrange("(p c) w -> p (c w)", p=P), zero[:, :]).then_inc(kept, 16)
                    sp.wait_ge(kept, 8 * 16)
                    sp.dma_start(keep[:, :], keep_row.rearrange("t c -> (t c)").unsqueeze(0).to_broadcast([P, NPAD]))\
                        .then_inc(kept, 16)
                    sp.wait_ge(taken, 3)
                    for k in range(TPG):
                        sp.dma_start(w_edge[k * ED:(k + 1) * ED, k, :], w_edge1[:, :]).then_inc(kept, 16)
                    sp.wait_ge(kept, 13 * 16)

            with ExitStack() as c3:
                N0 = Scope(nc, c3, "n0")
                x = N0.sb("x", [P, 2, TPG, D])
                h = N0.sb("h", [P, 2, TPG, D])
                ht = N0.sb("ht", [P, 2, ROWS])
                b = N0.sb("b", [P, 2, TPG, D])
                count, pt, pb = ps[0], ps[1:3], ps[3:5]
                x_in, h_out, b_out = N0.pair("x_in"), N0.pair("h_out"), N0.pair("b_out")
                turned, ht_there, prod, b_there, hot, used = (N0.sem(n) for n in (
                    "turned", "ht_there", "prod", "b_there", "hot", "used"))
                ln = Norm(N0, lambda u: x[:, u], lambda u: h[:, u])

                with nc.Block() as block:
                    @block.sync
                    def _(sp):
                        def load(g, u, r):
                            freed(sp, ln.done, g)
                            if is_last(g):
                                sp.dma_start(x[0:LAST_P, u, :, :], tail_rows(a["x"])).then_inc(x_in[u], 16)
                            else:
                                t = a["x"][0:(GROUPS - 1) * ROWS, :].rearrange("(g p k) d -> g p k d", p=P, k=TPG)
                                t = t[g] if isinstance(g, int) else t[bass.ds(g, 1)].rearrange("o p k d -> (o p) k d")
                                sp.dma_start(x[:, u, :, :], t).then_inc(x_in[u], 16)

                        pipeline(sp, load)
                        end_of(sp, h_out)
                        end_of(sp, b_out)

                    @block.vector
                    def _(v):
                        def moments(g, u, r):
                            landed(v, x_in, u, r)
                            ln.moments_of(v, g, u)

                        def scales(g, u, r):
                            ln.scale_of(v, g, u)

                        def take_turned(g, u, r):
                            ready(v, turned, g)
                            freed(v, prod, g)
                            v.tensor_copy(ht[:, u, :], pt[u][:, :]).then_inc(ht_there, 1)

                        def one_hots(g, u, r):
                            freed(v, used, g)
                            for k in range(TPG):
                                t = slice(g * TPG + k, g * TPG + k + 1) if isinstance(g, int) else bass.ds(g * TPG + k, 1)
                                v.tensor_scalar(hot_p[:, u, k, :], iota_p[:, :], p_col[:, t], None, ALU.is_equal)
                                ins = v.tensor_scalar(hot_q[:, u, k, :], iota_q[:, :], q_col[:, t], None, ALU.is_equal)
                            ins.then_inc(hot, 1)

                        pipeline(v, (1, scales), (2, take_turned), (0, moments), (0, one_hots))

                    @block.scalar
                    def _(act):
                        def root(g, u, r):
                            ln.root_of(act, g, u)

                        def relu(g, u, r):
                            drained(act, h_out, u, r)
                            freed(act, turned, g)
                            ln.relu_of(act, g, u)

                        def take_b(g, u, r):
                            ready(act, prod, g)
                            drained(act, b_out, u, r)
                            act.copy(flat(b[:, u]), pb[u][:, :]).then_inc(b_there, 1)

                        def store_h(g, u, r):
                            ready(act, ln.done, g)
                            act.dma_start(rows_of(h0_tab, g), h[:, u, :, :]).then_inc(h_out[u], 16)

                        def store_b(g, u, r):
                            ready(act, b_there, g)
                            act.dma_start(rows_of(b0_tab, g), b[:, u, :, :]).then_inc(b_out[u], 16)

                        pipeline(act, (1, relu), (1, store_h), (3, take_b), (3, store_b), (0, root))

                    @block.tensor
                    def _(pe):
                        def turn_h(g, u, r):
                            ready(pe, ln.done, g)
                            freed(pe, ht_there, g)
                            turn(pe, pt[u], h[:, u], turned)

                        def times_w(g, u, r):
                            ready(pe, ht_there, g)
                            freed(pe, b_there, g)
                            for k in range(TPG):
                                ins = pe.matmul(pb[u][:, k * D:(k + 1) * D], ht[:, u, k * P:(k + 1) * P], w_b[:, :],
                                                start=True, stop=True)
                            ins.then_inc(prod, 1)

                        def add_counts(g, u, r):
                            ready(pe, hot, g)
                            for k in range(TPG):
                                ins = pe.matmul(count[:, 0:TILES], hot_p[:, u, k, :], hot_q[:, u, k, :],
                                                start=isinstance(g, int) and g == 0 and k == 0,
                                                stop=is_last(g) and k == TPG - 1, skip_group_check=True)
                            ins.then_inc(used, 1)

                        pipeline(pe, (0, add_counts), (0, turn_h), (1, times_w))

            counted, scanned, logs = (S.sem(n) for n in ("counted", "scanned", "logs"))
            with nc.Block() as block:
                @block.vector
                def _(v):
                    link = Chain(v, counted)
                    link(v.tensor_copy(cnt[:, :, :].rearrange("p g k -> p (g k)"), ps[0][:, 0:TILES]))
                    link(v.tensor_reduce(col[0][:, :], cnt[:, :, :], AX_X, ALU.add))
                    v.wait_ge(scanned, 1)
                    v.tensor_copy(col[2][:, :], ps[1][:, 0:GROUPS])
                    link(v.tensor_tensor_scan(col[1][:, :], ones[:, 0:GROUPS], ps[2][:, 0:GROUPS], 0.0, ALU.mult, ALU.add))
                    link(v.tensor_tensor(col[1][:, :], col[1][:, :], ps[2][:, 0:GROUPS], ALU.subtract))
                    link(v.tensor_tensor(tmp[0][:, :, 0], cnt[:, :, 0], col[1][:, :], ALU.add))
                    link(v.tensor_tensor(tmp[0][:, :, 0], tmp[0][:, :, 0], col[2][:, :], ALU.add))
                    for k in range(1, TPG):
                        link(v.tensor_tensor(tmp[0][:, :, k], tmp[0][:, :, k - 1], cnt[:, :, k], ALU.add))
                    link(v.tensor_scalar(nsc[:, :, S_HAS, :], cnt[:, :, :], 0.0, None, ALU.is_gt))
                    link(v.tensor_tensor(first[:, :, :], tmp[0][:, :, :], cnt[:, :, :], ALU.subtract))
                    link(v.tensor_tensor(first[:, :, :], first[:, :, :], own_row[:, :, :], ALU.subtract))
                    link(v.tensor_tensor(first[:, :, :], first[:, :, :], nsc[:, :, S_HAS, :], ALU.mult))
                    v.tensor_tensor(first_i[:, :].rearrange("p (g k) -> p g k", k=TPG), first[:, :, :], own_row[:, :, :],
                                    ALU.add)
                    link(v.scalar_tensor_tensor(out=tmp[1][:, :, :], in0=tmp[0][:, :, :], scalar=-1.0 - ZERO_ROW,
                                                in1=nsc[:, :, S_HAS, :], op0=ALU.add, op1=ALU.mult))
                    link(v.tensor_scalar(hop[:, :, :, 0], tmp[1][:, :, :], float(ZERO_ROW), None, ALU.add))
                    v.tensor_copy(last_i[:, :].rearrange("p (g k) -> p g k", k=TPG), hop[:, :, :, 0])
                    link(v.tensor_scalar(tmp[1][:, :, :], cnt[:, :, :], 1.0, None, ALU.max))
                    link(v.reciprocal(nsc[:, :, S_INV, :], tmp[1][:, :, :]))
                    v.tensor_scalar(nsc[:, :, S_THIRD, :], nsc[:, :, S_INV, :], 1.0 / 3.0, None, ALU.mult)
                    v.tensor_tensor(hop[:, :, :, 1], nsc[:, :, S_INV, :], nsc[:, :, S_HAS, :], ALU.mult)
                    link(v.tensor_scalar(tmp[2][:, :, :], cnt[:, :, :], 1.0, None, ALU.add))
                    v.wait_ge(logs, 4)
                    v.reciprocal(nsc[:, :, S_GCN, :], nsc[:, :, S_GCN, :])
                    link(v.reciprocal(tmp[0][:, :, :], nsc[:, :, S_DINV, :]))
                    link(v.tensor_tensor(nsc[:, :, S_DINV, :], tmp[0][:, :, :], nsc[:, :, S_HAS, :], ALU.mult))
                    v.wait_ge(scanned, 2)
                    link(v.tensor_scalar(avg[:, 1:2], ps[3][:, 0:1], 1.0 / N, None, ALU.mult))
                    link(v.reciprocal(avg[:, 2:3], avg[:, 1:2]))
                    link(v.reciprocal(tmp[0][:, :, :], tmp[3][:, :, :]))
                    v.tensor_scalar(nsc[:, :, S_LOG, :], tmp[3][:, :, :], avg[:, 2:3], None, ALU.mult)
                    v.tensor_scalar(nsc[:, :, S_ALOG, :], tmp[0][:, :, :], avg[:, 1:2], None, ALU.mult)

                @block.scalar
                def _(act):
                    act.wait_ge(counted, 18)
                    act.activation(nsc[:, :, S_GCN, :], tmp[2][:, :, :], ACT.Sqrt).then_inc(logs, 1)
                    act.activation(nsc[:, :, S_DINV, :], tmp[1][:, :, :], ACT.Sqrt).then_inc(logs, 1)
                    act.activation(tmp[3][:, :, :], tmp[1][:, :, :], ACT.Ln, bias=1.0).then_inc(logs, 1)
                    act.activation(tmp[0][:, :, :], cnt[:, :, :], ACT.Ln, bias=1.0, accum_out=avg[:, 0:1])\
                        .then_inc(logs, 1)

                @block.tensor
                def _(pe):
                    pe.wait_ge(counted, 2)
                    pe.matmul(ps[1][:, 0:GROUPS], before[:, :], col[0][:, :], start=True, stop=True)
                    pe.matmul(ps[2][:, 0:GROUPS], ones[:, :], col[0][:, :], start=True, stop=True).then_inc(scanned, 1)
                    pe.wait_ge(logs, 4)
                    pe.matmul(ps[3][:, 0:1], ones[:, :], avg[:, 0:1], start=True, stop=True).then_inc(scanned, 1)

            hopped = S.sem("hopped")
            with nc.Block() as block:
                @block.sync
                def _(sp):
                    for h in range(2):
                        g0, g1 = h * GROUPS // 2, (h + 1) * GROUPS // 2
                        sp.dma_start(hop_tab.rearrange("(g p k) w -> p g (k w)", p=P, k=TPG)[:, g0:g1, :],
                                     hop[:, g0:g1, :, :].rearrange("p g k w -> p g (k w)")).then_inc(hopped, 16)
                    sp.wait_ge(hopped, 32)

        with ExitStack() as c2:
            S = Scope(nc, c2, "e0")
            rows = S.sb("rows", [P, 2, TPG, D])
            stage = S.sb("stage", [P, 2, TPG], I32)
            ea = S.sb("ea", [P, 2, TPG, ED])
            ea_t = S.sb("ea_t", [TPG * ED, 2, P])
            sq = S.sb("sq", [P, 2, ROWS])
            low, high = S.sb("low", [P, 2, ROWS]), S.sb("high", [P, 2, ROWS])
            run = [S.sb(f"run{q}", [P, 2, ROWS]) for q in range(4)]
            res = S.sb("res", [P, 2, TPG, 4, D])
            pt = [S.ps(f"pt{u}", [P, ROWS]) for u in range(2)]
            pe_t = S.ps("pe_t", [P, P])
            pr = [S.ps(f"pr{q}", [P, ROWS]) for q in range(4)]
            got, ea_in, res_out = S.pair("got"), S.pair("ea_in"), S.pair("res_out")
            staged, sent, ea_turned, ea_there, msg, squared, bounds, held = (
                S.sem(n) for n in ("staged", "sent", "ea_turned", "ea_there", "msg", "squared", "bounds", "held"))
            scanned = [S.sem(f"scanned{q}") for q in range(4)]
            back = [S.sem(f"back{q}") for q in range(4)]
            taken = [S.sem(f"taken{q}") for q in range(4)]
            EA_FULL = E // P - (GROUPS - 1) * TPG
            EA_REST = E - (E // P) * P

            with nc.Block() as block:
                @block.gpsimd
                def _(pool):
                    def gather(g, u, r):
                        drained(pool, got, u, r, 16 * TPG)
                        pool.sem_inc(sent, 1)
                        freed(pool, msg, g)
                        pool.sem_inc(sent, 1)
                        node_gather(pool, b0_tab, rows[:, u], src_i, stage, staged, got, sent, u, g)

                    pipeline(pool, gather)

                @block.sync
                def _(sp):
                    def load(g, u, r):
                        freed(sp, ea_turned, g)
                        src = a["edge_attr_10"]
                        if is_last(g):
                            o = (GROUPS - 1) * ROWS
                            sp.dma_start(ea[:, u, 0:EA_FULL, :], src[o:o + EA_FULL * P, :]
                                         .rearrange("(k p) d -> p k d", p=P)).then_inc(ea_in[u], 16)
                            sp.dma_start(ea[0:EA_REST, u, EA_FULL, :], src[o + EA_FULL * P:E, :]).then_inc(ea_in[u], 16)
                        else:
                            t = src[0:(GROUPS - 1) * ROWS, :].rearrange("(g k p) d -> g p k d", p=P, k=TPG)
                            t = t[g] if isinstance(g, int) else t[bass.ds(g, 1)].rearrange("o p k d -> (o p) k d")
                            sp.dma_start(ea[:, u, :, :], t).then_inc(ea_in[u], 16)

                    pipeline(sp, load)
                    end_of(sp, res_out)

                @block.tensor
                def _(pe):
                    def turn_ea(g, u, r):
                        if is_last(g):
                            pe.wait_ge(ea_in[u], 16 * (r + 2))
                        else:
                            landed(pe, ea_in, u, r)
                        passed(pe, ea_there, g)
                        pe.sem_inc(held, 1)
                        pe.transpose(pe_t[0:TPG * ED, :], ea[:, u].rearrange("p k d -> p (k d)"), ident[:, :])\
                            .then_inc(ea_turned, 1)

                    def messages(g, u, r):
                        landed(pe, got, u, r, 16 * TPG)
                        ready(pe, ea_there, g)
                        for q in range(4):
                            freed(pe, scanned[q], g)
                        for k in range(TPG):
                            pe.matmul(pt[u][:, k * P:(k + 1) * P], rows[:, u, k, :], ident[:, :], start=True, stop=False)
                            ins = pe.matmul(pt[u][:, k * P:(k + 1) * P], w_edge[:, k, :], ea_t[:, u, :],
                                            start=False, stop=True)
                        ins.then_inc(msg, 1)

                    def turn_back(g, u, r):
                        for q in range(4):
                            pe.wait_ge(scanned[q], g + 2)
                            passed(pe, taken[q], g)
                            for k in range(TPG):
                                ins = pe.transpose(pr[q][:, k * P:(k + 1) * P], run[q][:, u, k * P:(k + 1) * P],
                                                   ident[:, :])
                            ins.then_inc(back[q], 1)

                    pipeline(pe, (1, messages), (0, turn_ea), (2, turn_back))

                @block.vector
                def _(v):
                    for q in range(4):
                        v.memset(run[q][:, 1, ROWS - 1:ROWS], 0.0).then_inc(scanned[q], 1)

                    def scans(g, u, r):
                        m = keep[:, g * ROWS:(g + 1) * ROWS] if isinstance(g, int) else keep[:, bass.ds(g * ROWS, ROWS)]
                        ready(v, squared, g)
                        for q, (gate, data, op0, op1) in enumerate((
                                (m, pt[u][:, :], ALU.mult, ALU.add), (m, sq[:, u, :], ALU.mult, ALU.add),
                                (low[:, u, :], pt[u][:, :], ALU.add, ALU.max),
                                (high[:, u, :], pt[u][:, :], ALU.add, ALU.min))):
                            if q == 2:
                                ready(v, bounds, g)
                            v.wait_ge(scanned[q], g + 1)
                            freed(v, back[q], g)
                            v.tensor_tensor_scan(run[q][:, u, :], gate, data, run[q][:, 1 - u, ROWS - 1:ROWS],
                                                 op0, op1).then_inc(scanned[q], 1)

                    pipeline(v, (1, scans))

                @block.scalar
                def _(act):
                    def take_ea(g, u, r):
                        ready(act, ea_turned, g)
                        freed(act, msg, g)
                        act.copy(ea_t[:, u, :], pe_t[0:TPG * ED, :]).then_inc(ea_there, 1)

                    def gates(g, u, r):
                        m = keep[:, g * ROWS:(g + 1) * ROWS] if isinstance(g, int) else keep[:, bass.ds(g * ROWS, ROWS)]
                        if not at_start(g):
                            act.wait_ge(scanned[3], g)
                        act.activation(low[:, u, :], m, ACT.Copy, scale=BIG, bias=-BIG)
                        act.activation(high[:, u, :], m, ACT.Copy, scale=-BIG, bias=BIG).then_inc(bounds, 1)
                        ready(act, msg, g)
                        act.activation(sq[:, u, :], pt[u][:, :], ACT.Square).then_inc(squared, 1)

                    def take_back(g, u, r):
                        for q in range(4):
                            ready(act, back[q], g)
                            if q == 0:
                                drained(act, res_out, u, r)
                            act.copy(res[:, u, :, q, :], pr[q][:, :].rearrange("p (k d) -> p k d", k=TPG))\
                                .then_inc(taken[q], 1)

                    def store(g, u, r):
                        ready(act, taken[3], g)
                        act.dma_start(edge_rows_of(e0_tab, g), res[:, u, :, :, :].rearrange("p k q d -> p k (q d)"))\
                            .then_inc(res_out[u], 16)

                    pipeline(act, (1, gates), (0, take_ea), (3, store), (2, take_back))

        def scalars(g, which):
            s = nsc[:, g, which, :] if isinstance(g, int) else nsc[:, bass.ds(g, 1), which, :].rearrange("p o k -> p (o k)")
            return bc(s, D)

        def scalar_of(g, which, k):
            if isinstance(g, int):
                return nsc[:, g, which, k:k + 1]
            return nsc[:, bass.ds(g, 1), which, k]

        def row_bc(ap):
            return ap.unsqueeze(1).to_broadcast([P, TPG, D])

        def gather_steps(pool, table, rows, index, stage, staged, got, sent, used):
            def gather(g, u, r):
                drained(pool, got, u, r, 16 * TPG)
                pool.sem_inc(sent, 1)
                used(pool, g)
                pool.sem_inc(sent, 1)
                node_gather(pool, table, rows[:, u], index, stage, staged, got, sent, u, g)
            return gather

        with ExitStack() as c2:
            S = Scope(nc, c2, "n1")
            x, h0 = S.sb("x", [P, 2, TPG, D]), S.sb("h0", [P, 2, TPG, D])
            xc = S.sb("xc", [P, 2, TPG, D])
            h0t = S.sb("h0t", [P, 2, ROWS])
            agg = S.sb("agg", [P, 2, TPG, 4 * D])
            stage = S.sb("stage", [P, 2, TPG], I32)
            am, sq = S.sb("am", [P, TPG, D]), S.sb("sq", [P, TPG, D])
            mean = S.sb("mean", [P, TPG, D])
            var = S.sb("var", [P, 2, TPG, D])
            aggt = S.sb("aggt", [P, 4, ROWS])
            x1, h1 = S.sb("x1", [P, 2, TPG, D]), S.sb("h1", [P, 2, TPG, D])
            pt, pa = S.ps("pt", [P, ROWS]), S.ps("pa", [P, ROWS])
            pq = [S.ps(f"pq{i}", [P, ROWS]) for i in range(2)]
            py = [S.ps(f"py{k}", [P, 3 * D]) for k in range(TPG)]
            got, x_in, h_in, x_out, h_out = (S.pair(n) for n in ("got", "x_in", "h_in", "x_out", "h_out"))
            (staged, sent, turned, h0t_there, a_prod, a_biased, a_masked, means, sqs, squares, var_there, shifted, std_there, xc_there,
             q_turned, q_taken, prod, mix1, mix2, x1_there) = (S.sem(n) for n in (
                 "staged", "sent", "turned", "h0t_there", "a_prod", "a_biased", "a_masked", "means", "sqs", "squares",
                 "var_there", "shifted", "std_there", "xc_there", "q_turned", "q_taken", "prod", "mix1", "mix2", "x1_there"))
            relud, hop_staged, hop_taken = S.sem("relud"), S.sem("hop_staged"), S.sem("hop_taken")
            hop_rows = S.sb("hop_rows", [P, 2, TPG, 2])
            hop_stage = S.sb("hop_stage", [P, 2, TPG], I32)
            hop_got = S.pair("hop_got")
            ln = Norm(S, lambda u: x1[:, u], lambda u: h1[:, u])

            with nc.Block() as block:
                @block.gpsimd
                def _(pool):
                    gather = gather_steps(pool, e0_tab, agg, last_i, stage, staged, got, sent,
                                          lambda p, g: freed(p, q_turned, g, 4))

                    def add_bias(g, u, r):
                        landed(pool, x_in, u, r)
                        pool.sem_inc(sent, 1)
                        freed(pool, mix1, g)
                        pool.sem_inc(sent, 1)
                        pool.tensor_tensor(xc[:, u], x[:, u], row_bc(c_post[:, :]), ALU.add).then_inc(xc_there, 1)

                    hops = gather_steps(pool, hop_tab, hop_rows, src_i, hop_stage, hop_staged, hop_got, sent,
                                        lambda p, g: freed(p, hop_taken, g))
                    pipeline(pool, (0, gather), (0, add_bias), (0, hops))

                @block.sync
                def _(sp):
                    def load(g, u, r):
                        freed(sp, xc_there, g)
                        if is_last(g):
                            sp.dma_start(x[0:LAST_P, u, :, :], tail_rows(a["x"])).then_inc(x_in[u], 16)
                        else:
                            t = a["x"][0:(GROUPS - 1) * ROWS, :].rearrange("(g p k) d -> g p k d", p=P, k=TPG)
                            t = t[g] if isinstance(g, int) else t[bass.ds(g, 1)].rearrange("o p k d -> (o p) k d")
                            sp.dma_start(x[:, u, :, :], t).then_inc(x_in[u], 16)
                        freed(sp, turned, g)
                        sp.dma_start(h0[:, u, :, :], rows_of(h0_tab, g)).then_inc(h_in[u], 16)

                    pipeline(sp, load)
                    end_of(sp, x_out)
                    end_of(sp, h_out)

                @block.tensor
                def _(pe):
                    def turn_h0(g, u, r):
                        landed(pe, h_in, u, r)
                        passed(pe, h0t_there, g)
                        turn(pe, pt, h0[:, u], turned)

                    def times_a(g, u, r):
                        ready(pe, h0t_there, g)
                        passed(pe, a_biased, g)
                        for k in range(TPG):
                            ins = pe.matmul(pa[:, k * D:(k + 1) * D], h0t[:, u, k * P:(k + 1) * P], w_a[:, :],
                                            start=True, stop=True)
                        ins.then_inc(a_prod, 1)

                    def turn_agg(g, u, r):
                        for q in range(4):
                            if q == 0:
                                ready(pe, shifted, g)
                            if q == 3:
                                ready(pe, std_there, g)
                            if q < 2:
                                if not (isinstance(g, int) and g == 0):
                                    pe.wait_ge(q_taken, g * 4 - 1 + q)
                            else:
                                pe.wait_ge(q_taken, g * 4 + q - 1)
                            turn(pe, pq[q % 2], agg[:, u, :, q * D:(q + 1) * D], q_turned)

                    def project(g, u, r):
                        ready(pe, q_taken, g, 4)
                        for k in range(TPG):
                            if k == 0:
                                passed(pe, x1_there, g)
                            for q in range(4):
                                pe.matmul(py[k][:, :], aggt[:, q, k * P:(k + 1) * P],
                                          w_agg[:, q, :, :].rearrange("p j n -> p (j n)"), start=(q == 0), stop=False,
                                          skip_group_check=True)
                            ins = pe.matmul(py[k][:, 0:D], h0t[:, u, k * P:(k + 1) * P], w_self[:, :],
                                            start=False, stop=True, skip_group_check=True)
                        ins.then_inc(prod, 1)

                    def front(g, u, r):
                        turn_h0(g, u, r)
                        times_a(g, u, r)

                    pipeline(pe, (1, turn_agg), (0, front), (1, project))

                @block.vector
                def _(v):
                    def aggregates(g, u, r):
                        A = agg[:, u]
                        ready(v, a_prod, g)
                        passed(v, shifted, g)
                        v.tensor_tensor(am[:, :, :], pa[:, :].rearrange("p (k d) -> p k d", k=TPG), row_bc(c_pre[:, :]),
                                        ALU.add).then_inc(a_biased, 1)
                        landed(v, got, u, r, 16 * TPG)
                        v.tensor_tensor(mean[:, :, :], A[:, :, 0:D], scalars(g, S_INV), ALU.mult).then_inc(means, 1)
                        v.tensor_tensor(sq[:, :, :], A[:, :, D:2 * D], scalars(g, S_INV), ALU.mult).then_inc(sqs, 1)
                        ready(v, a_biased, g)
                        v.tensor_tensor(am[:, :, :], am[:, :, :], scalars(g, S_HAS), ALU.mult).then_inc(a_masked, 1)
                        ready(v, means, g)
                        freed(v, std_there, g)
                        v.tensor_tensor(var[:, u], mean[:, :, :], mean[:, :, :], ALU.mult).then_inc(squares, 1)
                        ready(v, a_masked, g)
                        ready(v, sqs, g)
                        v.tensor_tensor(A[:, :, 2 * D:3 * D], A[:, :, 2 * D:3 * D], am[:, :, :], ALU.add)
                        v.tensor_tensor(A[:, :, D:2 * D], A[:, :, 3 * D:4 * D], am[:, :, :], ALU.add)
                        v.tensor_tensor(A[:, :, 0:D], mean[:, :, :], am[:, :, :], ALU.add).then_inc(shifted, 1)
                        ready(v, squares, g)
                        v.tensor_tensor(var[:, u], sq[:, :, :], var[:, u], ALU.subtract).then_inc(var_there, 1)

                    def mix(g, u, r):
                        ready(v, prod, g)
                        ready(v, xc_there, g)
                        drained(v, x_out, u, r)
                        freed(v, ln.done, g)
                        for k in range(TPG):
                            ins = v.scalar_tensor_tensor(out=x1[:, u, k, :], in0=py[k][:, D:2 * D],
                                                         scalar=scalar_of(g, S_LOG, k), in1=xc[:, u, k, :],
                                                         op0=ALU.mult, op1=ALU.add)
                        ins.then_inc(mix1, 1)
                        ready(v, mix1, g)
                        for k in range(TPG):
                            ins = v.scalar_tensor_tensor(out=x1[:, u, k, :], in0=py[k][:, 2 * D:3 * D],
                                                         scalar=scalar_of(g, S_ALOG, k), in1=x1[:, u, k, :],
                                                         op0=ALU.mult, op1=ALU.add)
                        ins.then_inc(mix2, 1)
                        ready(v, mix2, g)
                        for k in range(TPG):
                            ins = v.tensor_tensor(x1[:, u, k, :], x1[:, u, k, :], py[k][:, 0:D], ALU.add)
                        ins.then_inc(x1_there, 1)
                        ready(v, x1_there, g)
                        ln.moments_of(v, g, u)

                    def scales(g, u, r):
                        ln.scale_of(v, g, u)

                    def take_hops(g, u, r):
                        landed(v, hop_got, u, r, 16 * TPG)
                        c = slice(g * TPG, (g + 1) * TPG) if isinstance(g, int) else bass.ds(g * TPG, TPG)
                        v.tensor_copy(hop_i[:, c], hop_rows[:, u, :, 0])
                        v.tensor_copy(hop_w[:, c], hop_rows[:, u, :, 1]).then_inc(hop_taken, 1)

                    pipeline(v, (2, scales), (0, aggregates), (1, take_hops), (1, mix))

                @block.scalar
                def _(act):
                    def take_h0t(g, u, r):
                        ready(act, turned, g)
                        freed(act, prod, g)
                        act.copy(h0t[:, u, :], pt[:, :]).then_inc(h0t_there, 1)

                    def std(g, u, r):
                        ready(act, var_there, g)
                        act.activation(var[:, u], var[:, u], ACT.Relu).then_inc(relud, 1)
                        ready(act, relud, g)
                        ready(act, shifted, g)
                        act.activation(agg[:, u, :, 3 * D:4 * D], var[:, u], ACT.Sqrt, bias=eps[:, :])\
                            .then_inc(std_there, 1)

                    def take_agg(g, u, r):
                        for q in range(4):
                            act.wait_ge(q_turned, g * 4 + q + 1)
                            if q == 0:
                                passed(act, prod, g)
                            act.copy(aggt[:, q, :], pq[q % 2][:, :]).then_inc(q_taken, 1)

                    def norm(g, u, r):
                        ln.root_of(act, g, u)
                        drained(act, h_out, u, r)
                        ln.relu_of(act, g, u)

                    def store(g, u, r):
                        ready(act, x1_there, g)
                        act.dma_start(rows_of(x1_tab, g), x1[:, u, :, :]).then_inc(x_out[u], 16)
                        ready(act, ln.done, g)
                        act.dma_start(rows_of(h1_tab, g), h1[:, u, :, :]).then_inc(h_out[u], 16)

                    pipeline(act, (1, take_agg), (0, take_h0t), (2, norm), (2, store), (0, std))

        with ExitStack() as c2:
            S = Scope(nc, c2, "m1")
            h1 = S.sb("h1", [P, 2, TPG, D])
            h1t, m1t, m2t = (S.sb(n, [P, 2, ROWS]) for n in ("h1t", "m1t", "m2t"))
            raw = S.sb("raw", [P, 2, TPG, D])
            msg = S.sb("msg", [P, 2, TPG, W_MSG])
            dlog = S.sb("dlog", [P, 2, TPG, 4])
            stage = S.sb("stage", [P, 2, TPG], I32)
            staged, sent = S.sem("staged"), S.sem("sent")
            pt, p1, p2 = (S.ps(n, [P, ROWS]) for n in ("pt", "p1", "p2"))
            p3 = [S.ps(f"p3_{u}", [P, ROWS]) for u in range(2)]
            p4 = [S.ps(f"p4_{u}", [P, TPG, 6]) for u in range(2)]
            h_in, m_out, d_out = S.pair("h_in"), S.pair("m_out"), S.pair("d_out")
            turned, h1t_there, prod1, m1_there, prod2, m2_there, prod3, raw_there, d_there, msg_there, cleared = (
                S.sem(n) for n in ("turned", "h1t_there", "prod1", "m1_there", "prod2", "m2_there", "prod3",
                                   "raw_there", "d_there", "msg_there", "cleared"))
            with nc.Block() as block:
                @block.sync
                def _(sp):
                    def load(g, u, r):
                        freed(sp, turned, g)
                        sp.dma_start(h1[:, u, :, :], rows_of(h1_tab, g)).then_inc(h_in[u], 16)

                    pipeline(sp, load)
                    end_of(sp, m_out)
                    end_of(sp, d_out, TPG * GROUPS // 2)

                @block.gpsimd
                def _(pool):
                    def scatter(g, u, r):
                        drained(pool, d_out, u, r, 16 * TPG)
                        pool.sem_inc(sent, 1)
                        cols = first_i[:, g * TPG:(g + 1) * TPG] if isinstance(g, int) else first_i[:, bass.ds(g * TPG, TPG)]
                        pool.tensor_copy(stage[:, u, :], cols).then_inc(staged, 1)
                        ready(pool, staged, g)
                        pool.sem_inc(sent, 1)
                        ready(pool, d_there, g)
                        pool.sem_inc(sent, 1)
                        for k in range(TPG):
                            pool.indirect_dma_start(out=dn_tab[:, :], in_=dlog[:, u, k, :], in_offset=None,
                                                    out_offset=bass.IndirectOffsetOnAxis(ap=stage[:, u, k:k + 1], axis=0))\
                                .then_inc(d_out[u], 16)

                    pool.wait_ge(cleared, 1)
                    pipeline(pool, scatter)

                @block.tensor
                def _(pe):
                    def turn_h(g, u, r):
                        landed(pe, h_in, u, r)
                        passed(pe, h1t_there, g)
                        turn(pe, pt, h1[:, u], turned)

                    def first(g, u, r):
                        ready(pe, h1t_there, g)
                        passed(pe, m1_there, g)
                        pe.matmul(p1[:, :], w_m1[:, :], h1t[:, u, :], start=True, stop=True).then_inc(prod1, 1)

                    def second(g, u, r):
                        ready(pe, m1_there, g)
                        passed(pe, m2_there, g)
                        pe.matmul(p2[:, :], w_m2[:, :], m1t[:, u, :], start=True, stop=True).then_inc(prod2, 1)

                    def third(g, u, r):
                        ready(pe, m2_there, g)
                        freed(pe, raw_there, g)
                        freed(pe, d_there, g)
                        for k in range(TPG):
                            rows = slice(k * P, (k + 1) * P)
                            pe.matmul(p4[u][:, k, :], h1t[:, u, rows], w_att[:, :], start=True, stop=True)
                            ins = pe.matmul(p3[u][:, k * D:(k + 1) * D], m2t[:, u, rows], w_m3[:, :],
                                            start=True, stop=True)
                        ins.then_inc(prod3, 1)

                    pipeline(pe, (0, turn_h), (2, third), (1, second), (0, first))

                @block.scalar
                def _(act):
                    def take_h(g, u, r):
                        ready(act, turned, g)
                        freed(act, prod3, g)
                        act.copy(h1t[:, u, :], pt[:, :]).then_inc(h1t_there, 1)

                    def relu1(g, u, r):
                        ready(act, prod1, g)
                        freed(act, prod2, g)
                        act.activation(m1t[:, u, :], p1[:, :], ACT.Relu, bias=c_m1[:, :]).then_inc(m1_there, 1)

                    def relu2(g, u, r):
                        ready(act, prod2, g)
                        freed(act, prod3, g)
                        act.activation(m2t[:, u, :], p2[:, :], ACT.Relu, bias=c_m2[:, :]).then_inc(m2_there, 1)

                    def relu3(g, u, r):
                        ready(act, raw_there, g)
                        drained(act, m_out, u, r)
                        act.activation(msg[:, u, :, 0:D], raw[:, u], ACT.Relu).then_inc(msg_there, 1)

                    def store(g, u, r):
                        ready(act, msg_there, g)
                        act.dma_start(rows_of(m1_tab, g), msg[:, u, :, :]).then_inc(m_out[u], 16)

                    pipeline(act, (0, take_h), (1, relu2), (0, relu1), (2, relu3), (2, store))

                @block.vector
                def _(v):
                    v.memset(msg[:, :, :, D + 3:D + 4], 0.0)
                    v.memset(dlog[:, :, :, 3:4], 0.0).then_inc(cleared, 1)

                    def take(g, u, r):
                        ready(v, prod3, g)
                        freed(v, msg_there, g)
                        drained(v, m_out, u, r)
                        v.tensor_tensor(raw[:, u], p3[u][:, :].rearrange("p (k d) -> p k d", k=TPG),
                                        row_bc(c_m3[:, :]), ALU.add)
                        v.tensor_copy(msg[:, u, :, D:D + 3], p4[u][:, :, 0:3]).then_inc(raw_there, 1)
                        drained(v, d_out, u, r, 16 * TPG)
                        v.tensor_tensor(dlog[:, u, :, 0:3], p4[u][:, :, 3:6],
                                        c_att[:, 0:3].unsqueeze(1).to_broadcast([P, TPG, 3]), ALU.add).then_inc(d_there, 1)

                    pipeline(v, (2, take))

        with ExitStack() as c2:
            S = Scope(nc, c2, "sd")
            sparse, spread = S.sb("sparse", [P, TILES, 4]), S.sb("spread", [P, TILES, 4])
            same = S.sb("same", [P, TILES], U8)
            through = S.sb("through", [P, TILES])
            ends = S.sb("ends", [P, 2, 4])
            gate = S.sb("gate", [4, P])
            ends_t = S.sb("ends_t", [4, P + 1])
            carry = S.sb("carry", [P, 4])
            pv, pg, pc = S.ps("pv", [4, P]), S.ps("pg", [4, P]), S.ps("pc", [P, 4])
            loaded, scanned, ended, turned, gated, linked, back, carried, fixed, stored = (S.sem(n) for n in (
                "loaded", "scanned", "ended", "turned", "gated", "linked", "back", "carried", "fixed", "stored"))
            with nc.Block() as block:
                @block.sync
                def _(sp):
                    sp.dma_start(same[:, :], keep_row.rearrange("t c -> (t c)").rearrange("(p c) -> p c", p=P))\
                        .then_inc(loaded, 16)
                    sp.dma_start(sparse[:, :, :], dn_tab[0:NPAD, :].rearrange("(p c) w -> p c w", p=P)).then_inc(loaded, 16)
                    sp.wait_ge(fixed, 3)
                    sp.dma_start(d1_tab.rearrange("(p c) w -> p c w", p=P), spread[:, :, :]).then_inc(stored, 16)
                    sp.wait_ge(stored, 16)

                @block.vector
                def _(v):
                    v.memset(ends_t[:, 0:1], 0.0).then_inc(ended, 1)
                    v.memset(spread[:, :, 3:4], 0.0)
                    v.wait_ge(loaded, 32)
                    for j in range(3):
                        v.tensor_tensor_scan(spread[:, :, j], same[:, :], sparse[:, :, j], 0.0, ALU.mult, ALU.add)
                    v.tensor_tensor_scan(through[:, :], same[:, :], same[:, :], 1.0, ALU.mult, ALU.min).then_inc(scanned, 1)
                    v.wait_ge(scanned, 1)
                    v.tensor_copy(ends[:, 0, :], spread[:, TILES - 1, :])
                    v.tensor_copy(ends[:, 1, :], through[:, TILES - 1:TILES].to_broadcast([P, 4])).then_inc(ended, 1)
                    v.wait_ge(turned, 1)
                    v.tensor_copy(gate[:, :], pg[:, :]).then_inc(gated, 1)
                    v.wait_ge(gated, 1)
                    v.wait_ge(ended, 2)
                    v.tensor_tensor_scan(ends_t[:, 1:P + 1], gate[:, :], pv[:, :], 0.0, ALU.mult, ALU.add).then_inc(linked, 1)
                    v.wait_ge(back, 1)
                    v.tensor_copy(carry[:, :], pc[:, :]).then_inc(carried, 1)
                    v.wait_ge(carried, 1)
                    for j in range(3):
                        v.scalar_tensor_tensor(out=spread[:, :, j], in0=through[:, :], scalar=carry[:, j:j + 1],
                                               in1=spread[:, :, j], op0=ALU.mult, op1=ALU.add).then_inc(fixed, 1)

                @block.tensor
                def _(pe):
                    pe.wait_ge(ended, 2)
                    pe.transpose(pv[:, :], ends[:, 0, :], ident[:, :])
                    pe.transpose(pg[:, :], ends[:, 1, :], ident[:, :]).then_inc(turned, 1)
                    pe.wait_ge(linked, 1)
                    pe.transpose(pc[:, :], ends_t[:, 0:P], ident[0:4, 0:4]).then_inc(back, 1)

        with ExitStack() as c2:
            S = Scope(nc, c2, "e1")
            rows = S.sb("rows", [P, 2, TPG, W_MSG])
            drow = S.sb("drow", [P, 2, TPG, 4])
            stage = S.sb("stage", [P, 2, TPG], I32)
            logit = S.sb("logit", [P, 2, TPG, 3])
            weight = S.sb("weight", [P, 2, TPG, 3])
            scaled = S.sb("scaled", [P, 2, TPG, 3, D])
            run = [S.sb(f"run{j}", [P, 2, ROWS]) for j in range(3)]
            runw = S.sb("runw", [3, 2, ROWS])
            res = S.sb("res", [P, 2, TPG, W_ATT])
            pt = [S.ps(f"pt{j}", [P, ROWS]) for j in range(3)]
            pw = S.ps("pw", [3, ROWS])
            pr = [S.ps(f"pr{j}", [P, ROWS]) for j in range(3)]
            prw = S.ps("prw", [P, TPG, 4])
            got, d_in, res_out = S.pair("got"), S.pair("d_in"), S.pair("res_out")
            (staged, sent, logits, logits2, weights, scaled_there, cleared, held) = (
                S.sem(n) for n in ("staged", "sent", "logits", "logits2", "weights", "scaled_there", "cleared", "held"))
            turned = [S.sem(f"turned{j}") for j in range(4)]
            scanned = [S.sem(f"scanned{j}") for j in range(4)]
            back = [S.sem(f"back{j}") for j in range(4)]
            taken = [S.sem(f"taken{j}") for j in range(4)]

            with nc.Block() as block:
                @block.gpsimd
                def _(pool):
                    pipeline(pool, gather_steps(pool, m1_tab, rows, src_i, stage, staged, got, sent,
                                                lambda p, g: freed(p, scaled_there, g)))

                @block.vector
                def _(v):
                    for j in range(3):
                        v.memset(run[j][:, 1, ROWS - 1:ROWS], 0.0).then_inc(scanned[j], 1)
                    v.memset(runw[:, 1, ROWS - 1:ROWS], 0.0).then_inc(scanned[3], 1)
                    v.memset(res[:, :, :, 3 * D + 3:W_ATT], 0.0).then_inc(cleared, 1)

                    def logits_of(g, u, r):
                        landed(v, got, u, r, 16 * TPG)
                        landed(v, d_in, u, r)
                        freed(v, weights, g)
                        v.tensor_tensor(logit[:, u], rows[:, u, :, D:D + 3], drow[:, u, :, 0:3], ALU.add)\
                            .then_inc(logits, 1)
                        ready(v, logits, g)
                        v.tensor_scalar(logit[:, u], logit[:, u], 0.0, None, ALU.max).then_inc(logits2, 1)

                    def scale_rows(g, u, r):
                        ready(v, weights, g)
                        for j in range(4):
                            freed(v, turned[j], g)
                        for k in range(TPG):
                            ins = v.tensor_tensor(scaled[:, u, k], rows[:, u, k, 0:D].unsqueeze(1).to_broadcast([P, 3, D]),
                                                  bc(weight[:, u, k, :], D), ALU.mult)
                        ins.then_inc(scaled_there, 1)

                    def scans(g, u, r):
                        m = keep[:, g * ROWS:(g + 1) * ROWS] if isinstance(g, int) else keep[:, bass.ds(g * ROWS, ROWS)]
                        for j in range(4):
                            ready(v, turned[j], g)
                            v.wait_ge(scanned[j], g + 1)
                            freed(v, back[j], g)
                            t, p = (run[j], pt[j]) if j < 3 else (runw, pw)
                            n = P if j < 3 else 3
                            v.tensor_tensor_scan(t[:, u, :], m[0:n], p[:, :], t[:, 1 - u, ROWS - 1:ROWS],
                                                 ALU.mult, ALU.add).then_inc(scanned[j], 1)

                    pipeline(v, (2, scans), (0, logits_of), (0, scale_rows))

                @block.scalar
                def _(act):
                    def exps(g, u, r):
                        ready(act, logits2, g)
                        freed(act, scaled_there, g)
                        freed(act, turned[3], g)
                        act.activation(weight[:, u], logit[:, u], ACT.Exp).then_inc(weights, 1)

                    def take_back(g, u, r):
                        for j in range(4):
                            ready(act, back[j], g)
                            if j == 0:
                                drained(act, res_out, u, r)
                            if j < 3:
                                act.copy(res[:, u, :, j * D:(j + 1) * D],
                                         pr[j][:, :].rearrange("p (k d) -> p k d", k=TPG)).then_inc(taken[j], 1)
                            else:
                                act.copy(res[:, u, :, 3 * D:3 * D + 3], prw[:, :, 0:3]).then_inc(taken[3], 1)

                    def store(g, u, r):
                        ready(act, taken[3], g)
                        act.dma_start(edge_rows_of(e1_tab, g), res[:, u, :, :]).then_inc(res_out[u], 16)

                    act.wait_ge(cleared, 1)
                    pipeline(act, (0, exps), (3, take_back), (4, store))

                @block.tensor
                def _(pe):
                    def turn_in(g, u, r):
                        ready(pe, scaled_there, g)
                        for j in range(3):
                            pe.wait_ge(scanned[j], g + 1)
                            turn(pe, pt[j], scaled[:, u, :, j, :], turned[j])
                        pe.wait_ge(scanned[3], g + 1)
                        pe.sem_inc(held, 1)
                        for k in range(TPG):
                            ins = pe.transpose(pw[0:3, k * P:(k + 1) * P], weight[:, u, k, :], ident[:, :])
                        ins.then_inc(turned[3], 1)

                    def turn_back(g, u, r):
                        for j in range(3):
                            pe.wait_ge(scanned[j], g + 2)
                            passed(pe, taken[j], g)
                            for k in range(TPG):
                                ins = pe.transpose(pr[j][:, k * P:(k + 1) * P], run[j][:, u, k * P:(k + 1) * P],
                                                   ident[:, :])
                            ins.then_inc(back[j], 1)
                        pe.wait_ge(scanned[3], g + 2)
                        passed(pe, taken[3], g)
                        pe.sem_inc(held, 1)
                        for k in range(TPG):
                            ins = pe.transpose(prw[:, k, 0:3], runw[0:3, u, k * P:(k + 1) * P], ident[0:3, 0:3])
                        ins.then_inc(back[3], 1)

                    pipeline(pe, (2, turn_back), (0, turn_in))

                @block.sync
                def _(sp):
                    def load(g, u, r):
                        freed(sp, logits, g)
                        sp.dma_start(drow[:, u, :, :], edge_rows_of(d1_tab, g)).then_inc(d_in[u], 16)

                    pipeline(sp, load)
                    end_of(sp, res_out)

        with ExitStack() as c2:
            S = Scope(nc, c2, "n2")
            x1, h1 = S.sb("x1", [P, 2, TPG, D]), S.sb("h1", [P, 2, TPG, D])
            x1c = S.sb("x1c", [P, 2, TPG, D])
            sums = S.sb("sums", [P, 2, TPG, W_ATT])
            stage = S.sb("stage", [P, 2, TPG], I32)
            wsum = S.sb("wsum", [P, TPG, 3])
            winv = S.sb("winv", [P, TPG, 3])
            wnode = S.sb("wnode", [P, TPG, 3])
            hn = S.sb("hn", [P, 2, TPG, D])
            h1t, hnt, ut, h2t = (S.sb(n, [P, 2, ROWS]) for n in ("h1t", "hnt", "ut", "h2t"))
            x2, h2, t2 = (S.sb(n, [P, 2, TPG, D]) for n in ("x2", "h2", "t2"))
            pt, pn, pu, pt2 = (S.ps(n, [P, ROWS]) for n in ("pt", "pn", "pu", "pt2"))
            po = [S.ps(f"po{u}", [P, ROWS]) for u in range(2)]
            pg = [S.ps(f"pg{u}", [P, ROWS]) for u in range(2)]
            got, x_in, h_in, x_out, t_out = (S.pair(n) for n in ("got", "x_in", "h_in", "x_out", "t_out"))
            (staged, sent, w_floor, w_inv, w_there, hn1, hn2, hn_there, h_turned, n_turned, h1t_there, hnt_there, u_prod,
             u_there, o_prod, x1c_there, x2_there, h2_turned, h2t_there, g_prod, t2_there) = (S.sem(n) for n in (
                 "staged", "sent", "w_floor", "w_inv", "w_there", "hn1", "hn2", "hn_there", "h_turned", "n_turned",
                 "h1t_there", "hnt_there", "u_prod", "u_there", "o_prod", "x1c_there", "x2_there", "h2_turned",
                 "h2t_there", "g_prod", "t2_there"))
            ln = Norm(S, lambda u: x2[:, u], lambda u: h2[:, u])

            with nc.Block() as block:
                @block.gpsimd
                def _(pool):
                    gather = gather_steps(pool, e1_tab, sums, last_i, stage, staged, got, sent,
                                          lambda p, g: freed(p, hn_there, g))

                    def add_bias(g, u, r):
                        landed(pool, x_in, u, r)
                        pool.sem_inc(sent, 1)
                        freed(pool, x2_there, g)
                        pool.sem_inc(sent, 1)
                        pool.tensor_tensor(x1c[:, u], x1[:, u], row_bc(c_c2[:, :]), ALU.add).then_inc(x1c_there, 1)

                    pipeline(pool, (0, gather), (0, add_bias))

                @block.sync
                def _(sp):
                    def load(g, u, r):
                        freed(sp, x1c_there, g)
                        sp.dma_start(x1[:, u, :, :], rows_of(x1_tab, g)).then_inc(x_in[u], 16)
                        freed(sp, h_turned, g)
                        sp.dma_start(h1[:, u, :, :], rows_of(h1_tab, g)).then_inc(h_in[u], 16)

                    pipeline(sp, load)
                    end_of(sp, x_out)
                    end_of(sp, t_out)

                @block.vector
                def _(v):
                    def neighbours(g, u, r):
                        landed(v, got, u, r, 16 * TPG)
                        v.tensor_scalar(wsum[:, :, :], sums[:, u, :, 3 * D:3 * D + 3], 1.0, None, ALU.max).then_inc(w_floor, 1)
                        ready(v, w_floor, g)
                        v.reciprocal(winv[:, :, :], wsum[:, :, :]).then_inc(w_inv, 1)
                        ready(v, w_inv, g)
                        third = nsc[:, g, S_THIRD, :] if isinstance(g, int) else nsc[:, bass.ds(g, 1), S_THIRD, :]\
                            .rearrange("p o k -> p (o k)")
                        v.tensor_tensor(wnode[:, :, :], winv[:, :, :], bc(third, 3), ALU.mult).then_inc(w_there, 1)
                        ready(v, w_there, g)
                        freed(v, n_turned, g)
                        for k in range(TPG):
                            ins = v.tensor_scalar(hn[:, u, k, :], sums[:, u, k, 0:D], wnode[:, k, 0:1], None, ALU.mult)
                        ins.then_inc(hn1, 1)
                        for j, (before_, after_) in ((1, (hn1, hn2)), (2, (hn2, hn_there))):
                            ready(v, before_, g)
                            for k in range(TPG):
                                ins = v.scalar_tensor_tensor(out=hn[:, u, k, :], in0=sums[:, u, k, j * D:(j + 1) * D],
                                                             scalar=wnode[:, k, j:j + 1], in1=hn[:, u, k, :],
                                                             op0=ALU.mult, op1=ALU.add)
                            ins.then_inc(after_, 1)

                    def update(g, u, r):
                        ready(v, o_prod, g)
                        ready(v, x1c_there, g)
                        drained(v, x_out, u, r)
                        freed(v, ln.done, g)
                        v.tensor_tensor(flat(x2[:, u]), flat(x1c[:, u]), po[u][:, :], ALU.add).then_inc(x2_there, 1)
                        ready(v, x2_there, g)
                        ln.moments_of(v, g, u)

                    def scales(g, u, r):
                        ln.scale_of(v, g, u)

                    def gcn_rows(g, u, r):
                        ready(v, g_prod, g)
                        drained(v, t_out, u, r)
                        v.tensor_tensor(t2[:, u], pg[u][:, :].rearrange("p (k d) -> p k d", k=TPG), scalars(g, S_GCN),
                                        ALU.mult).then_inc(t2_there, 1)

                    pipeline(v, (0, neighbours), (2, scales), (3, gcn_rows), (1, update))

                @block.scalar
                def _(act):
                    def take_in(g, u, r):
                        ready(act, h_turned, g)
                        freed(act, u_prod, g)
                        act.copy(h1t[:, u, :], pt[:, :]).then_inc(h1t_there, 1)
                        ready(act, n_turned, g)
                        act.copy(hnt[:, u, :], pn[:, :]).then_inc(hnt_there, 1)

                    def relu_u(g, u, r):
                        ready(act, u_prod, g)
                        freed(act, o_prod, g)
                        act.activation(ut[:, u, :], pu[:, :], ACT.Relu, bias=c_c1[:, :]).then_inc(u_there, 1)

                    def norm(g, u, r):
                        ln.root_of(act, g, u)
                        freed(act, h2_turned, g)
                        ln.relu_of(act, g, u)

                    def take_h2(g, u, r):
                        ready(act, h2_turned, g)
                        freed(act, g_prod, g)
                        act.copy(h2t[:, u, :], pt2[:, :]).then_inc(h2t_there, 1)

                    def store(g, u, r):
                        ready(act, x2_there, g)
                        act.dma_start(rows_of(x2_tab, g), x2[:, u, :, :]).then_inc(x_out[u], 16)

                    def store_t(g, u, r):
                        ready(act, t2_there, g)
                        act.dma_start(rows_of(t2_tab, g), t2[:, u, :, :]).then_inc(t_out[u], 16)

                    pipeline(act, (2, norm), (0, take_in), (4, store_t), (2, store), (2, take_h2), (0, relu_u))

                @block.tensor
                def _(pe):
                    def turn_in(g, u, r):
                        landed(pe, h_in, u, r)
                        passed(pe, h1t_there, g)
                        turn(pe, pt, h1[:, u], h_turned)
                        ready(pe, hn_there, g)
                        passed(pe, hnt_there, g)
                        turn(pe, pn, hn[:, u], n_turned)

                    def hidden(g, u, r):
                        ready(pe, hnt_there, g)
                        passed(pe, u_there, g)
                        pe.matmul(pu[:, :], w_c1a[:, :], h1t[:, u, :], start=True, stop=False)
                        pe.matmul(pu[:, :], w_c1b[:, :], hnt[:, u, :], start=False, stop=True).then_inc(u_prod, 1)

                    def output(g, u, r):
                        ready(pe, u_there, g)
                        freed(pe, x2_there, g)
                        for k in range(TPG):
                            ins = pe.matmul(po[u][:, k * D:(k + 1) * D], ut[:, u, k * P:(k + 1) * P], w_c2[:, :],
                                            start=True, stop=True)
                        ins.then_inc(o_prod, 1)

                    def turn_h2(g, u, r):
                        ready(pe, ln.done, g)
                        passed(pe, h2t_there, g)
                        turn(pe, pt2, h2[:, u], h2_turned)

                    def gcn(g, u, r):
                        ready(pe, h2t_there, g)
                        freed(pe, t2_there, g)
                        for k in range(TPG):
                            ins = pe.matmul(pg[u][:, k * D:(k + 1) * D], h2t[:, u, k * P:(k + 1) * P], w_gcn[:, :],
                                            start=True, stop=True)
                        ins.then_inc(g_prod, 1)

                    pipeline(pe, (1, output), (0, turn_in), (2, turn_h2), (0, hidden), (2, gcn))

        def edge_sums(name, table, index, weights, out_tab, sum_in=None, sum_out=None):
            with ExitStack() as c2:
                S = Scope(nc, c2, name)
                rows = S.sb("rows", [P, 2, TPG, D])
                diag = S.sb("diag", [P, 2, TPG, P])
                stage = S.sb("stage", [P, 2, TPG], I32)
                run = S.sb("run", [P, 2, ROWS])
                res, tot, more = (S.sb(n, [P, 2, TPG, D]) for n in ("res", "tot", "more"))
                pt = [S.ps(f"pt{u}", [P, ROWS]) for u in range(2)]
                pr = [S.ps(f"pr{u}", [P, ROWS]) for u in range(2)]
                got, res_out, tot_out, more_in = (S.pair(n) for n in ("got", "res_out", "tot_out", "more_in"))
                staged, sent, weighted, turned, scanned, back, res_there, tot_there = (S.sem(n) for n in (
                    "staged", "sent", "weighted", "turned", "scanned", "back", "res_there", "tot_there"))
                with nc.Block() as block:
                    @block.gpsimd
                    def _(pool):
                        pipeline(pool, gather_steps(pool, table, rows, index, stage, staged, got, sent,
                                                    lambda p, g: freed(p, turned, g)))

                    @block.tensor
                    def _(pe):
                        def turn_in(g, u, r):
                            landed(pe, got, u, r, 16 * TPG)
                            if weights is not None:
                                ready(pe, weighted, g)
                            if not at_start(g):
                                pe.wait_ge(scanned, g)
                            if weights is None:
                                turn(pe, pt[u], rows[:, u], turned)
                            else:
                                for k in range(TPG):
                                    ins = pe.matmul(pt[u][:, k * P:(k + 1) * P], rows[:, u, k, :], diag[:, u, k, :],
                                                    start=True, stop=True)
                                ins.then_inc(turned, 1)

                        def turn_back(g, u, r):
                            pe.wait_ge(scanned, g + 2)
                            freed(pe, res_there if out_tab is not None else tot_there, g)
                            if out_tab is not None and sum_in is not None:
                                freed(pe, tot_there, g)
                            for k in range(TPG):
                                ins = pe.transpose(pr[u][:, k * P:(k + 1) * P], run[:, u, k * P:(k + 1) * P], ident[:, :])
                            ins.then_inc(back, 1)

                        pipeline(pe, turn_in, turn_back)

                    @block.vector
                    def _(v):
                        v.memset(run[:, 1, ROWS - 1:ROWS], 0.0).then_inc(scanned, 1)

                        def scan(g, u, r):
                            m = keep[:, g * ROWS:(g + 1) * ROWS] if isinstance(g, int) else keep[:, bass.ds(g * ROWS, ROWS)]
                            ready(v, turned, g)
                            v.wait_ge(scanned, g + 1)
                            freed(v, back, g)
                            v.tensor_tensor_scan(run[:, u, :], m, pt[u][:, :], run[:, 1 - u, ROWS - 1:ROWS],
                                                 ALU.mult, ALU.add).then_inc(scanned, 1)

                        def total(g, u, r):
                            landed(v, more_in, u, r)
                            drained(v, tot_out, u, r)
                            if out_tab is not None:
                                ready(v, res_there, g)
                                v.tensor_tensor(tot[:, u], res[:, u], more[:, u], ALU.add).then_inc(tot_there, 1)
                            else:
                                ready(v, back, g)
                                v.tensor_tensor(flat(tot[:, u]), pr[u][:, :], flat(more[:, u]), ALU.add).then_inc(tot_there, 1)

                        pipeline(v, *([(0, scan)] + [(1, total)] * (sum_in is not None)))

                    @block.scalar
                    def _(act):
                        def weigh(g, u, r):
                            freed(act, turned, g)
                            for k in range(TPG):
                                c = slice(g * TPG + k, g * TPG + k + 1) if isinstance(g, int) else bass.ds(g * TPG + k, 1)
                                ins = act.activation(diag[:, u, k, :], ident[:, :], ACT.Copy, scale=weights[:, c])
                            ins.then_inc(weighted, 1)

                        def take(g, u, r):
                            ready(act, back, g)
                            drained(act, res_out, u, r)
                            if sum_in is not None:
                                freed(act, tot_there, g)
                            act.copy(flat(res[:, u]), pr[u][:, :]).then_inc(res_there, 1)

                        def store(g, u, r):
                            ready(act, res_there, g)
                            act.dma_start(edge_rows_of(out_tab, g), res[:, u, :, :]).then_inc(res_out[u], 16)

                        def store_tot(g, u, r):
                            ready(act, tot_there, g)
                            act.dma_start(edge_rows_of(sum_out, g), tot[:, u, :, :]).then_inc(tot_out[u], 16)

                        pipeline(act, *([(0, weigh)] * (weights is not None)
                                        + [(2, take), (2, store)] * (out_tab is not None)
                                        + [(3, store_tot)] * (sum_in is not None)))

                    @block.sync
                    def _(sp):
                        def load(g, u, r):
                            freed(sp, tot_there, g)
                            sp.dma_start(more[:, u, :, :], edge_rows_of(sum_in, g)).then_inc(more_in[u], 16)

                        if sum_in is not None:
                            pipeline(sp, load)
                        if out_tab is not None:
                            end_of(sp, res_out)
                        if sum_in is not None:
                            end_of(sp, tot_out)

        edge_sums("e2", t2_tab, src_i, None, e2_tab)

        with ExitStack() as c2:
            S = Scope(nc, c2, "n3")
            e2, x2, t2, x2c, s2, x3, h3, z0, y = (S.sb(n, [P, 2, TPG, D]) for n in (
                "e2", "x2", "t2", "x2c", "s2", "x3", "h3", "z0", "y"))
            stage = S.sb("stage", [P, 2, TPG], I32)
            got, x_in, t_in, z_out, y_out = (S.pair(n) for n in ("got", "x_in", "t_in", "z_out", "y_out"))
            staged, sent, x2c_there, sum1, sum2, x3_there, z0_there, y_there = (S.sem(n) for n in (
                "staged", "sent", "x2c_there", "sum1", "sum2", "x3_there", "z0_there", "y_there"))
            ln = Norm(S, lambda u: x3[:, u], lambda u: h3[:, u])
            with nc.Block() as block:
                @block.gpsimd
                def _(pool):
                    gather = gather_steps(pool, e2_tab, e2, last_i, stage, staged, got, sent,
                                          lambda p, g: freed(p, sum1, g))

                    pipeline(pool, gather)

                @block.sync
                def _(sp):
                    def load(g, u, r):
                        freed(sp, x2c_there, g)
                        sp.dma_start(x2[:, u, :, :], rows_of(x2_tab, g)).then_inc(x_in[u], 16)
                        freed(sp, sum1, g)
                        sp.dma_start(t2[:, u, :, :], rows_of(t2_tab, g)).then_inc(t_in[u], 16)

                    pipeline(sp, load)
                    end_of(sp, z_out)
                    end_of(sp, y_out)

                @block.vector
                def _(v):
                    def update(g, u, r):
                        landed(v, x_in, u, r)
                        freed(v, x3_there, g)
                        v.tensor_tensor(x2c[:, u], x2[:, u], row_bc(c_gcn[:, :]), ALU.add).then_inc(x2c_there, 1)
                        landed(v, got, u, r, 16 * TPG)
                        landed(v, t_in, u, r)
                        v.tensor_tensor(s2[:, u], e2[:, u], t2[:, u], ALU.add).then_inc(sum1, 1)
                        ready(v, sum1, g)
                        v.tensor_tensor(s2[:, u], s2[:, u], scalars(g, S_GCN), ALU.mult).then_inc(sum2, 1)
                        ready(v, sum2, g)
                        ready(v, x2c_there, g)
                        freed(v, ln.done, g)
                        freed(v, y_there, g)
                        v.tensor_tensor(x3[:, u], s2[:, u], x2c[:, u], ALU.add).then_inc(x3_there, 1)
                        ready(v, x3_there, g)
                        ln.moments_of(v, g, u)

                    def scales(g, u, r):
                        ln.scale_of(v, g, u)

                    def outputs(g, u, r):
                        ready(v, ln.done, g)
                        drained(v, y_out, u, r)
                        v.scalar_tensor_tensor(out=y[:, u], in0=h3[:, u], scalar=0.25, in1=x3[:, u],
                                               op0=ALU.mult, op1=ALU.add).then_inc(y_there, 1)

                    pipeline(v, (1, scales), (0, update), (1, outputs))

                @block.scalar
                def _(act):
                    def norm(g, u, r):
                        ln.root_of(act, g, u)
                        freed(act, y_there, g)
                        freed(act, z0_there, g)
                        ln.relu_of(act, g, u)

                    def z0_rows(g, u, r):
                        ready(act, ln.done, g)
                        drained(act, z_out, u, r)
                        for k in range(TPG):
                            ins = act.activation(z0[:, u, k, :], h3[:, u, k, :], ACT.Copy, scale=scalar_of(g, S_DINV, k))
                        ins.then_inc(z0_there, 1)

                    def store(g, u, r):
                        ready(act, z0_there, g)
                        act.dma_start(rows_of(z0_tab, g), z0[:, u, :, :]).then_inc(z_out[u], 16)
                        ready(act, y_there, g)
                        act.dma_start(rows_of(y_tab, g), y[:, u, :, :]).then_inc(y_out[u], 16)

                    pipeline(act, (0, norm), (1, z0_rows), (1, store))

        edge_sums("g1", z0_tab, src_i, None, r1_tab)
        edge_sums("g2", r1_tab, hop_i, hop_w, r2_tab, sum_in=r1_tab, sum_out=a2_tab)
        edge_sums("g3", r2_tab, hop_i, hop_w, None, sum_in=a2_tab, sum_out=a3_tab)

        with ExitStack() as c2:
            S = Scope(nc, c2, "n4")
            e3, y, s3, res = (S.sb(n, [P, 2, TPG, D]) for n in ("e3", "y", "s3", "res"))
            stage = S.sb("stage", [P, 2, TPG], I32)
            got, y_in, res_out = (S.pair(n) for n in ("got", "y_in", "res_out"))
            staged, sent, scaled, res_there = (S.sem(n) for n in ("staged", "sent", "scaled", "res_there"))
            with nc.Block() as block:
                @block.gpsimd
                def _(pool):
                    pipeline(pool, gather_steps(pool, a3_tab, e3, last_i, stage, staged, got, sent,
                                                lambda p, g: freed(p, scaled, g)))

                @block.vector
                def _(v):
                    def update(g, u, r):
                        landed(v, got, u, r, 16 * TPG)
                        v.tensor_tensor(s3[:, u], e3[:, u], scalars(g, S_DINV), ALU.mult).then_inc(scaled, 1)
                        ready(v, scaled, g)
                        landed(v, y_in, u, r)
                        drained(v, res_out, u, r)
                        v.scalar_tensor_tensor(out=res[:, u], in0=s3[:, u], scalar=0.25, in1=y[:, u],
                                               op0=ALU.mult, op1=ALU.add).then_inc(res_there, 1)

                    pipeline(v, update)

                @block.sync
                def _(sp):
                    def load(g, u, r):
                        freed(sp, res_there, g)
                        sp.dma_start(y[:, u, :, :], rows_of(y_tab, g)).then_inc(y_in[u], 16)

                    pipeline(sp, load)
                    end_of(sp, res_out)

                @block.scalar
                def _(act):
                    def store(g, u, r):
                        ready(act, res_there, g)
                        if is_last(g):
                            act.dma_start(tail_rows(out), res[0:LAST_P, u, :, :]).then_inc(res_out[u], 16)
                        else:
                            t = out[0:(GROUPS - 1) * ROWS, :].rearrange("(g p k) d -> g p k d", p=P, k=TPG)
                            t = t[g] if isinstance(g, int) else t[bass.ds(g, 1)].rearrange("o p k d -> (o p) k d")
                            act.dma_start(t, res[:, u, :, :]).then_inc(res_out[u], 16)

                    pipeline(act, store)


_OUT = ((N, D), "float32")


def kernel(**inputs):
    import numpy as np
    import concourse.bacc as bacc
    from concourse.bass_utils import run_bass_kernel_spmd as run

    nc = bacc.Bacc("TRN2", target_bir_lowering=False, num_devices=1)
    arrays, aps = {}, {}
    for name, value in inputs.items():
        v = np.ascontiguousarray(value)
        arrays["in_" + name] = v
        aps[name] = nc.dram_tensor("in_" + name, v.shape, mybir.dt.from_np(v.dtype), kind="ExternalInput").ap()
    out = nc.dram_tensor("out_x", _OUT[0], F32, kind="ExternalOutput").ap()
    build(nc, aps, out)
    r = run(nc, [arrays], core_ids=[0])
    return r.results[0]["out_x"]
```
